# Optimizing a Trainium2 kernel written in Bass

```python
import numpy as np
import jax
import jax.numpy as jnp

def _softmax(x, axis=-1):
    return jax.nn.softmax(x, axis=axis)

def _gelu(x):
    return jax.nn.gelu(x, approximate=True)

def _silu(x):
    return jax.nn.silu(x)

def _sigmoid(x):
    return jax.nn.sigmoid(x)

def _layernorm(x, axis=-1, eps=1e-05):
    m = jnp.mean(x, axis=axis, keepdims=True)
    v = jnp.var(x, axis=axis, keepdims=True)
    return (x - m) / jnp.sqrt(v + eps)

def _scatter_add(tgt, idx, src, axis=0):
    return tgt.at[idx].add(src)

def _segment_sum(src, seg, n):
    return jax.ops.segment_sum(src, seg, n)
kernel_name = 'mk_adaln_d2_jaxref_r4_4881b5'

def setup_inputs(seed: int=0):
    np.random.seed(seed)
    _w = jnp.asarray

    def _L0_attn_setup():
        import jax, jax.numpy as jnp
        import numpy as np
        from jax import lax
        B, S, E, H, KS = (2, 512, 256, 16, 3)
        DH = E // H
        key = jax.random.key(seed)
        ks = jax.random.split(key, 11)
        s = 1.0 / np.sqrt(E)
        sc = 1.0 / np.sqrt(H * KS)
        return {'query': jax.random.normal(ks[0], (B, S, E), jnp.float32), 'Wq': jax.random.uniform(ks[1], (E, E), jnp.float32, -s, s), 'bq': jax.random.uniform(ks[2], (E,), jnp.float32, -s, s), 'Wk': jax.random.uniform(ks[3], (E, E), jnp.float32, -s, s), 'bk': jax.random.uniform(ks[4], (E,), jnp.float32, -s, s), 'Wv': jax.random.uniform(ks[5], (E, E), jnp.float32, -s, s), 'bv': jax.random.uniform(ks[6], (E,), jnp.float32, -s, s), 'Wo': jax.random.uniform(ks[7], (E, E), jnp.float32, -s, s), 'bo': jax.random.uniform(ks[8], (E,), jnp.float32, -s, s), 'conv_w': jax.random.uniform(ks[9], (H, H, KS), jnp.float32, -sc, sc), 'conv_b': jax.random.uniform(ks[10], (H,), jnp.float32, -sc, sc)}
    _L0_attn_in = _L0_attn_setup()

    def _L0_ffn_setup():
        import jax, jax.numpy as jnp
        import numpy as np
        import math
        BETA = 0.9
        THRESHOLD = 1.0
        NUM_STEPS = 5
        ALPHA = 2.0

        @jax.custom_vjp
        def spike_fn(u):
            return (u > 0).astype(u.dtype)

        def _spike_fwd(u):
            return (spike_fn(u), u)

        def _spike_bwd(u, g):
            s = jnp.pi / 2.0 * ALPHA * u
            return (g * (ALPHA / 2.0) / (1.0 + s * s),)
        spike_fn.defvjp(_spike_fwd, _spike_bwd)
        key = jax.random.key(seed)
        k1, k2, k3 = jax.random.split(key, 3)
        n_embd = 256
        x = jax.random.normal(k1, (4, 512, n_embd), dtype=jnp.float32)
        W_fc = jax.random.normal(k2, (4 * n_embd, n_embd), dtype=jnp.float32) / math.sqrt(n_embd)
        W_proj = jax.random.normal(k3, (n_embd, 4 * n_embd), dtype=jnp.float32) / math.sqrt(4 * n_embd)
        return {'x': x, 'W_fc': W_fc, 'W_proj': W_proj}
    _L0_ffn_in = _L0_ffn_setup()
    _L0_c = _w((lambda *s: np.random.randn(*s).astype(np.float32) * 0.05)(4, 256))
    _L0_wmod = _w((lambda *s: np.random.randn(*s).astype(np.float32) * 0.05)(256, 6 * 256) * 256 ** (-0.5))

    def _L1_attn_setup():
        import jax, jax.numpy as jnp
        import numpy as np
        B, N, E, H = (2, 512, 256, 8)
        HID = 256
        D = HID // H
        EPS = 1e-08

        def rms_norm(x, scale):
            rms = jnp.linalg.norm(x, axis=-1, keepdims=True) * x.shape[-1] ** (-0.5)
            return scale * (x / (rms + EPS))
        key = jax.random.key(seed)
        ks = jax.random.split(key, 12)
        s = 0.02
        return {'x': jax.random.normal(ks[0], (B, N, E), jnp.float32), 'Wq': jax.random.normal(ks[1], (HID, E), jnp.float32) * s, 'bq': jnp.zeros((HID,), jnp.float32), 'Wk': jax.random.normal(ks[2], (HID, E), jnp.float32) * s, 'bk': jnp.zeros((HID,), jnp.float32), 'Wv': jax.random.normal(ks[3], (HID, E), jnp.float32) * s, 'bv': jnp.zeros((HID,), jnp.float32), 'Wu': jax.random.normal(ks[4], (HID, E), jnp.float32) * s, 'bu': jnp.zeros((HID,), jnp.float32), 'Wo': jax.random.normal(ks[5], (E, HID), jnp.float32) * s, 'bo': jnp.zeros((E,), jnp.float32), 'scale': jnp.ones((HID,), jnp.float32)}
    _L1_attn_in = _L1_attn_setup()

    def _L1_ffn_setup():
        import jax, jax.numpy as jnp
        import numpy as np
        E = 8
        TOP_K = 2
        DIM = 256
        HID = 512
        key = jax.random.key(seed)
        k1, k2, k3, k4, k5 = jax.random.split(key, 5)
        s = 0.02
        x = jax.random.normal(k1, (2, 512, DIM), dtype=jnp.float32)
        Wg = jax.random.normal(k2, (DIM, E), dtype=jnp.float32) * s
        W1 = jax.random.normal(k3, (E, DIM, HID), dtype=jnp.float32) * s
        W2 = jax.random.normal(k4, (E, DIM, HID), dtype=jnp.float32) * s
        W3 = jax.random.normal(k5, (E, HID, DIM), dtype=jnp.float32) * s
        return {'x': x, 'Wg': Wg, 'W1': W1, 'W2': W2, 'W3': W3}
    _L1_ffn_in = _L1_ffn_setup()
    _L1_c = _w((lambda *s: np.random.randn(*s).astype(np.float32) * 0.05)(4, 256))
    _L1_wmod = _w((lambda *s: np.random.randn(*s).astype(np.float32) * 0.05)(256, 6 * 256) * 256 ** (-0.5))
    _d = {'L0_attn_query': _L0_attn_in['query'], 'L0_attn_Wq': _L0_attn_in['Wq'], 'L0_attn_bq': _L0_attn_in['bq'], 'L0_attn_Wk': _L0_attn_in['Wk'], 'L0_attn_bk': _L0_attn_in['bk'], 'L0_attn_Wv': _L0_attn_in['Wv'], 'L0_attn_bv': _L0_attn_in['bv'], 'L0_attn_Wo': _L0_attn_in['Wo'], 'L0_attn_bo': _L0_attn_in['bo'], 'L0_attn_conv_w': _L0_attn_in['conv_w'], 'L0_attn_conv_b': _L0_attn_in['conv_b'], 'L0_ffn_W_fc': _L0_ffn_in['W_fc'], 'L0_ffn_W_proj': _L0_ffn_in['W_proj'], 'L0_c': _L0_c, 'L0_wmod': _L0_wmod, 'L1_attn_Wq': _L1_attn_in['Wq'], 'L1_attn_bq': _L1_attn_in['bq'], 'L1_attn_Wk': _L1_attn_in['Wk'], 'L1_attn_bk': _L1_attn_in['bk'], 'L1_attn_Wv': _L1_attn_in['Wv'], 'L1_attn_bv': _L1_attn_in['bv'], 'L1_attn_Wu': _L1_attn_in['Wu'], 'L1_attn_bu': _L1_attn_in['bu'], 'L1_attn_Wo': _L1_attn_in['Wo'], 'L1_attn_bo': _L1_attn_in['bo'], 'L1_attn_scale': _L1_attn_in['scale'], 'L1_ffn_Wg': _L1_ffn_in['Wg'], 'L1_ffn_W1': _L1_ffn_in['W1'], 'L1_ffn_W2': _L1_ffn_in['W2'], 'L1_ffn_W3': _L1_ffn_in['W3'], 'L1_c': _L1_c, 'L1_wmod': _L1_wmod}
    _x0 = _d['L0_attn_query']
    _d['L0_attn_query'] = jax.random.normal(jax.random.fold_in(jax.random.key(seed), 1), (4, 1024, 256), dtype=_x0.dtype)
    del _x0
    return _d

def reference(L0_attn_query, L0_attn_Wq, L0_attn_bq, L0_attn_Wk, L0_attn_bk, L0_attn_Wv, L0_attn_bv, L0_attn_Wo, L0_attn_bo, L0_attn_conv_w, L0_attn_conv_b, L0_ffn_W_fc, L0_ffn_W_proj, L0_c, L0_wmod, L1_attn_Wq, L1_attn_bq, L1_attn_Wk, L1_attn_bk, L1_attn_Wv, L1_attn_bv, L1_attn_Wu, L1_attn_bu, L1_attn_Wo, L1_attn_bo, L1_attn_scale, L1_ffn_Wg, L1_ffn_W1, L1_ffn_W2, L1_ffn_W3, L1_c, L1_wmod):

    def _L0_attn_ref(query, Wq, bq, Wk, bk, Wv, bv, Wo, bo, conv_w, conv_b):
        import jax, jax.numpy as jnp
        import numpy as np
        from jax import lax
        B, S, E, H, KS = (2, 512, 256, 16, 3)
        DH = E // H
        b, s, e = query.shape
        h, dh = (H, DH)
        Q = (query @ Wq.T + bq).reshape(b, s, h, dh).transpose(0, 2, 1, 3)
        K = (query @ Wk.T + bk).reshape(b, s, h, dh).transpose(0, 2, 1, 3)
        V = (query @ Wv.T + bv).reshape(b, s, h, dh).transpose(0, 2, 1, 3)
        scores = jnp.einsum('bhqd,bhkd->bhqk', Q, K) / np.sqrt(dh).astype(np.float32)
        x = scores.transpose(0, 2, 1, 3).reshape(b * s, h, s)
        x = lax.conv_general_dilated(x, conv_w, window_strides=(1,), padding=[(KS // 2, KS // 2)], dimension_numbers=('NCW', 'OIW', 'NCW'))
        x = x + conv_b[None, :, None]
        scores = x.reshape(b, s, h, s).transpose(0, 2, 1, 3)
        weights = jax.nn.softmax(scores, axis=-1)
        out = jnp.einsum('bhqk,bhkd->bqhd', weights, V).reshape(b, s, e)
        return out @ Wo.T + bo

    def _L0_ffn_ref(x, W_fc, W_proj):
        import jax, jax.numpy as jnp
        import numpy as np
        import math
        BETA = 0.9
        THRESHOLD = 1.0
        NUM_STEPS = 5
        ALPHA = 2.0

        @jax.custom_vjp
        def spike_fn(u):
            return (u > 0).astype(u.dtype)

        def _spike_fwd(u):
            return (spike_fn(u), u)

        def _spike_bwd(u, g):
            s = jnp.pi / 2.0 * ALPHA * u
            return (g * (ALPHA / 2.0) / (1.0 + s * s),)
        spike_fn.defvjp(_spike_fwd, _spike_bwd)
        h = jnp.square(jax.nn.relu(jnp.einsum('bsd,fd->bsf', x, W_fc)))
        y = jnp.einsum('bsf,df->bsd', h, W_proj)

        def step(mem, _):
            reset = jax.lax.stop_gradient(spike_fn(mem - THRESHOLD))
            mem_new = BETA * mem + y - reset * THRESHOLD
            spk = spike_fn(mem_new - THRESHOLD)
            return (mem_new, spk)
        mem0 = jnp.zeros_like(y)
        _, spks = jax.lax.scan(step, mem0, None, length=NUM_STEPS)
        return jnp.sum(spks, axis=0) / NUM_STEPS

    def _L1_attn_ref(x, Wq, bq, Wk, bk, Wv, bv, Wu, bu, Wo, bo, scale):
        import jax, jax.numpy as jnp
        import numpy as np
        B, N, E, H = (2, 512, 256, 8)
        HID = 256
        D = HID // H
        EPS = 1e-08

        def rms_norm(x, scale):
            rms = jnp.linalg.norm(x, axis=-1, keepdims=True) * x.shape[-1] ** (-0.5)
            return scale * (x / (rms + EPS))
        n = x.shape[-2]
        q = x @ Wq.T + bq
        u = x @ Wu.T + bu
        k = x @ Wk.T + bk
        v = x @ Wv.T + bv
        u = jax.nn.silu(u)
        v = jax.nn.silu(v)
        to_heads = lambda t: t.reshape(*t.shape[:-1], H, D).swapaxes(-3, -2)
        q, k, v = map(to_heads, (q, k, v))
        q = jax.nn.elu(q)
        k = jax.nn.elu(k)
        mask = jnp.tril(jnp.ones((n, n), q.dtype))
        energy = jnp.einsum('bhnd,bhmd->bhnm', q, k) * mask
        out = jnp.einsum('bhnm,bhmd->bhnd', energy, v)
        out = out.swapaxes(-3, -2).reshape(*x.shape[:-1], HID)
        out = rms_norm(out, scale)
        out = u * out
        return out @ Wo.T + bo

    def _L1_ffn_ref(x, Wg, W1, W2, W3):
        import jax, jax.numpy as jnp
        import numpy as np
        E = 8
        TOP_K = 2
        DIM = 256
        HID = 512
        B, T, C = x.shape
        xf = x.reshape(-1, C)
        logits = xf @ Wg
        top_w, top_i = jax.lax.top_k(logits, TOP_K)
        top_w = jax.nn.softmax(top_w, axis=-1)
        one_hot = jax.nn.one_hot(top_i, E, dtype=xf.dtype)
        combine = jnp.einsum('nk,nke->ne', top_w, one_hot)
        h = jnp.einsum('nc,ech->enh', xf, W1)
        g = jnp.einsum('nc,ech->enh', xf, W2)
        y = jnp.einsum('enh,ehc->enc', jax.nn.silu(h) * g, W3)
        out = jnp.einsum('enc,ne->nc', y, combine)
        return out.reshape(B, T, C)
    x = L0_attn_query
    mod = (_silu(L0_c) @ L0_wmod).reshape(L0_c.shape[0], 6, 1, -1)
    sa, ca, ga, sb, cb, gb = (mod[:, 0], mod[:, 1], mod[:, 2], mod[:, 3], mod[:, 4], mod[:, 5])
    ga = (2 * (ga >= 0) - 1) * jnp.maximum(jnp.abs(ga), 0.25)
    gb = (2 * (gb >= 0) - 1) * jnp.maximum(jnp.abs(gb), 0.25)
    h = _layernorm(x, axis=-1) * (1 + ca) + sa
    x = x + ga * _L0_attn_ref(h, L0_attn_Wq, L0_attn_bq, L0_attn_Wk, L0_attn_bk, L0_attn_Wv, L0_attn_bv, L0_attn_Wo, L0_attn_bo, L0_attn_conv_w, L0_attn_conv_b)
    h = _layernorm(x, axis=-1) * (1 + cb) + sb
    x = x + gb * _L0_ffn_ref(h, L0_ffn_W_fc, L0_ffn_W_proj)
    mod = (_silu(L1_c) @ L1_wmod).reshape(L1_c.shape[0], 6, 1, -1)
    sa, ca, ga, sb, cb, gb = (mod[:, 0], mod[:, 1], mod[:, 2], mod[:, 3], mod[:, 4], mod[:, 5])
    ga = (2 * (ga >= 0) - 1) * jnp.maximum(jnp.abs(ga), 0.25)
    gb = (2 * (gb >= 0) - 1) * jnp.maximum(jnp.abs(gb), 0.25)
    h = _layernorm(x, axis=-1) * (1 + ca) + sa
    x = x + ga * _L1_attn_ref(h, L1_attn_Wq, L1_attn_bq, L1_attn_Wk, L1_attn_bk, L1_attn_Wv, L1_attn_bv, L1_attn_Wu, L1_attn_bu, L1_attn_Wo, L1_attn_bo, L1_attn_scale)
    h = _layernorm(x, axis=-1) * (1 + cb) + sb
    x = x + gb * _L1_ffn_ref(h, L1_ffn_Wg, L1_ffn_W1, L1_ffn_W2, L1_ffn_W3)
    return x

_drawn_inputs = setup_inputs


def setup_inputs(seed=0):
    import zlib

    import numpy as np

    out = dict(_drawn_inputs(seed))
    spreads = {'L1_attn_bq': (0.0, 0.8),
     'L1_attn_bk': (0.0, 0.693),
     'L1_attn_bv': (0.0, 0.742),
     'L1_attn_bu': (0.0, 0.8),
     'L1_attn_bo': (0.0, 0.334),
     'L1_attn_scale': (1.0, 0.6)}
    factors = {'L0_attn_Wq': 8.0,
     'L0_attn_bq': 8.0,
     'L0_attn_Wk': 8.0,
     'L0_attn_bk': 64.0,
     'L0_attn_Wv': 8.0,
     'L0_attn_bv': 8.0,
     'L0_attn_Wo': 8.0,
     'L0_attn_bo': 5.795,
     'L0_attn_conv_w': 8.0,
     'L0_attn_conv_b': 64.0,
     'L1_attn_Wq': 4.174,
     'L1_attn_Wk': 5.848,
     'L1_attn_Wv': 5.968,
     'L1_attn_Wu': 4.052,
     'L1_attn_Wo': 3.791,
     'L1_ffn_Wg': 8.0,
     'L1_ffn_W1': 8.0,
     'L1_ffn_W2': 8.0,
     'L1_ffn_W3': 8.0}
    for name, (base, spread) in spreads.items():
        noise = np.random.default_rng([zlib.crc32(name.encode()), seed]).standard_normal(out[name].shape)
        drawn = base * np.exp(spread * noise) if base else spread * noise
        out[name] = jnp.asarray(drawn.astype(out[name].dtype))
    for name, factor in factors.items():
        out[name] = (out[name] * factor).astype(out[name].dtype)
    return out
```

```python
from contextlib import ExitStack

import numpy as np

import concourse.bass as bass
from concourse import mybir

ALU = mybir.AluOpType
ACT = mybir.ActivationFunctionType
AX = mybir.AxisListType.X
F32 = mybir.dt.float32
F32R = mybir.dt.float32r
P = 128


def adaln_two_layer_kernel(nc, query, Wq0, bq0, Wk0, bk0, Wv0, bv0, Wo0, bo0, conv_w, conv_b, W_fc, W_proj, c0, wmod0,
                           Wq1, bq1, Wk1, bk1, Wv1, bv1, Wu1, bu1, Wo1, bo1, scale1, Wg, W1, W2, W3, c1, wmod1, out):
    B, S, E = query.shape
    H0, _, KS = conv_w.shape
    D0 = E // H0
    H1, D1 = 8, E // 8
    F = W_fc.shape[0]
    NX, _, HID = W1.shape
    T = S // P
    C = E // P
    FC = F // P
    HC = HID // P
    G = 2
    TG = T // G
    N = S // G
    TILES = H0 * T
    QB = 2 * P
    NQB = S // QB
    NMOD = 6 * E
    NLN = 4

    mod_rows_dram = nc.dram_tensor("mod_rows_scratch", (2, B, NMOD), F32, kind="Internal").ap()

    with ExitStack() as ctx:
        def sb(name, shape, dt=F32):
            return ctx.enter_context(nc.sbuf_tensor(name, shape, dt))

        def sem(name):
            return ctx.enter_context(nc.semaphore(name))

        ident = sb("ident", [P, P])
        causal = sb("causal", [P, P])
        blockdiag = sb("blockdiag", [P, P])
        rank_bonus = sb("rank_bonus", [P, NX])
        eps_ln = sb("eps_ln", [P, 1])
        WqT0 = sb("WqT0", [P, C, E])
        WkT0 = sb("WkT0", [P, C, E])
        WvT0 = sb("WvT0", [P, C, E])
        WoT0 = sb("WoT0", [P, C, E])
        WqkvuT1 = sb("WqkvuT1", [P, C, 4 * E])
        WoT1 = sb("WoT1", [P, C, E])
        WfcT = sb("WfcT", [P, C, F])
        WprojT = sb("WprojT", [P, FC, E])
        Wg_sb = sb("Wg_sb", [P, C, NX])
        bq_col = sb("bq_col", [P, C])
        bk_col = sb("bk_col", [P, C])
        bv_row = sb("bv_row", [P, E])
        bo0_row = sb("bo0_row", [P, E])
        bqkvu_row = sb("bqkvu_row", [P, 4 * E])
        bo1_row = sb("bo1_row", [P, E])
        scale_row = sb("scale_row", [P, E])
        conv_raw = sb("conv_raw", [P, C, H0, KS])
        conv_col = sb("conv_col", [P, C, H0, KS])
        convb_row = sb("convb_row", [P, H0])
        siluT = sb("siluT", [P, 2, C, B])

        X = sb("X", [P, T, E])
        MOD = sb("MOD", [P, 2, 6, E])
        Hn = sb("Hn", [P, T, E])
        hT = sb("hT", [P, C, S])
        c_rows = X[0:B, 0:2, :]
        silu_rows = X[0:B, 2:4, :]
        mod_rows = MOD[0:B, :, :, :].rearrange("b l m e -> b l (m e)")
        mod_tmp = Hn[0:B, 0:4, :].rearrange("b (l i) e -> b l i e", l=2)
        mod_tmp2 = Hn[0:B, 4:8, :].rearrange("b (l i) e -> b l i e", l=2)
        stats = sb("stats", [P, T, 6])
        mv = sb("mv", [P, T, 2])
        std = sb("std", [P, T])
        rstd = sb("rstd", [P, T])
        K_hi = sb("K_hi", [P, C, S + 2], F32R)
        K_lo = sb("K_lo", [P, C, S + 2], F32R)
        QW_hi = [sb(f"QW_hi{i}", [P, C * KS, QB], F32R) for i in range(2)]
        QW_lo = [sb(f"QW_lo{i}", [P, C * KS, QB], F32R) for i in range(2)]
        V_head = sb("V_head", [P, T, D0])
        row_max = sb("row_max", [P, 2])
        neg_max_b = sb("neg_max_b", [P, 2])
        exp_bias = sb("exp_bias", [P, 2])
        row_sum = sb("row_sum", [P, 2])
        row_inv = sb("row_inv", [P, 2])
        qexp = [sb(f"qexp{i}", [P, C, 4, P]) for i in range(2)]
        KV = sb("KV", [P, C, P])
        kv_new = sb("kv_new", [P, C, P])
        sumsq = sb("sumsq", [P, T])
        rms = sb("rms", [P, T])
        rms_inv = sb("rms_inv", [P, T])
        gate = sb("gate", [P, 10, T, NX])
        top = sb("top", [P, 8, T])
        ACC = sb("ACC", [P, T, E])

        KB = 256
        work = sb("work", [P, 64 * KB])

        def at(kib, *shape):
            n = int(np.prod(shape))
            flat = work[:, int(kib * KB):int(kib * KB) + n]
            if len(shape) == 1:
                return flat
            if len(shape) == 2:
                return flat.rearrange("p (a b) -> p a b", b=shape[1])
            return flat.rearrange("p (a b c) -> p a b c", b=shape[1], c=shape[2])

        stage_sq = [at(2 * i, C, E) for i in range(9)]
        stage_fc = at(18, FC, E)
        stage_proj = at(26, C, F)
        stage_mod = [at(34 + 12 * l, C, NMOD) for l in range(2)]
        QT = at(0, C, S)
        V = at(8, T, E)
        Pr = [at(16 + 4 * i, S) for i in range(2)]
        PT = at(24, T, P)
        A = at(32, T, E)
        AT = [at(28 + i, C, P) for i in range(2)]
        prod = [at(30 + i, E) for i in range(2)]
        hid = at(0, FC, N)
        mem = at(16, TG, E)
        Y = at(20, TG, E)
        leak = at(24, TG, E)
        cnt = at(28, TG, E)
        relu = [at(32 + 2 * i, N) for i in range(2)]
        spk = at(36, TG, E)
        T1 = at(0, TG, 4 * E)
        EX = at(16, TG, 2 * E)
        qT = [at(24 + i, C, P) for i in range(2)]
        kT = [at(26 + i, C, P) for i in range(2)]
        EM = at(28, C, 4, P)
        O1 = at(32, TG, E)
        AT1 = [at(36 + i, C, P) for i in range(2)]
        prod1 = [at(38 + i, E) for i in range(2)]
        GT = [at(8 * g, HC, N) for g in range(G)]
        silu = [at(16 + 2 * i, N) for i in range(2)]
        W1s = [at(40 + 12 * s, C, HID) for s in range(2)]
        W2s = [at(44 + 12 * s, C, HID) for s in range(2)]
        W3s = [at(48 + 12 * s, HC, E) for s in range(2)]

        bank = [ctx.enter_context(nc.psum_tensor(f"bank{i}", [P, 512], F32)) for i in range(4)]
        score_a = ctx.enter_context(nc.psum_tensor("score_a", [P, 1024], F32))
        score_b = ctx.enter_context(nc.psum_tensor("score_b", [P, 1024], F32))
        scores = [score_a, score_b]
        wide = [score_a[:, 0:512], score_a[:, 512:1024], score_b[:, 0:512], score_b[:, 512:1024]]

        s_ident = sem("s_ident")
        s_load = sem("s_load")
        s_loadm = sem("s_loadm")
        s_wt_ps = sem("s_wt_ps")
        s_wt_sb = sem("s_wt_sb")
        s_silu_c = sem("s_silu_c")
        s_silu_ps = sem("s_silu_ps")
        s_silu_sb = sem("s_silu_sb")
        s_modps = sem("s_modps")
        s_modcp = sem("s_modcp")
        s_modrow = sem("s_modrow")
        s_modst = sem("s_modst")
        s_const = sem("s_const")
        s_x = sem("s_x")
        s_out = sem("s_out")
        s_var = sem("s_var")
        s_std = sem("s_std")
        s_h = sem("s_h")
        s_hT_ps = sem("s_hT_ps")
        s_hT = sem("s_hT")
        s_qkv_ps = sem("s_qkv_ps")
        s_qk_act = sem("s_qk_act")
        s_kv_dve = sem("s_kv_dve")
        s_vhead = sem("s_vhead")
        s_qw_hi = sem("s_qw_hi")
        s_qw_lo = sem("s_qw_lo")
        s_score = sem("s_score")
        s_max = sem("s_max")
        s_exp = sem("s_exp")
        s_tr = sem("s_tr")
        s_pt_act = sem("s_pt_act")
        s_pt_dve = sem("s_pt_dve")
        s_pv = sem("s_pv")
        s_att = sem("s_att")
        s_at_ps = sem("s_at_ps")
        s_at = sem("s_at")
        s_op = sem("s_op")
        s_op_used = sem("s_op_used")
        s_fc = sem("s_fc")
        s_relu = sem("s_relu")
        s_hid = sem("s_hid")
        s_y = sem("s_y")
        s_ysb = sem("s_ysb")
        s_p1 = sem("s_p1")
        s_t1 = sem("s_t1")
        s_neg = sem("s_neg")
        s_eluexp = sem("s_eluexp")
        s_silu1 = sem("s_silu1")
        s_elu = sem("s_elu")
        s_qk_ps = sem("s_qk_ps")
        s_qkT = sem("s_qkT")
        s_qexp = sem("s_qexp")
        s_en = sem("s_en")
        s_em = sem("s_em")
        s_kvps = sem("s_kvps")
        s_kv = sem("s_kv")
        s_o1 = sem("s_o1")
        s_o1sb = sem("s_o1sb")
        s_rms = sem("s_rms")
        s_gated = sem("s_gated")
        s_logit = sem("s_logit")
        s_gap = sem("s_gap")
        s_gexp = sem("s_gexp")
        s_acc0 = sem("s_acc0")
        s_w = [sem(f"s_w{s}") for s in range(2)]
        s_hx = sem("s_hx")
        s_silux = sem("s_silux")
        s_g = sem("s_g")
        s_yx = sem("s_yx")
        s_yx_used = sem("s_yx_used")
        s_fin = sem("s_fin")

        NLOAD = 9 + 2 + 1 + 2 + 8 + H0 + 1
        square_weights = [(Wq0, WqT0, None), (Wk0, WkT0, None), (Wv0, WvT0, None), (Wo0, WoT0, None),
                          (Wq1, WqkvuT1, 0), (Wk1, WqkvuT1, 1), (Wv1, WqkvuT1, 2), (Wu1, WqkvuT1, 3),
                          (Wo1, WoT1, None)]
        wt_banks = []
        for i, (_, dst, slot) in enumerate(square_weights):
            blocks = [stage_sq[i][:, oc, ic * P:(ic + 1) * P] for ic in range(C) for oc in range(C)]
            wt_banks.append((blocks, dst[:, :, :] if slot is None else dst[:, :, slot * E:(slot + 1) * E]))
        for ic in range(C):
            for half in range(2):
                blocks = [stage_fc[:, 4 * half + k, ic * P:(ic + 1) * P] for k in range(4)]
                wt_banks.append((blocks, WfcT[:, ic:ic + 1, half * 512:(half + 1) * 512]))
        for pair in range(FC // 2):
            blocks = [stage_proj[:, oc, f * P:(f + 1) * P] for f in (2 * pair, 2 * pair + 1) for oc in range(C)]
            wt_banks.append((blocks, WprojT[:, 2 * pair:2 * pair + 2, :]))

        x_dram = query.rearrange("b (t p) e -> b p t e", p=P)
        out_dram = out.rearrange("b (t p) e -> b p t e", p=P)

        block = ctx.enter_context(nc.Block())

        @block.sync
        def _(sp):
            for i, (w, _, _) in enumerate(square_weights):
                sp.dma_start(stage_sq[i], w.rearrange("(o p) i -> p o i", p=P)).then_inc(s_load, 16)
            sp.dma_start(stage_fc, W_fc.rearrange("(o p) i -> p o i", p=P)).then_inc(s_load, 16)
            sp.dma_start(stage_proj, W_proj.rearrange("(o p) i -> p o i", p=P)).then_inc(s_load, 16)
            sp.dma_start(Wg_sb[:, :, :], Wg.rearrange("(c p) x -> p c x", p=P)).then_inc(s_load, 16)
            sp.dma_start(bq_col[:, :], bq0.rearrange("(c p) -> p c", p=P), allow_slow_non_contiguous=True).then_inc(s_load, 16)
            sp.dma_start(bk_col[:, :], bk0.rearrange("(c p) -> p c", p=P), allow_slow_non_contiguous=True).then_inc(s_load, 16)
            for dst, src in ((bv_row[:, :], bv0), (bo0_row[:, :], bo0), (bo1_row[:, :], bo1), (scale_row[:, :], scale1),
                             (bqkvu_row[:, 0:E], bq1), (bqkvu_row[:, E:2 * E], bk1),
                             (bqkvu_row[:, 2 * E:3 * E], bv1), (bqkvu_row[:, 3 * E:4 * E], bu1)):
                sp.dma_start(dst, src.partition_broadcast(P)).then_inc(s_load, 16)
            sp.dma_start(convb_row[:, :], conv_b.partition_broadcast(P)).then_inc(s_load, 16)
            for i in range(H0):
                rows = slice(D0 * (i % 8), D0 * (i % 8) + D0)
                sp.dma_start(conv_raw[rows, i // 8, :, :],
                             conv_w[:, i, :].partition_broadcast(D0)).then_inc(s_load, 16)

            def load_expert(e, s):
                sp.dma_start(W1s[s], W1[e].rearrange("(c p) h -> p c h", p=P)).then_inc(s_w[s], 16)
                sp.dma_start(W2s[s], W2[e].rearrange("(c p) h -> p c h", p=P)).then_inc(s_w[s], 16)
                sp.dma_start(W3s[s], W3[e].rearrange("(c p) n -> p c n", p=P)).then_inc(s_w[s], 16)

            sp.wait_ge(s_modps, 6)
            for s in range(2):
                load_expert(s, s)
            with sp.Fori(1, NX // 2) as pair:
                for s in range(2):
                    sp.wait_ge(s_yx, pair * 16 + (8 * s - 8))
                    load_expert(pair * 2 + s, s)
            with sp.Fori(1, B) as b:
                with sp.Fori(0, NX // 2) as pair:
                    for s in range(2):
                        sp.wait_ge(s_yx, b * (NX * T) + pair * 16 + (8 * s - 8))
                        load_expert(pair * 2 + s, s)

        @block.gpsimd
        def _(pool):
            pool.dma_start(c_rows[:, 0, :], c0).then_inc(s_loadm, 16)
            pool.dma_start(c_rows[:, 1, :], c1).then_inc(s_loadm, 16)
            pool.dma_start(stage_mod[0], wmod0.rearrange("(c p) n -> p c n", p=P)).then_inc(s_loadm, 16)
            pool.dma_start(stage_mod[1], wmod1.rearrange("(c p) n -> p c n", p=P)).then_inc(s_loadm, 16)
            nc.gpsimd.memset(ident[:, :], 0.0)
            nc.gpsimd.memset(causal[:, :], 1.0)
            nc.gpsimd.drain()
            nc.gpsimd.affine_select(out=ident[:, :], in_=ident[:, :], compare_op=ALU.not_equal, fill=1.0, base=0,
                                    pattern=[[-1, P]], channel_multiplier=1)
            nc.gpsimd.affine_select(out=causal[:, :], in_=causal[:, :], compare_op=ALU.is_ge, fill=0.0, base=0,
                                    pattern=[[1, P]], channel_multiplier=-1)
            nc.gpsimd.drain()
            nc.gpsimd.memset(eps_ln[:, :], 1e-5).then_inc(s_ident, 1)

            pool.wait_ge(s_modrow, 1)
            for l in range(2):
                pool.dma_start(mod_rows_dram[l], mod_rows[:, l, :]).then_inc(s_modst, 16)
            pool.wait_ge(s_modst, 32)

            def load_batch(b):
                pool.dma_start(X[:, :, :], x_dram[b]).then_inc(s_x, 16)
                pool.dma_start(MOD[:, :, :, :].rearrange("p l m e -> p l (m e)"),
                               mod_rows_dram[:, b, :].partition_broadcast(P)).then_inc(s_x, 16)

            load_batch(0)
            for b in range(B):
                pool.wait_ge(s_fin, (b + 1) * G)
                pool.dma_start(out_dram[b], X[:, :, :]).then_inc(s_out, 16)
                pool.wait_ge(s_out, 16 * (b + 1))
                if b + 1 < B:
                    load_batch(b + 1)

        @block.tensor
        def _(pe):
            mm = nc.tensor.matmul

            pe.wait_ge(s_ident, 1)
            pe.wait_ge(s_load, 16 * NLOAD)
            for i, (blocks, _) in enumerate(wt_banks):
                if i >= 4:
                    pe.wait_ge(s_wt_sb, i - 3)
                for k, blk in enumerate(blocks):
                    last = nc.tensor.transpose(bank[i % 4][:, k * P:(k + 1) * P], blk, ident[:, :])
                last.then_inc(s_wt_ps, 1)

            pe.wait_ge(s_silu_c, 1)
            for l in range(2):
                for c in range(C):
                    k = l * C + c
                    last = nc.tensor.transpose(wide[0][:, k * B:(k + 1) * B], silu_rows[:, l, c * P:(c + 1) * P],
                                               ident[0:B, 0:B])
            last.then_inc(s_silu_ps, 1)
            pe.wait_ge(s_loadm, 64)
            pe.wait_ge(s_silu_sb, 1)
            for l in range(2):
                if l == 1:
                    pe.wait_ge(s_modcp, 3)
                for n in range(3):
                    for c in range(C):
                        last = mm(wide[n + 1][0:B, :], siluT[:, l, c, :],
                                  stage_mod[l][:, c, n * 512:(n + 1) * 512], start=(c == 0), stop=(c == C - 1))
                    last.then_inc(s_modps, 1)

            def transpose_norm(b, k, g):
                for c in range(C):
                    pe.wait_ge(s_h, b * (NLN * G) + k * G + g + 1)
                    if g == 1:
                        pe.wait_ge(s_hT, b * (NLN * G * C) + (k * G) * C + c + 1)
                    for j in range(TG):
                        last = nc.tensor.transpose(bank[c][:, j * P:(j + 1) * P],
                                                   Hn[:, g * TG + j, c * P:(c + 1) * P], ident[:, :])
                    last.then_inc(s_hT_ps, 1)

            def project_qkv(b):
                pe.wait_ge(s_hT, b * 16 + 4)
                for u in range(12):
                    if 4 <= u < 8:
                        pe.wait_ge(s_qk_act, b * 8 + u - 3)
                    if u >= 8:
                        pe.wait_ge(s_kv_dve, b * 8 + u - 7)
                    dst = wide[u % 4]
                    if u < 8:
                        w, oc, g = (WqT0, WkT0)[u // 4], (u % 4) // 2, u % 2
                        for c in range(C):
                            last = mm(dst, w[:, c, oc * P:(oc + 1) * P], hT[:, c, g * N:(g + 1) * N],
                                      start=(c == 0), stop=(c == C - 1))
                    else:
                        for k in range(2):
                            j = 2 * (u - 8) + k
                            for c in range(C):
                                last = mm(dst[:, k * E:(k + 1) * E], hT[:, c, j * P:(j + 1) * P], WvT0[:, c, :],
                                          start=(c == 0), stop=(c == C - 1))
                    last.then_inc(s_qkv_ps, 1)

            def score_tile(b, h, qt):
                ring, col = qt // 2 % 2, (qt % 2) * P
                if qt % 2 == 0:
                    pe.wait_ge(s_qw_lo, b * (NQB * H0) + h * NQB + qt // 2 + 1)
                s = scores[qt % 2]
                n = C * KS
                for i in range(n):
                    c, tap = i // KS, i % KS
                    hi, lo = QW_hi[ring][:, i, col:col + P], QW_lo[ring][:, i, col:col + P]
                    for w, k in ((hi, K_hi), (hi, K_lo), (lo, K_hi)):
                        for kh in range(2):
                            last = mm(s[:, kh * N:(kh + 1) * N], w, k[:, c, kh * N + tap:(kh + 1) * N + tap],
                                      start=(i == 0 and w is hi and k is K_hi), stop=(i == n - 1 and w is lo))
                last.then_inc(s_score, 1)

            def transpose_probs(b, h, qt):
                pe.wait_ge(s_exp, b * TILES + h * T + qt + 1)
                for half in range(2):
                    for k in range(4):
                        kt = 4 * half + k
                        last = nc.tensor.transpose(bank[half][:, k * P:(k + 1) * P],
                                                   Pr[qt % 2][:, kt * P:(kt + 1) * P], ident[:, :])
                    last.then_inc(s_tr, 1)

            def times_v(b, h, qt):
                if qt == 0:
                    pe.wait_ge(s_vhead, b * H0 + h + 1)
                pe.wait_ge(s_pt_act, b * TILES + h * T + qt + 1)
                pe.wait_ge(s_pt_dve, b * TILES + h * T + qt + 1)
                for kt in range(T):
                    last = mm(bank[2 + qt % 2][:, 0:D0], PT[:, kt, :], V_head[:, kt, :],
                              start=(kt == 0), stop=(kt == T - 1))
                last.then_inc(s_pv, 1)

            def attention_head(b, h, last_head):
                for qt in range(T):
                    transpose_probs(b, h, qt)
                    if qt + 2 < T:
                        score_tile(b, h, qt + 2)
                    elif not last_head:
                        score_tile(b, h + 1, qt + 2 - T)
                    times_v(b, h, qt)

            def project_out(b, layer, j, src, srcT, WoT, ready, need):
                n = b * 2 * T + layer * T
                if j < T:
                    if ready is not None:
                        pe.wait_ge(ready, need)
                    if j >= 2:
                        pe.wait_ge(s_at, n + j - 1)
                    for c in range(C):
                        last = nc.tensor.transpose(bank[j % 2][:, c * P:(c + 1) * P], src[:, c * P:(c + 1) * P],
                                                   ident[:, :])
                    last.then_inc(s_at_ps, 1)

            def project_out_mm(b, layer, j, srcT, WoT):
                n = b * 2 * T + layer * T
                pe.wait_ge(s_at, n + j + 1)
                if j >= 2:
                    pe.wait_ge(s_op_used, n + j - 1)
                for c in range(C):
                    last = mm(bank[2 + j % 2][:, 0:E], srcT[j % 2][:, c, :], WoT[:, c, :],
                              start=(c == 0), stop=(c == C - 1))
                last.then_inc(s_op, 1)

            def ffn(b, g):
                pe.wait_ge(s_hT, b * 16 + 4 + 2 * g + 2)
                for f in range(FC):
                    n = g * FC + f
                    if n >= 4:
                        pe.wait_ge(s_relu, b * (G * FC) + n - 3)
                    for c in range(C):
                        last = mm(wide[n % 4], WfcT[:, c, f * P:(f + 1) * P], hT[:, c, g * N:(g + 1) * N],
                                  start=(c == 0), stop=(c == C - 1))
                    last.then_inc(s_fc, 1)
                pe.wait_ge(s_hid, b * (G * FC) + (g + 1) * FC)
                for i in range(2):
                    if g == 1:
                        pe.wait_ge(s_ysb, b * 4 + i + 1)
                    for k in range(2):
                        j = 2 * i + k
                        for f in range(FC):
                            last = mm(bank[2 + i][:, k * E:(k + 1) * E], hid[:, f, j * P:(j + 1) * P],
                                      WprojT[:, f, :], start=(f == 0), stop=(f == FC - 1))
                    last.then_inc(s_y, 1)

            def project1(b, g):
                pe.wait_ge(s_hT, b * 16 + 8 + 2 * g + 2)
                for k in range(TG):
                    j = g * TG + k
                    if j >= 2:
                        pe.wait_ge(s_t1, b * T + j - 1)
                    for n in range(2):
                        for c in range(C):
                            last = mm(scores[j % 2][:, n * 512:(n + 1) * 512], hT[:, c, j * P:(j + 1) * P],
                                      WqkvuT1[:, c, n * 512:(n + 1) * 512], start=(c == 0), stop=(c == C - 1))
                    last.then_inc(s_p1, 1)

            def linear_tile(b, j):
                k = j % TG
                pe.wait_ge(s_elu, b * T + j + 1)
                pe.wait_ge(s_silu1, b * T + j + 1)
                if j > 0:
                    pe.wait_ge(s_o1sb, b * T + j)
                for i in range(4):
                    last = nc.tensor.transpose(bank[0][:, i * P:(i + 1) * P], T1[:, k, i * P:(i + 1) * P], ident[:, :])
                last.then_inc(s_qk_ps, 1)
                for c in range(C):
                    last = mm(bank[1][:, c * P:(c + 1) * P], T1[:, k, E + c * P:E + (c + 1) * P],
                              T1[:, k, 2 * E + c * P:2 * E + (c + 1) * P], start=True, stop=True)
                last.then_inc(s_kvps, 1)
                pe.wait_ge(s_qkT, b * T + j + 1)
                pe.wait_ge(s_qexp, b * T + j + 1)
                for c in range(C):
                    last = mm(bank[2 + c][:, :], kT[j % 2][:, c, :], qexp[j % 2][:, c, :, :].rearrange("p h n -> p (h n)"),
                              start=True, stop=True)
                last.then_inc(s_en, 1)
                pe.wait_ge(s_em, b * T + j + 1)
                o = bank[0][:, 0:E]
                if j > 0:
                    for c in range(C):
                        mm(o[:, c * P:(c + 1) * P], qT[j % 2][:, c, :], KV[:, c, :], start=(c == 0), stop=False)
                for h in range(H1):
                    last = mm(o[:, h * D1:(h + 1) * D1], EM[:, h // 4, h % 4, :],
                              T1[:, k, 2 * E + h * D1:2 * E + (h + 1) * D1], start=(j == 0 and h == 0),
                              stop=(h == H1 - 1))
                last.then_inc(s_o1, 1)

            def experts(b):
                pe.wait_ge(s_hT, b * 16 + 16)
                for j in range(T):
                    for c in range(C):
                        last = mm(bank[2][:, j * NX:(j + 1) * NX], hT[:, c, j * P:(j + 1) * P], Wg_sb[:, c, :],
                                  start=(c == 0), stop=(c == C - 1))
                last.then_inc(s_logit, 1)
                pe.wait_ge(s_acc0, b + 1)
                mm(bank[2][:, 0:NX], hT[:, 0, 0:P], Wg_sb[:, 0, :], start=True, stop=True)
                with pe.Fori(0, NX // 2) as pair:
                    for s in range(2):
                        pe.wait_ge(s_w[s], b * (NX // 2 * 48) + pair * 48 + 48)
                        for g in range(G):
                            for hc in range(HC):
                                u = (s * G + g) * HC + hc
                                pe.wait_ge(s_g, b * (NX * G * HC + 2) + pair * (2 * G * HC) + u + 1)
                                for w, dst in ((W1s[s], wide[u % 2]), (W2s[s], wide[2 + u % 2])):
                                    for c in range(C):
                                        last = mm(dst, w[:, c, hc * P:(hc + 1) * P], hT[:, c, g * N:(g + 1) * N],
                                                  start=(c == 0), stop=(c == C - 1))
                                last.then_inc(s_hx, 1)
                        for g in range(G):
                            u = (s * G + g + 1) * HC
                            pe.wait_ge(s_g, b * (NX * G * HC + 2) + pair * (2 * G * HC) + u + 2)
                            for k in range(TG):
                                j = g * TG + k
                                if k % 2 == 0:
                                    pe.wait_ge(s_yx_used, b * (NX * T + T) + pair * (2 * T) + s * T + j + 2)
                                for hc in range(HC):
                                    last = mm(bank[j // 2][:, (j % 2) * E:(j % 2 + 1) * E],
                                              GT[g][:, hc, k * P:(k + 1) * P], W3s[s][:, hc, :],
                                              start=(hc == 0), stop=(hc == HC - 1))
                                last.then_inc(s_yx, 1)

            with pe.Fori(0, B) as b:
                for g in range(G):
                    transpose_norm(b, 0, g)
                project_qkv(b)
                score_tile(b, 0, 0)
                score_tile(b, 0, 1)
                with pe.Fori(0, H0 - 1) as h:
                    attention_head(b, h, False)
                attention_head(b, H0 - 1, True)
                for j in range(T + 1):
                    if j < T:
                        project_out(b, 0, j, A[:, j, :], AT, WoT0, s_att, (b + 1) * TILES)
                    if j > 0:
                        project_out_mm(b, 0, j - 1, AT, WoT0)
                for g in range(G):
                    transpose_norm(b, 1, g)
                    ffn(b, g)
                for g in range(G):
                    transpose_norm(b, 2, g)
                    project1(b, g)
                    for k in range(TG):
                        linear_tile(b, g * TG + k)
                    for k in range(TG + 1):
                        j = g * TG + k
                        if k < TG:
                            project_out(b, 1, j, O1[:, k, :], AT1, WoT1, s_gated, b * G + g + 1)
                        if k > 0:
                            project_out_mm(b, 1, j - 1, AT1, WoT1)
                for g in range(G):
                    transpose_norm(b, 3, g)
                experts(b)

        @block.scalar
        def _(act):
            def copy(dst, src):
                return nc.scalar.activation(dst, src, ACT.Copy)

            act.wait_ge(s_loadm, 64)
            nc.scalar.activation(silu_rows, c_rows, ACT.Silu).then_inc(s_silu_c, 1)
            for i, (_, dst) in enumerate(wt_banks):
                act.wait_ge(s_wt_ps, i + 1)
                copy(dst, bank[i % 4][:, :].rearrange("p (a b) -> p a b", a=dst.shape[1])).then_inc(s_wt_sb, 1)
            act.wait_ge(s_silu_ps, 1)
            copy(siluT[:, :, :, :].rearrange("p l c b -> p (l c b)"), wide[0][:, 0:2 * C * B]).then_inc(s_silu_sb, 1)
            for l in range(2):
                for n in range(3):
                    act.wait_ge(s_modps, 3 * l + n + 1)
                    copy(mod_rows[:, l, n * 512:(n + 1) * 512], wide[n + 1][0:B, :]).then_inc(s_modcp, 1)

            def norm(b, k, g):
                act.wait_ge(s_var, b * (NLN * G) + k * G + g + 1)
                nc.scalar.activation(std[:, g * TG:(g + 1) * TG], mv[:, g * TG:(g + 1) * TG, 1], ACT.Sqrt,
                                     bias=eps_ln[:, 0:1]).then_inc(s_std, 1)
                for c in range(C):
                    act.wait_ge(s_hT_ps, b * (NLN * G * C) + (k * G + g) * C + c + 1)
                    copy(hT[:, c, g * N:(g + 1) * N], bank[c][:, :]).then_inc(s_hT, 1)

            def queries_hi(b, h, blk):
                ring = blk % 2
                for i in range(C * KS):
                    c, tap = i // KS, i % KS
                    last = nc.scalar.activation(QW_hi[ring][:, i, :], QT[:, c, blk * QB:(blk + 1) * QB], ACT.Copy,
                                                scale=conv_col[:, c, h, tap:tap + 1])
                last.then_inc(s_qw_hi, 1)

            def exponentials(b, h, qt):
                act.wait_ge(s_max, b * TILES + h * T + qt + 1)
                nc.scalar.activation(Pr[qt % 2], scores[qt % 2][:, :], ACT.Exp, bias=exp_bias[:, qt % 2:qt % 2 + 1],
                                     accum_out=row_sum[:, qt % 2:qt % 2 + 1]).then_inc(s_exp, 1)

            def attention_head(b, h, last_head):
                for qt in range(T):
                    act.wait_ge(s_tr, (b * TILES + h * T + qt) * 2 + 1)
                    copy(PT[:, 0:4, :].rearrange("p a b -> p (a b)"), bank[0][:, :]).then_inc(s_pt_act, 1)
                    if qt == 0:
                        copy(V_head[:, :, :], V[:, :, bass.ds(h * D0, D0)]).then_inc(s_vhead, 1)
                    if qt + 1 < T:
                        exponentials(b, h, qt + 1)
                    elif not last_head:
                        exponentials(b, h + 1, 0)
                    if qt in (0, 2):
                        queries_hi(b, h, qt // 2 + 2)
                    elif qt in (4, 6) and not last_head:
                        queries_hi(b, h + 1, qt // 2 - 2)

            def project_out(b, layer, j, srcT):
                n = b * 2 * T + layer * T
                act.wait_ge(s_at_ps, n + j + 1)
                if j >= 2:
                    act.wait_ge(s_op, n + j - 1)
                copy(srcT[j % 2].rearrange("p a b -> p (a b)"), bank[j % 2][:, 0:E]).then_inc(s_at, 1)

            def ffn(b, g):
                for f in range(FC):
                    n = g * FC + f
                    act.wait_ge(s_fc, b * (G * FC) + n + 1)
                    if n >= 2:
                        act.wait_ge(s_hid, b * (G * FC) + n - 1)
                    nc.scalar.activation(relu[n % 2], wide[n % 4], ACT.Relu).then_inc(s_relu, 1)
                for i in range(2):
                    act.wait_ge(s_y, b * 4 + g * 2 + i + 1)
                    if g == 1:
                        act.wait_ge(s_h, b * (NLN * G) + 4)
                    copy(Y[:, 2 * i:2 * i + 2, :].rearrange("p a b -> p (a b)"), bank[2 + i][:, :]).then_inc(s_ysb, 1)

            def second_attention(b, g):
                for k in range(TG):
                    j = g * TG + k
                    act.wait_ge(s_t1, b * T + j + 1)
                    nc.scalar.activation(T1[:, k, 2 * E:4 * E], T1[:, k, 2 * E:4 * E], ACT.Silu).then_inc(s_silu1, 1)
                for k in range(TG):
                    j = g * TG + k
                    act.wait_ge(s_neg, b * T + j + 1)
                    nc.scalar.activation(EX[:, k, :], EX[:, k, :], ACT.Exp).then_inc(s_eluexp, 1)
                for k in range(TG):
                    j = g * TG + k
                    act.wait_ge(s_qk_ps, b * T + j + 1)
                    copy(qT[j % 2].rearrange("p a b -> p (a b)"), bank[0][:, 0:E])
                    copy(kT[j % 2].rearrange("p a b -> p (a b)"), bank[0][:, E:2 * E]).then_inc(s_qkT, 1)
                    act.wait_ge(s_o1, b * T + j + 1)
                    copy(O1[:, k, :], bank[0][:, 0:E])
                    nc.scalar.activation(prod1[0], bank[0][:, 0:E], ACT.Square,
                                         accum_out=sumsq[:, j:j + 1]).then_inc(s_o1sb, 1)
                nc.scalar.drain()
                nc.scalar.activation(rms[:, g * TG:(g + 1) * TG], sumsq[:, g * TG:(g + 1) * TG],
                                     ACT.Sqrt).then_inc(s_rms, 1)
                for k in range(TG):
                    project_out(b, 1, g * TG + k, AT1)

            def experts(b):
                act.wait_ge(s_gap, b + 1)
                nc.scalar.activation(top[:, 3, :], top[:, 2, :], ACT.Exp).then_inc(s_gexp, 1)
                with act.Fori(0, NX // 2) as pair:
                    for s in range(2):
                        for u in range(s * G * HC, (s + 1) * G * HC):
                            act.wait_ge(s_hx, b * (NX * G * HC) + pair * (2 * G * HC) + u + 1)
                            nc.scalar.activation(silu[u % 2], wide[u % 2], ACT.Silu).then_inc(s_silux, 1)

            with act.Fori(0, B) as b:
                for g in range(G):
                    norm(b, 0, g)
                for u in range(8):
                    oc, g = (u % 4) // 2, u % 2
                    act.wait_ge(s_qkv_ps, b * 12 + u + 1)
                    if u < 4:
                        nc.scalar.activation(QT[:, oc, g * N:(g + 1) * N], wide[u % 4], ACT.Identity,
                                             bias=bq_col[:, oc:oc + 1]).then_inc(s_qk_act, 1)
                    else:
                        nc.scalar.activation(K_hi[:, oc, 1 + g * N:1 + (g + 1) * N], wide[u % 4], ACT.Identity,
                                             bias=bk_col[:, oc:oc + 1]).then_inc(s_qk_act, 1)
                nc.scalar.drain()
                act.wait_ge(s_kv_dve, b * 8 + 8)
                queries_hi(b, 0, 0)
                queries_hi(b, 0, 1)
                exponentials(b, 0, 0)
                with act.Fori(0, H0 - 1) as h:
                    attention_head(b, h, False)
                attention_head(b, H0 - 1, True)
                for j in range(T):
                    project_out(b, 0, j, AT)
                for g in range(G):
                    norm(b, 1, g)
                    ffn(b, g)
                for g in range(G):
                    norm(b, 2, g)
                    second_attention(b, g)
                for g in range(G):
                    norm(b, 3, g)
                experts(b)

        @block.vector
        def _(dve):
            V_ = nc.vector

            V_.memset(K_hi[:, :, :].bitcast(F32), 0.0)
            V_.memset(K_lo[:, :, :].bitcast(F32), 0.0)
            for i in range(2):
                V_.memset(qexp[i][:, :, :, :], 0.0)
            V_.memset(blockdiag[:, :], 0.0)
            for x in range(NX):
                V_.memset(rank_bonus[:, x:x + 1], float(NX - x))
            V_.drain()
            for h in range(4):
                V_.memset(blockdiag[32 * h:32 * h + 32, 32 * h:32 * h + 32], 1.0)
            dve.wait_ge(s_load, 16 * NLOAD)
            V_.tensor_scalar(conv_col[:, :, :, :], conv_raw[:, :, :, :], float(1.0 / np.sqrt(D0)), None, ALU.mult)
            V_.drain()
            dve.wait_ge(s_modcp, 6)
            m6 = mod_rows[:, :, :].rearrange("b l (m e) -> b l m e", e=E)
            for m in (1, 4):
                V_.tensor_scalar(m6[:, :, m, :], m6[:, :, m, :], 1.0, None, ALU.add)
            for i, m in enumerate((2, 5)):
                V_.tensor_scalar(mod_tmp[:, :, i, :], m6[:, :, m, :], -1.0, None, ALU.mult)
                V_.tensor_scalar(mod_tmp2[:, :, i, :], m6[:, :, m, :], 0.0, 2.0, ALU.is_ge, ALU.mult)
            V_.drain()
            for i, m in enumerate((2, 5)):
                V_.tensor_tensor(mod_tmp[:, :, i, :], mod_tmp[:, :, i, :], m6[:, :, m, :], ALU.max)
            V_.tensor_scalar(mod_tmp2[:, :, :, :], mod_tmp2[:, :, :, :], -1.0, None, ALU.add)
            V_.drain()
            V_.tensor_scalar(mod_tmp[:, :, :, :], mod_tmp[:, :, :, :], 0.25, None, ALU.max)
            V_.drain()
            for i, m in enumerate((2, 5)):
                V_.tensor_tensor(m6[:, :, m, :], mod_tmp[:, :, i, :], mod_tmp2[:, :, i, :], ALU.mult)
            V_.drain()
            V_.memset(mod_tmp[:, 0, 0, 0:1], 0.0).then_inc(s_modrow, 1)

            def row(l, m, n):
                return MOD[:, l, m:m + 1, :].to_broadcast([P, n, E])

            def norm(b, k, g):
                l, m = k // 2, 3 * (k % 2)
                js = slice(g * TG, (g + 1) * TG)
                if k == 0:
                    dve.wait_ge(s_x, b * 32 + 32)
                for j in range(g * TG, (g + 1) * TG):
                    V_.bn_stats(stats[:, j, :], X[:, j, :])
                V_.drain()
                for j in range(g * TG, (g + 1) * TG):
                    last = V_.bn_aggr(mv[:, j, :], stats[:, j, :])
                last.then_inc(s_var, 1)
                dve.wait_ge(s_std, b * (NLN * G) + k * G + g + 1)
                V_.reciprocal(rstd[:, js], std[:, js])
                V_.drain()
                for j in range(g * TG, (g + 1) * TG):
                    V_.tensor_scalar(Hn[:, j, :], X[:, j, :], mv[:, j, 0:1], rstd[:, j:j + 1], ALU.subtract, ALU.mult)
                V_.drain()
                V_.tensor_tensor(Hn[:, js, :], Hn[:, js, :], row(l, m + 1, TG), ALU.mult)
                V_.drain()
                V_.tensor_tensor(Hn[:, js, :], Hn[:, js, :], row(l, m, TG), ALU.add).then_inc(s_h, 1)

            def queries_lo(b, h, blk):
                ring = blk % 2
                dve.wait_ge(s_qw_hi, b * (NQB * H0) + h * NQB + blk + 1)
                for i in range(C * KS):
                    c, tap = i // KS, i % KS
                    last = V_.scalar_tensor_tensor(out=QW_lo[ring][:, i, :], in0=QT[:, c, blk * QB:(blk + 1) * QB],
                                                   scalar=conv_col[:, c, h, tap:tap + 1],
                                                   in1=QW_hi[ring][:, i, :].bitcast(F32), op0=ALU.mult, op1=ALU.subtract)
                last.then_inc(s_qw_lo, 1)

            def maximum(b, h, qt):
                i = qt % 2
                dve.wait_ge(s_score, b * TILES + h * T + qt + 1)
                V_.reduce_max(row_max[:, i:i + 1], scores[i][:, :], AX)
                V_.drain()
                V_.tensor_scalar(neg_max_b[:, i:i + 1], row_max[:, i:i + 1], convb_row[:, bass.ds(h, 1)], -1.0,
                                 ALU.add, ALU.mult)
                V_.drain()
                V_.tensor_scalar(exp_bias[:, i:i + 1], neg_max_b[:, i:i + 1], convb_row[:, bass.ds(h, 1)], None,
                                 ALU.add).then_inc(s_max, 1)

            def attention_head(b, h, last_head):
                for qt in range(T):
                    t = b * TILES + h * T + qt
                    dve.wait_ge(s_tr, t * 2 + 2)
                    V_.tensor_copy(PT[:, 4:8, :].rearrange("p a b -> p (a b)"), bank[1][:, :]).then_inc(s_pt_dve, 1)
                    V_.reciprocal(row_inv[:, qt % 2:qt % 2 + 1], row_sum[:, qt % 2:qt % 2 + 1])
                    if qt + 1 < T:
                        maximum(b, h, qt + 1)
                    elif not last_head:
                        maximum(b, h + 1, 0)
                    else:
                        V_.drain()
                    if qt in (0, 2):
                        queries_lo(b, h, qt // 2 + 2)
                    elif qt in (4, 6) and not last_head:
                        queries_lo(b, h + 1, qt // 2 - 2)
                    dve.wait_ge(s_pv, t + 1)
                    V_.tensor_scalar(A[:, qt, bass.ds(h * D0, D0)], bank[2 + qt % 2][:, 0:D0],
                                     row_inv[:, qt % 2:qt % 2 + 1], None, ALU.mult).then_inc(s_att, 1)

            def project_out(b, layer, j, buf, bias):
                n = b * 2 * T + layer * T
                t = buf[j % 2]
                dve.wait_ge(s_op, n + j + 1)
                V_.tensor_tensor(t, bank[2 + j % 2][:, 0:E], bias[:, :], ALU.add).then_inc(s_op_used, 1)
                V_.drain()
                V_.tensor_tensor(t, t, MOD[:, layer, 2, :], ALU.mult)
                V_.drain()
                V_.tensor_tensor(X[:, j, :], X[:, j, :], t, ALU.add)
                V_.drain()

            def ffn(b, g):
                js = slice(g * TG, (g + 1) * TG)
                for f in range(FC):
                    n = g * FC + f
                    dve.wait_ge(s_relu, b * (G * FC) + n + 1)
                    if g == 1 and f == 0:
                        dve.wait_ge(s_y, b * 4 + 2)
                    V_.tensor_tensor(hid[:, f, :], relu[n % 2], relu[n % 2], ALU.mult).then_inc(s_hid, 1)
                dve.wait_ge(s_ysb, b * 4 + g * 2 + 2)
                V_.tensor_scalar(cnt, Y, 1.0, None, ALU.is_gt)
                V_.tensor_scalar(spk, Y, 1.0, None, ALU.is_gt)
                for step in range(4):
                    V_.scalar_tensor_tensor(out=leak, in0=(Y if step == 0 else mem), scalar=0.9, in1=Y,
                                            op0=ALU.mult, op1=ALU.add)
                    V_.drain()
                    V_.tensor_tensor(mem, leak, spk, ALU.subtract)
                    V_.drain()
                    V_.tensor_scalar(spk, mem, 1.0, None, ALU.is_gt)
                    V_.scalar_tensor_tensor(out=cnt, in0=mem, scalar=1.0, in1=cnt, op0=ALU.is_gt, op1=ALU.add)
                V_.drain()
                V_.tensor_scalar(cnt, cnt, 0.2, None, ALU.mult)
                V_.drain()
                V_.tensor_tensor(cnt, cnt, row(0, 5, TG), ALU.mult)
                V_.drain()
                V_.tensor_tensor(X[:, js, :], X[:, js, :], cnt, ALU.add)
                V_.drain()

            def second_attention(b, g):
                js = slice(g * TG, (g + 1) * TG)
                for k in range(TG):
                    j = g * TG + k
                    dve.wait_ge(s_p1, b * T + j + 1)
                    V_.tensor_tensor(T1[:, k, :], scores[j % 2][:, :], bqkvu_row[:, :], ALU.add).then_inc(s_t1, 1)
                V_.drain()
                for k in range(TG):
                    V_.tensor_scalar(EX[:, k, :], T1[:, k, 0:2 * E], 0.0, None, ALU.min).then_inc(s_neg, 1)
                for k in range(TG):
                    j = g * TG + k
                    dve.wait_ge(s_eluexp, b * T + j + 1)
                    V_.tensor_scalar(EX[:, k, :], EX[:, k, :], -1.0, None, ALU.add)
                V_.drain()
                for k in range(TG):
                    V_.scalar_tensor_tensor(out=T1[:, k, 0:2 * E], in0=T1[:, k, 0:2 * E], scalar=0.0, in1=EX[:, k, :],
                                            op0=ALU.max, op1=ALU.add).then_inc(s_elu, 1)
                for k in range(TG):
                    j = g * TG + k
                    dve.wait_ge(s_qkT, b * T + j + 1)
                    for h in range(4):
                        r = slice(32 * h, 32 * h + 32)
                        last = V_.tensor_copy(qexp[j % 2][r, :, h, :],
                                              bank[0][r, 0:E].rearrange("p (c n) -> p c n", c=C))
                    last.then_inc(s_qexp, 1)
                    dve.wait_ge(s_kvps, b * T + j + 1)
                    V_.tensor_tensor(kv_new[:, :, :], bank[1][:, 0:E].rearrange("p (c n) -> p c n", c=C),
                                     blockdiag[:, :].unsqueeze(1).to_broadcast([P, C, P]), ALU.mult)
                    dve.wait_ge(s_en, b * T + j + 1)
                    for c in range(C):
                        last = V_.tensor_tensor(EM[:, c, :, :], bank[2 + c][:, :].rearrange("p (h n) -> p h n", h=4),
                                                causal[:, :].unsqueeze(1).to_broadcast([P, 4, P]), ALU.mult)
                    last.then_inc(s_em, 1)
                    dve.wait_ge(s_o1, b * T + j + 1)
                    if j == 0:
                        V_.tensor_copy(KV[:, :, :], kv_new[:, :, :])
                    else:
                        V_.tensor_tensor(KV[:, :, :], KV[:, :, :], kv_new[:, :, :], ALU.add)
                    V_.drain()
                dve.wait_ge(s_rms, b * G + g + 1)
                V_.tensor_scalar(rms[:, js], rms[:, js], float(E) ** -0.5, 1e-8, ALU.mult, ALU.add)
                V_.drain()
                V_.reciprocal(rms_inv[:, js], rms[:, js])
                V_.drain()
                for k in range(TG):
                    j = g * TG + k
                    V_.scalar_tensor_tensor(out=O1[:, k, :], in0=O1[:, k, :], scalar=rms_inv[:, j:j + 1],
                                            in1=scale_row[:, :], op0=ALU.mult, op1=ALU.mult)
                V_.drain()
                V_.tensor_tensor(O1[:, :, :], O1[:, :, :], T1[:, :, 3 * E:4 * E], ALU.mult).then_inc(s_gated, 1)
                for k in range(TG):
                    project_out(b, 1, g * TG + k, prod1, bo1_row)

            def router(b):
                L, eq, one1, L2, one2, cmb = (gate[:, i, :, :] for i in range(6))
                bonus = rank_bonus[:, :].unsqueeze(1).to_broadcast([P, T, NX])

                def wide_(i):
                    return top[:, i, :].unsqueeze(2).to_broadcast([P, T, NX])

                def first_largest(src, one, m):
                    V_.tensor_reduce(top[:, m, :], src, AX, ALU.max)
                    V_.drain()
                    V_.tensor_tensor(eq, src, wide_(m), ALU.is_equal)
                    V_.drain()
                    V_.tensor_tensor(eq, eq, bonus, ALU.mult)
                    V_.drain()
                    V_.tensor_reduce(top[:, 4, :], eq, AX, ALU.max)
                    V_.drain()
                    V_.tensor_tensor(one, eq, wide_(4), ALU.is_equal)
                    V_.drain()

                dve.wait_ge(s_logit, b + 1)
                V_.tensor_copy(L, bank[2][:, 0:T * NX].rearrange("p (t x) -> p t x", x=NX))
                V_.drain()
                first_largest(L, one1, 0)
                V_.tensor_scalar(L2, one1, -1.0, 1.0, ALU.mult, ALU.add)
                V_.drain()
                V_.tensor_tensor(L2, L2, L, ALU.mult)
                V_.tensor_scalar(cmb, one1, -3.0e38, None, ALU.mult)
                V_.drain()
                V_.tensor_tensor(L2, L2, cmb, ALU.add)
                V_.drain()
                first_largest(L2, one2, 1)
                V_.tensor_tensor(top[:, 2, :], top[:, 1, :], top[:, 0, :], ALU.subtract).then_inc(s_gap, 1)
                dve.wait_ge(s_gexp, b + 1)
                V_.tensor_scalar(top[:, 5, :], top[:, 3, :], 1.0, None, ALU.add)
                V_.drain()
                V_.reciprocal(top[:, 6, :], top[:, 5, :])
                V_.drain()
                V_.tensor_tensor(top[:, 7, :], top[:, 3, :], top[:, 6, :], ALU.mult)
                V_.tensor_tensor(one1, one1, wide_(6), ALU.mult)
                V_.drain()
                V_.tensor_tensor(one2, one2, wide_(7), ALU.mult)
                V_.drain()
                V_.tensor_tensor(cmb, one1, one2, ALU.add).then_inc(s_g, 1)
                V_.memset(top[:, 4, 0:1], 0.0).then_inc(s_g, 1)
                for j in range(T):
                    V_.memset(ACC[:, j, :], 0.0).then_inc(s_yx_used, 1)
                V_.drain()
                V_.memset(top[:, 4, 0:1], 0.0).then_inc(s_acc0, 1)
                return cmb

            def experts(b, cmb):
                V_.drain()
                with dve.Fori(0, NX // 2) as pair:
                    for s in range(2):
                        for g in range(G):
                            for hc in range(HC):
                                u = (s * G + g) * HC + hc
                                dve.wait_ge(s_silux, b * (NX * G * HC) + pair * (2 * G * HC) + u + 1)
                                V_.tensor_tensor(GT[g][:, hc, :], silu[u % 2], wide[2 + u % 2],
                                                 ALU.mult).then_inc(s_g, 1)
                        for j in range(T):
                            if j % 2 == 0:
                                dve.wait_ge(s_yx, b * (NX * T) + pair * (2 * T) + s * T + j + 2)
                            V_.scalar_tensor_tensor(out=ACC[:, j, :], in0=bank[j // 2][:, (j % 2) * E:(j % 2 + 1) * E],
                                                    scalar=gate[:, 5, j, bass.ds(pair * 2 + s, 1)], in1=ACC[:, j, :],
                                                    op0=ALU.mult, op1=ALU.add).then_inc(s_yx_used, 1)
                V_.drain()
                for g in range(G):
                    js = slice(g * TG, (g + 1) * TG)
                    V_.tensor_tensor(ACC[:, js, :], ACC[:, js, :], row(1, 5, TG), ALU.mult)
                V_.drain()
                for g in range(G):
                    js = slice(g * TG, (g + 1) * TG)
                    V_.tensor_tensor(X[:, js, :], X[:, js, :], ACC[:, js, :], ALU.add).then_inc(s_fin, 1)

            with dve.Fori(0, B) as b:
                for g in range(G):
                    norm(b, 0, g)
                for u in range(4, 12):
                    if u < 8:
                        oc, g = (u % 4) // 2, u % 2
                        dve.wait_ge(s_qk_act, b * 8 + u + 1)
                        V_.scalar_tensor_tensor(out=K_lo[:, oc, 1 + g * N:1 + (g + 1) * N], in0=wide[u % 4],
                                                scalar=bk_col[:, oc:oc + 1],
                                                in1=K_hi[:, oc, 1 + g * N:1 + (g + 1) * N].bitcast(F32),
                                                op0=ALU.add, op1=ALU.subtract).then_inc(s_kv_dve, 1)
                    else:
                        j = 2 * (u - 8)
                        dve.wait_ge(s_qkv_ps, b * 12 + u + 1)
                        V_.tensor_tensor(V[:, j:j + 2, :], wide[u % 4].rearrange("p (k e) -> p k e", k=2),
                                         bv_row[:, :].unsqueeze(1).to_broadcast([P, 2, E]),
                                         ALU.add).then_inc(s_kv_dve, 1)
                queries_lo(b, 0, 0)
                queries_lo(b, 0, 1)
                maximum(b, 0, 0)
                with dve.Fori(0, H0 - 1) as h:
                    attention_head(b, h, False)
                attention_head(b, H0 - 1, True)
                for j in range(T):
                    project_out(b, 0, j, prod, bo0_row)
                for g in range(G):
                    norm(b, 1, g)
                    ffn(b, g)
                for g in range(G):
                    norm(b, 2, g)
                    second_attention(b, g)
                for g in range(G):
                    norm(b, 3, g)
                cmb = router(b)
                experts(b, cmb)


_INS = ['L0_attn_query', 'L0_attn_Wq', 'L0_attn_bq', 'L0_attn_Wk', 'L0_attn_bk', 'L0_attn_Wv', 'L0_attn_bv',
        'L0_attn_Wo', 'L0_attn_bo', 'L0_attn_conv_w', 'L0_attn_conv_b', 'L0_ffn_W_fc', 'L0_ffn_W_proj', 'L0_c',
        'L0_wmod', 'L1_attn_Wq', 'L1_attn_bq', 'L1_attn_Wk', 'L1_attn_bk', 'L1_attn_Wv', 'L1_attn_bv', 'L1_attn_Wu',
        'L1_attn_bu', 'L1_attn_Wo', 'L1_attn_bo', 'L1_attn_scale', 'L1_ffn_Wg', 'L1_ffn_W1', 'L1_ffn_W2',
        'L1_ffn_W3', 'L1_c', 'L1_wmod']
_OUTS = [((4, 1024, 256), 'float32')]


def kernel(**inputs):
    import numpy as _np
    import concourse.bacc as _bacc
    from concourse import mybir as _mybir
    from concourse.bass_utils import run_bass_kernel_spmd as _run

    nc = _bacc.Bacc("TRN2", target_bir_lowering=False, num_devices=1)
    arrays, args = {}, []
    for name in _INS:
        a = _np.ascontiguousarray(inputs[name])
        arrays[f"in_{name}_dram"] = a
        args.append(nc.dram_tensor(f"in_{name}_dram", a.shape, _mybir.dt.from_np(a.dtype), kind="ExternalInput").ap())
    for i, (shape, dtype) in enumerate(_OUTS):
        dt = _mybir.dt.from_np(_np.dtype(dtype))
        args.append(nc.dram_tensor(f"out_{i}_dram", shape, dt, kind="ExternalOutput").ap())
    adaln_two_layer_kernel(nc, *args)
    r = _run(nc, [arrays], core_ids=[0])
    got = tuple(r.results[0][f"out_{i}_dram"] for i in range(len(_OUTS)))
    return got[0]
```

```python
from contextlib import ExitStack

import numpy as np

import concourse.bass as bass
from concourse import mybir

ALU = mybir.AluOpType
ACT = mybir.ActivationFunctionType
AX = mybir.AxisListType.X
F32 = mybir.dt.float32
F32R = mybir.dt.float32r
F16 = mybir.dt.float16
BF16 = mybir.dt.bfloat16
P = 128


def adaln_two_layer_kernel(nc, query, Wq0, bq0, Wk0, bk0, Wv0, bv0, Wo0, bo0, conv_w, conv_b, W_fc, W_proj, c0, wmod0,
                           Wq1, bq1, Wk1, bk1, Wv1, bv1, Wu1, bu1, Wo1, bo1, scale1, Wg, W1, W2, W3, c1, wmod1, out):
    B, S, E = query.shape
    H0, _, KS = conv_w.shape
    D0 = E // H0
    H1, D1 = 8, E // 8
    F = W_fc.shape[0]
    NX, _, HID = W1.shape
    T = S // P
    C = E // P
    FC = F // P
    HC = HID // P
    G = 2
    TG = T // G
    N = S // G
    TILES = H0 * T
    QB = 2 * P
    NQB = S // QB
    NMOD = 6 * E
    U = 4
    SUM, FIRST, LAST, DIFF = range(U)
    VP = 3
    PSCALE = float(2 ** 15)
    NLN = 4

    mod_rows_dram = nc.dram_tensor("mod_rows_scratch", (2, B, NMOD), F32, kind="Internal").ap()

    with ExitStack() as ctx:
        def sb(name, shape, dt=F32):
            return ctx.enter_context(nc.sbuf_tensor(name, shape, dt))

        def sem(name):
            return ctx.enter_context(nc.semaphore(name))

        ident = sb("ident", [P, P])
        causal = sb("causal", [P, P])
        blockdiag = sb("blockdiag", [P, P])
        rank_bonus = sb("rank_bonus", [P, NX])
        eps_ln = sb("eps_ln", [P, 1])
        WqT0 = sb("WqT0", [P, C, E])
        WkT0 = sb("WkT0", [P, C, E])
        WvT0 = sb("WvT0", [P, C, E])
        WoT0 = sb("WoT0", [P, C, E])
        WqkvuT1 = sb("WqkvuT1", [P, C, 4 * E])
        WoT1 = sb("WoT1", [P, C, E])
        WfcT = sb("WfcT", [P, C, F])
        WprojT = sb("WprojT", [P, FC, E])
        Wg_sb = sb("Wg_sb", [P, C, NX])
        bq_col = sb("bq_col", [P, C])
        bk_col = sb("bk_col", [P, C])
        bv_row = sb("bv_row", [P, E])
        bo0_row = sb("bo0_row", [P, E])
        bqkvu_row = sb("bqkvu_row", [P, 4 * E])
        bo1_row = sb("bo1_row", [P, E])
        scale_row = sb("scale_row", [P, E])
        conv_raw = sb("conv_raw", [P, C, H0, KS])
        conv_sum = sb("conv_sum", [P, C, H0])
        filt = sb("filt", [P, C, H0, U])
        convb_row = sb("convb_row", [P, H0])
        siluT = sb("siluT", [P, 2, C, B])

        X = sb("X", [P, T, E])
        MOD = sb("MOD", [P, 2, 6, E])
        Hn = sb("Hn", [P, T, E])
        hT = sb("hT", [P, C, S])
        c_rows = X[0:B, 0:2, :]
        silu_rows = X[0:B, 2:4, :]
        mod_rows = MOD[0:B, :, :, :].rearrange("b l m e -> b l (m e)")
        mod_tmp = Hn[0:B, 0:4, :].rearrange("b (l i) e -> b l i e", l=2)
        mod_tmp2 = Hn[0:B, 4:8, :].rearrange("b (l i) e -> b l i e", l=2)
        stats = sb("stats", [P, T, 6])
        mv = sb("mv", [P, T, 2])
        std = sb("std", [P, T])
        rstd = sb("rstd", [P, T])
        V_head = sb("V_head", [P, T, VP * D0], BF16)
        V_rest = sb("V_rest", [P, T, D0])
        pv_sum = sb("pv_sum", [P, D0])
        carrier = sb("carrier", [P, 1])
        row_max = sb("row_max", [P, 2, 2])
        max_b = sb("max_b", [P, 2])
        exp_bias = sb("exp_bias", [P, 2])
        row_sum = sb("row_sum", [P, 2])
        row_inv = sb("row_inv", [P, 2])
        qexp = sb("qexp", [P, C, 4, P])
        KV = sb("KV", [P, C, P])
        kv_new = sb("kv_new", [P, C, P])
        sumsq = sb("sumsq", [P, T])
        rms = sb("rms", [P, T])
        rms_inv = sb("rms_inv", [P, T])
        gate = sb("gate", [P, 10, T, NX])
        top = sb("top", [P, 8, T])
        ACC = Hn

        KB = 256
        work = sb("work", [P, 52 * KB])
        split = sb("split", [P, 64 * KB], F32R)

        def at(kib, *shape, space=work):
            n = int(np.prod(shape))
            flat = space[:, int(kib * KB):int(kib * KB) + n]
            if len(shape) == 1:
                return flat
            if len(shape) == 2:
                return flat.rearrange("p (a b) -> p a b", b=shape[1])
            return flat.rearrange("p (a b c) -> p a b c", b=shape[1], c=shape[2])

        stage_sq = [at(2 * i, C, E) for i in range(9)]
        stage_fc = at(18, FC, E)
        stage_proj = hT[:, :, :]
        stage_mod = [at(26 + 12 * l, C, NMOD) for l in range(2)]
        QT = at(0, C, S)
        V = at(8, T, E)
        SC = [at(16 + 4 * i, 2, N) for i in range(2)]
        PT_hi = at(24, 2 * KB).bitcast(F16).rearrange("p (t q) -> p t q", q=P)
        PT_lo = at(26, 2 * KB).bitcast(F16).rearrange("p (t q) -> p t q", q=P)
        sum_sb = at(28, N)
        K_raw = at(16, C, S + 2)
        K_pair = [at(24.5, U, N), Hn[:, :, :].rearrange("p (u a) e -> p u (a e)", u=U)]
        A = at(32, T, E)
        K_hi = at(0, C, U, N, space=split)
        K_lo = at(16, C, U, N, space=split)
        QW_hi = [at(32 + 8 * i, U * C, QB, space=split) for i in range(2)]
        QW_lo = [at(48 + 8 * i, U * C, QB, space=split) for i in range(2)]
        AT = [at(28 + i, C, P) for i in range(2)]
        prod = [at(30 + i, E) for i in range(2)]
        hid = at(0, FC, N)
        mem = at(16, TG, E)
        Y = at(20, TG, E)
        leak = at(24, TG, E)
        cnt = at(28, TG, E)
        relu = [at(32 + 2 * i, N) for i in range(2)]
        spk = at(36, TG, E)
        T1 = at(0, TG, 4 * E)
        EX = at(16, TG, 2 * E)
        qT = [at(24 + i, C, P) for i in range(2)]
        kT = [at(26 + i, C, P) for i in range(2)]
        EM = at(28, C, 4, P)
        O1 = at(32, TG, E)
        AT1 = [at(36 + i, C, P) for i in range(2)]
        prod1 = [at(38 + i, E) for i in range(2)]
        silu = [at(2 * i, N) for i in range(2)]
        gated = [at(4 + 2 * i, N) for i in range(2)]
        slot_at = (40, 20)
        W12s = [at(slot_at[s], 2 * C, HID) for s in range(2)]
        W3s = [at(slot_at[s] + 8, HC, E) for s in range(2)]
        hT_hi = at(0, C, S, space=split)
        hT_lo = at(8, C, S, space=split)
        W12_hi = [at(16 + 16 * s, 2 * C, HID, space=split) for s in range(2)]
        W12_lo = [at(24 + 16 * s, 2 * C, HID, space=split) for s in range(2)]
        W3_hi = at(48, HC, E, space=split)
        W3_lo = at(52, HC, E, space=split)
        G_hi = [at(56 + 2 * i, N, space=split) for i in range(2)]
        G_lo = [at(60 + 2 * i, N, space=split) for i in range(2)]

        bank = [ctx.enter_context(nc.psum_tensor(f"bank{i}", [P, 512], F32)) for i in range(4)]
        score_a = ctx.enter_context(nc.psum_tensor("score_a", [P, 1024], F32))
        score_b = ctx.enter_context(nc.psum_tensor("score_b", [P, 1024], F32))
        scores = [score_a, score_b]
        wide = [score_a[:, 0:512], score_a[:, 512:1024], score_b[:, 0:512], score_b[:, 512:1024]]

        s_ident = sem("s_ident")
        s_load = sem("s_load")
        s_loadm = sem("s_loadm")
        s_wt_ps = sem("s_wt_ps")
        s_wt_sb = sem("s_wt_sb")
        s_silu_c = sem("s_silu_c")
        s_silu_ps = sem("s_silu_ps")
        s_silu_sb = sem("s_silu_sb")
        s_modps = sem("s_modps")
        s_modcp = sem("s_modcp")
        s_modrow = sem("s_modrow")
        s_modst = sem("s_modst")
        s_const = sem("s_const")
        s_x = sem("s_x")
        s_out = sem("s_out")
        s_var = sem("s_var")
        s_std = sem("s_std")
        s_h = sem("s_h")
        s_hT_ps = sem("s_hT_ps")
        s_hT = sem("s_hT")
        s_qkv_ps = sem("s_qkv_ps")
        s_qk_act = sem("s_qk_act")
        s_v = sem("s_v")
        s_kpair = sem("s_kpair")
        s_khi = sem("s_khi")
        s_klo = sem("s_klo")
        s_vhead = sem("s_vhead")
        s_qw_hi = sem("s_qw_hi")
        s_qw_lo = sem("s_qw_lo")
        s_prod = sem("s_prod")
        s_sum = sem("s_sum")
        s_comb = sem("s_comb")
        s_max = sem("s_max")
        s_exp = sem("s_exp")
        s_tr = sem("s_tr")
        s_pt_hi = sem("s_pt_hi")
        s_pt_lo = sem("s_pt_lo")
        s_pv = sem("s_pv")
        s_att = sem("s_att")
        s_at_ps = sem("s_at_ps")
        s_at = sem("s_at")
        s_op = sem("s_op")
        s_op_used = sem("s_op_used")
        s_fc = sem("s_fc")
        s_relu = sem("s_relu")
        s_hid = sem("s_hid")
        s_y = sem("s_y")
        s_ysb = sem("s_ysb")
        s_p1 = sem("s_p1")
        s_t1 = sem("s_t1")
        s_neg = sem("s_neg")
        s_eluexp = sem("s_eluexp")
        s_silu1 = sem("s_silu1")
        s_elu = sem("s_elu")
        s_qk_ps = sem("s_qk_ps")
        s_qkT = sem("s_qkT")
        s_qexp = sem("s_qexp")
        s_en = sem("s_en")
        s_em = sem("s_em")
        s_kvps = sem("s_kvps")
        s_kv = sem("s_kv")
        s_o1 = sem("s_o1")
        s_o1sb = sem("s_o1sb")
        s_rms = sem("s_rms")
        s_gated = sem("s_gated")
        s_logit = sem("s_logit")
        s_gap = sem("s_gap")
        s_gexp = sem("s_gexp")
        s_hsp_hi = sem("s_hsp_hi")
        s_hsp_lo = sem("s_hsp_lo")
        s_w = [sem(f"s_w{s}") for s in range(2)]
        s_w12_hi = sem("s_w12_hi")
        s_w12_lo = sem("s_w12_lo")
        s_w3_hi = sem("s_w3_hi")
        s_w3_lo = sem("s_w3_lo")
        s_hx = sem("s_hx")
        s_silux = sem("s_silux")
        s_gatedx = sem("s_gatedx")
        s_g_hi = sem("s_g_hi")
        s_g = sem("s_g")
        s_yx = sem("s_yx")
        s_yx_used = sem("s_yx_used")
        s_fin = sem("s_fin")

        NLOAD = 9 + 2 + 1 + 2 + 8 + H0 + 1
        square_weights = [(Wq0, WqT0, None), (Wk0, WkT0, None), (Wv0, WvT0, None), (Wo0, WoT0, None),
                          (Wq1, WqkvuT1, 0), (Wk1, WqkvuT1, 1), (Wv1, WqkvuT1, 2), (Wu1, WqkvuT1, 3),
                          (Wo1, WoT1, None)]
        wt_banks = []
        for i, (_, dst, slot) in enumerate(square_weights):
            blocks = [stage_sq[i][:, oc, ic * P:(ic + 1) * P] for ic in range(C) for oc in range(C)]
            wt_banks.append((blocks, dst[:, :, :] if slot is None else dst[:, :, slot * E:(slot + 1) * E]))
        for ic in range(C):
            for half in range(2):
                blocks = [stage_fc[:, 4 * half + k, ic * P:(ic + 1) * P] for k in range(4)]
                wt_banks.append((blocks, WfcT[:, ic:ic + 1, half * 512:(half + 1) * 512]))
        for pair in range(FC // 2):
            blocks = [stage_proj[:, oc, f * P:(f + 1) * P] for f in (2 * pair, 2 * pair + 1) for oc in range(C)]
            wt_banks.append((blocks, WprojT[:, 2 * pair:2 * pair + 2, :]))

        x_dram = query.rearrange("b (t p) e -> b p t e", p=P)
        out_dram = out.rearrange("b (t p) e -> b p t e", p=P)

        block = ctx.enter_context(nc.Block())

        @block.sync
        def _(sp):
            for i, (w, _, _) in enumerate(square_weights):
                sp.dma_start(stage_sq[i], w.rearrange("(o p) i -> p o i", p=P)).then_inc(s_load, 16)
            sp.dma_start(stage_fc, W_fc.rearrange("(o p) i -> p o i", p=P)).then_inc(s_load, 16)
            sp.dma_start(stage_proj, W_proj.rearrange("(o p) i -> p o i", p=P)).then_inc(s_load, 16)
            sp.dma_start(Wg_sb[:, :, :], Wg.rearrange("(c p) x -> p c x", p=P)).then_inc(s_load, 16)
            sp.dma_start(bq_col[:, :], bq0.rearrange("(c p) -> p c", p=P), allow_slow_non_contiguous=True).then_inc(s_load, 16)
            sp.dma_start(bk_col[:, :], bk0.rearrange("(c p) -> p c", p=P), allow_slow_non_contiguous=True).then_inc(s_load, 16)
            for dst, src in ((bv_row[:, :], bv0), (bo0_row[:, :], bo0), (bo1_row[:, :], bo1), (scale_row[:, :], scale1),
                             (bqkvu_row[:, 0:E], bq1), (bqkvu_row[:, E:2 * E], bk1),
                             (bqkvu_row[:, 2 * E:3 * E], bv1), (bqkvu_row[:, 3 * E:4 * E], bu1)):
                sp.dma_start(dst, src.partition_broadcast(P)).then_inc(s_load, 16)
            sp.dma_start(convb_row[:, :], conv_b.partition_broadcast(P)).then_inc(s_load, 16)
            for i in range(H0):
                rows = slice(D0 * (i % 8), D0 * (i % 8) + D0)
                sp.dma_start(conv_raw[rows, i // 8, :, :],
                             conv_w[:, i, :].partition_broadcast(D0)).then_inc(s_load, 16)

            def load_expert(e, s):
                for i, w in enumerate((W1, W2)):
                    sp.dma_start(W12s[s][:, C * i:C * i + C, :],
                                 w[e].rearrange("(c p) h -> p c h", p=P)).then_inc(s_w[s], 16)
                sp.dma_start(W3s[s], W3[e].rearrange("(c p) n -> p c n", p=P)).then_inc(s_w[s], 16)

            def later_experts(b):
                with sp.Fori(1, NX // 2) as pair:
                    for s in range(2):
                        sp.wait_ge(s_w3_lo, b * NX + pair * 2 + (s - 1))
                        load_expert(pair * 2 + s, s)

            sp.wait_ge(s_modps, 6)
            load_expert(0, 0)
            sp.wait_ge(s_h, NLN * G - 1)
            load_expert(1, 1)
            later_experts(0)
            with sp.Fori(1, B) as b:
                sp.wait_ge(s_w3_lo, b * NX - 1)
                load_expert(0, 0)
                sp.wait_ge(s_h, b * (NLN * G) + (NLN * G - 1))
                load_expert(1, 1)
                later_experts(b)

        @block.gpsimd
        def _(pool):
            pool.dma_start(c_rows[:, 0, :], c0).then_inc(s_loadm, 16)
            pool.dma_start(c_rows[:, 1, :], c1).then_inc(s_loadm, 16)
            pool.dma_start(stage_mod[0], wmod0.rearrange("(c p) n -> p c n", p=P)).then_inc(s_loadm, 16)
            pool.dma_start(stage_mod[1], wmod1.rearrange("(c p) n -> p c n", p=P)).then_inc(s_loadm, 16)
            nc.gpsimd.memset(ident[:, :], 0.0)
            nc.gpsimd.memset(causal[:, :], 1.0)
            nc.gpsimd.drain()
            nc.gpsimd.affine_select(out=ident[:, :], in_=ident[:, :], compare_op=ALU.not_equal, fill=1.0, base=0,
                                    pattern=[[-1, P]], channel_multiplier=1)
            nc.gpsimd.affine_select(out=causal[:, :], in_=causal[:, :], compare_op=ALU.is_ge, fill=0.0, base=0,
                                    pattern=[[1, P]], channel_multiplier=-1)
            nc.gpsimd.drain()
            nc.gpsimd.memset(eps_ln[:, :], 1e-5).then_inc(s_ident, 1)

            pool.wait_ge(s_modrow, 1)
            for l in range(2):
                pool.dma_start(mod_rows_dram[l], mod_rows[:, l, :]).then_inc(s_modst, 16)
            pool.wait_ge(s_modst, 32)

            def load_batch(b):
                pool.dma_start(X[:, :, :], x_dram[b]).then_inc(s_x, 16)
                pool.dma_start(MOD[:, :, :, :].rearrange("p l m e -> p l (m e)"),
                               mod_rows_dram[:, b, :].partition_broadcast(P)).then_inc(s_x, 16)

            load_batch(0)
            for b in range(B):
                pool.wait_ge(s_fin, (b + 1) * G)
                pool.dma_start(out_dram[b], X[:, :, :]).then_inc(s_out, 16)
                pool.wait_ge(s_out, 16 * (b + 1))
                if b + 1 < B:
                    load_batch(b + 1)

        @block.tensor
        def _(pe):
            mm = nc.tensor.matmul

            pe.wait_ge(s_ident, 1)
            pe.wait_ge(s_load, 16 * NLOAD)
            for i, (blocks, _) in enumerate(wt_banks):
                if i >= 4:
                    pe.wait_ge(s_wt_sb, i - 3)
                for k, blk in enumerate(blocks):
                    last = nc.tensor.transpose(bank[i % 4][:, k * P:(k + 1) * P], blk, ident[:, :])
                last.then_inc(s_wt_ps, 1)

            pe.wait_ge(s_silu_c, 1)
            for l in range(2):
                for c in range(C):
                    k = l * C + c
                    last = nc.tensor.transpose(wide[0][:, k * B:(k + 1) * B], silu_rows[:, l, c * P:(c + 1) * P],
                                               ident[0:B, 0:B])
            last.then_inc(s_silu_ps, 1)
            pe.wait_ge(s_loadm, 64)
            pe.wait_ge(s_silu_sb, 1)
            for l in range(2):
                if l == 1:
                    pe.wait_ge(s_modcp, 3)
                for n in range(3):
                    for c in range(C):
                        last = mm(wide[n + 1][0:B, :], siluT[:, l, c, :],
                                  stage_mod[l][:, c, n * 512:(n + 1) * 512], start=(c == 0), stop=(c == C - 1))
                    last.then_inc(s_modps, 1)

            def transpose_norm(b, k, g):
                for c in range(C):
                    pe.wait_ge(s_h, b * (NLN * G) + k * G + g + 1)
                    if g == 1:
                        pe.wait_ge(s_hT, b * (NLN * G * C) + (k * G) * C + c + 1)
                    for j in range(TG):
                        last = nc.tensor.transpose(bank[c][:, j * P:(j + 1) * P],
                                                   Hn[:, g * TG + j, c * P:(c + 1) * P], ident[:, :])
                    last.then_inc(s_hT_ps, 1)

            def project_qkv(b):
                pe.wait_ge(s_hT, b * 16 + 4)
                for u in range(12):
                    if u >= 4:
                        pe.wait_ge(s_qk_act, b * 8 + u - 3)
                    dst = wide[u % 4]
                    if u < 8:
                        w, oc, g = (WqT0, WkT0)[u // 4], (u % 4) // 2, u % 2
                        for c in range(C):
                            last = mm(dst, w[:, c, oc * P:(oc + 1) * P], hT[:, c, g * N:(g + 1) * N],
                                      start=(c == 0), stop=(c == C - 1))
                    else:
                        for k in range(2):
                            j = 2 * (u - 8) + k
                            start = 2 * P * (j % 4) + j // 4
                            for c in range(C):
                                last = mm(dst[:, k * E:(k + 1) * E], hT[:, c, start:start + 2 * P - 1:2], WvT0[:, c, :],
                                          start=(c == 0), stop=(c == C - 1))
                    last.then_inc(s_qkv_ps, 1)

            def score_tile(b, h, qt, first=False):
                ring, col = qt // 2 % 2, (qt % 2) * P
                t = b * TILES + h * T + qt
                if qt % 2 == 0:
                    pe.wait_ge(s_qw_lo, b * (2 * NQB * H0) + h * (2 * NQB) + qt + 2)
                for u in range(U):
                    if not first:
                        done, count = {SUM: (s_sum, t), FIRST: (s_comb, t * 2 - 1), LAST: (s_comb, t * 2),
                                       DIFF: (s_max, t)}[u]
                        pe.wait_ge(done, count)
                    for c in range(C):
                        i = u * C + c
                        hi, lo = QW_hi[ring][:, i, col:col + P], QW_lo[ring][:, i, col:col + P]
                        for w, k in ((hi, K_hi), (hi, K_lo), (lo, K_hi)):
                            last = mm(wide[u], w, k[:, c, u, :], start=(c == 0 and w is hi and k is K_hi),
                                      stop=(c == C - 1 and w is lo))
                    last.then_inc(s_prod, 1)

            def transpose_probs(b, h, qt):
                pe.wait_ge(s_exp, b * TILES + h * T + qt + 1)
                for half in range(2):
                    for k in range(4):
                        last = nc.tensor.transpose(bank[half][:, k * P:(k + 1) * P],
                                                   SC[qt % 2][:, half, k * P:(k + 1) * P], ident[:, :])
                    last.then_inc(s_tr, 1)

            def times_v(b, h, qt):
                if qt == 0:
                    pe.wait_ge(s_vhead, b * H0 + h + 1)
                pe.wait_ge(s_pt_lo, b * TILES + h * T + qt + 1)
                for kt in range(T):
                    mm(bank[2 + qt % 2][:, 0:3 * D0], PT_hi[:, kt, :], V_head[:, kt, :],
                       start=(kt == 0), stop=False)
                    last = mm(bank[2 + qt % 2][:, 0:2 * D0], PT_lo[:, kt, :], V_head[:, kt, 0:2 * D0],
                              start=False, stop=(kt == T - 1))
                last.then_inc(s_pv, 1)

            def attention_head(b, h, last_head):
                for qt in range(T):
                    transpose_probs(b, h, qt)
                    if qt + 2 < T:
                        score_tile(b, h, qt + 2)
                    elif not last_head:
                        score_tile(b, h + 1, qt + 2 - T)
                    times_v(b, h, qt)

            def project_out(b, layer, j, src, srcT, WoT, ready, need):
                n = b * 2 * T + layer * T
                if j < T:
                    if ready is not None:
                        pe.wait_ge(ready, need)
                    if j >= 2:
                        pe.wait_ge(s_at, n + j - 1)
                    for c in range(C):
                        last = nc.tensor.transpose(bank[j % 2][:, c * P:(c + 1) * P], src[:, c * P:(c + 1) * P],
                                                   ident[:, :])
                    last.then_inc(s_at_ps, 1)

            def project_out_mm(b, layer, j, srcT, WoT):
                n = b * 2 * T + layer * T
                pe.wait_ge(s_at, n + j + 1)
                if j >= 2:
                    pe.wait_ge(s_op_used, n + j - 1)
                for c in range(C):
                    last = mm(bank[2 + j % 2][:, 0:E], srcT[j % 2][:, c, :], WoT[:, c, :],
                              start=(c == 0), stop=(c == C - 1))
                last.then_inc(s_op, 1)

            def ffn(b, g):
                pe.wait_ge(s_hT, b * 16 + 4 + 2 * g + 2)
                for f in range(FC):
                    n = g * FC + f
                    if n >= 4:
                        pe.wait_ge(s_relu, b * (G * FC) + n - 3)
                    for c in range(C):
                        last = mm(wide[n % 4], WfcT[:, c, f * P:(f + 1) * P], hT[:, c, g * N:(g + 1) * N],
                                  start=(c == 0), stop=(c == C - 1))
                    last.then_inc(s_fc, 1)
                pe.wait_ge(s_hid, b * (G * FC) + (g + 1) * FC)
                for i in range(2):
                    if g == 1:
                        pe.wait_ge(s_ysb, b * 4 + i + 1)
                    for k in range(2):
                        j = 2 * i + k
                        for f in range(FC):
                            last = mm(bank[2 + i][:, k * E:(k + 1) * E], hid[:, f, j * P:(j + 1) * P],
                                      WprojT[:, f, :], start=(f == 0), stop=(f == FC - 1))
                    last.then_inc(s_y, 1)

            def project1(b, g):
                pe.wait_ge(s_hT, b * 16 + 8 + 2 * g + 2)
                for k in range(TG):
                    j = g * TG + k
                    if j >= 2:
                        pe.wait_ge(s_t1, b * T + j - 1)
                    for n in range(2):
                        for c in range(C):
                            last = mm(scores[j % 2][:, n * 512:(n + 1) * 512], hT[:, c, j * P:(j + 1) * P],
                                      WqkvuT1[:, c, n * 512:(n + 1) * 512], start=(c == 0), stop=(c == C - 1))
                    last.then_inc(s_p1, 1)

            def linear_tile(b, j):
                k = j % TG
                pe.wait_ge(s_elu, b * T + j + 1)
                pe.wait_ge(s_silu1, b * T + j + 1)
                if j > 0:
                    pe.wait_ge(s_o1sb, b * T + j)
                for i in range(4):
                    last = nc.tensor.transpose(bank[0][:, i * P:(i + 1) * P], T1[:, k, i * P:(i + 1) * P], ident[:, :])
                last.then_inc(s_qk_ps, 1)
                for c in range(C):
                    last = mm(bank[1][:, c * P:(c + 1) * P], T1[:, k, E + c * P:E + (c + 1) * P],
                              T1[:, k, 2 * E + c * P:2 * E + (c + 1) * P], start=True, stop=True)
                last.then_inc(s_kvps, 1)
                pe.wait_ge(s_qkT, b * T + j + 1)
                pe.wait_ge(s_qexp, b * T + j + 1)
                for c in range(C):
                    last = mm(bank[2 + c][:, :], kT[j % 2][:, c, :], qexp[:, c, :, :].rearrange("p h n -> p (h n)"),
                              start=True, stop=True)
                last.then_inc(s_en, 1)
                pe.wait_ge(s_em, b * T + j + 1)
                o = bank[0][:, 0:E]
                if j > 0:
                    for c in range(C):
                        mm(o[:, c * P:(c + 1) * P], qT[j % 2][:, c, :], KV[:, c, :], start=(c == 0), stop=False)
                for h in range(H1):
                    last = mm(o[:, h * D1:(h + 1) * D1], EM[:, h // 4, h % 4, :],
                              T1[:, k, 2 * E + h * D1:2 * E + (h + 1) * D1], start=(j == 0 and h == 0),
                              stop=(h == H1 - 1))
                last.then_inc(s_o1, 1)

            def three(dst, w_hi, w_lo, x_hi, x_lo, start, stop):
                mm(dst, w_hi, x_hi, start=start, stop=False)
                mm(dst, w_hi, x_lo, start=False, stop=False)
                return mm(dst, w_lo, x_hi, start=False, stop=stop)

            def expert_features(b, pair, u):
                s, g, hc = u // (G * HC), u // HC % G, u % HC
                if u % (G * HC) == 0:
                    pe.wait_ge(s_w12_lo, b * (2 * C * NX) + pair * (4 * C) + (s + 1) * 2 * C)
                for i in range(2):
                    for c in range(C):
                        cols = slice(hc * P, (hc + 1) * P)
                        toks = slice(g * N, (g + 1) * N)
                        last = three(wide[2 * i + u % 2], W12_hi[s][:, C * i + c, cols], W12_lo[s][:, C * i + c, cols],
                                     hT_hi[:, c, toks], hT_lo[:, c, toks], start=(c == 0), stop=(c == C - 1))
                last.then_inc(s_hx, 1)

            def expert_output(b, pair, u):
                s, g, hc = u // (G * HC), u // HC % G, u % HC
                if u % (G * HC) == 0:
                    pe.wait_ge(s_w3_lo, b * NX + pair * 2 + s + 1)
                if hc == 0:
                    pe.wait_ge(s_yx_used, b * (NX * T + T) + pair * (2 * T) + s * T + (g + 1) * TG)
                pe.wait_ge(s_g, b * (NX * G * HC) + pair * (2 * G * HC) + u + 1)
                for k in range(TG):
                    toks = slice(k * P, (k + 1) * P)
                    last = three(bank[2 * g + k // 2][:, (k % 2) * E:(k % 2 + 1) * E], G_hi[u % 2][:, toks],
                                 G_lo[u % 2][:, toks], W3_hi[:, hc, :], W3_lo[:, hc, :],
                                 start=(hc == 0 and k % 2 == 0), stop=(hc == HC - 1 and k % 2 == 1))
                last.then_inc(s_yx, 1)

            def expert_pair(b, pair, last_pair):
                for u in range(2 * G * HC):
                    if u + 1 < 2 * G * HC:
                        expert_features(b, pair, u + 1)
                    elif not last_pair:
                        expert_features(b, pair + 1, 0)
                    expert_output(b, pair, u)

            def experts(b):
                pe.wait_ge(s_hT, b * 16 + 16)
                for j in range(T):
                    for c in range(C):
                        last = mm(bank[2][:, j * NX:(j + 1) * NX], hT[:, c, j * P:(j + 1) * P], Wg_sb[:, c, :],
                                  start=(c == 0), stop=(c == C - 1))
                        if j == 0 and c == 0:
                            last.then_inc(s_yx, 1)
                last.then_inc(s_logit, 1)
                pe.wait_ge(s_hsp_lo, b + 1)
                expert_features(b, 0, 0)
                with pe.Fori(0, NX // 2 - 1) as pair:
                    expert_pair(b, pair, False)
                expert_pair(b, NX // 2 - 1, True)

            with pe.Fori(0, B) as b:
                for g in range(G):
                    transpose_norm(b, 0, g)
                project_qkv(b)
                pe.wait_ge(s_klo, b + 1)
                score_tile(b, 0, 0, first=True)
                score_tile(b, 0, 1)
                with pe.Fori(0, H0 - 1) as h:
                    attention_head(b, h, False)
                attention_head(b, H0 - 1, True)
                for j in range(T + 1):
                    if j < T:
                        project_out(b, 0, j, A[:, j, :], AT, WoT0, s_att, (b + 1) * TILES)
                    if j > 0:
                        project_out_mm(b, 0, j - 1, AT, WoT0)
                for g in range(G):
                    transpose_norm(b, 1, g)
                    ffn(b, g)
                for g in range(G):
                    transpose_norm(b, 2, g)
                    project1(b, g)
                    for k in range(TG):
                        linear_tile(b, g * TG + k)
                    for k in range(TG + 1):
                        j = g * TG + k
                        if k < TG:
                            project_out(b, 1, j, O1[:, k, :], AT1, WoT1, s_gated, b * G + g + 1)
                        if k > 0:
                            project_out_mm(b, 1, j - 1, AT1, WoT1)
                for g in range(G):
                    transpose_norm(b, 3, g)
                experts(b)

        @block.scalar
        def _(act):
            def copy(dst, src):
                return nc.scalar.activation(dst, src, ACT.Copy)

            act.wait_ge(s_loadm, 64)
            nc.scalar.activation(silu_rows, c_rows, ACT.Silu).then_inc(s_silu_c, 1)
            for i, (_, dst) in enumerate(wt_banks):
                act.wait_ge(s_wt_ps, i + 1)
                copy(dst, bank[i % 4][:, :].rearrange("p (a b) -> p a b", a=dst.shape[1])).then_inc(s_wt_sb, 1)
            act.wait_ge(s_silu_ps, 1)
            copy(siluT[:, :, :, :].rearrange("p l c b -> p (l c b)"), wide[0][:, 0:2 * C * B]).then_inc(s_silu_sb, 1)
            for l in range(2):
                for n in range(3):
                    act.wait_ge(s_modps, 3 * l + n + 1)
                    copy(mod_rows[:, l, n * 512:(n + 1) * 512], wide[n + 1][0:B, :]).then_inc(s_modcp, 1)

            def norm(b, k, g):
                act.wait_ge(s_var, b * (NLN * G) + k * G + g + 1)
                nc.scalar.activation(std[:, g * TG:(g + 1) * TG], mv[:, g * TG:(g + 1) * TG, 1], ACT.Sqrt,
                                     bias=eps_ln[:, 0:1]).then_inc(s_std, 1)
                for c in range(C):
                    act.wait_ge(s_hT_ps, b * (NLN * G * C) + (k * G + g) * C + c + 1)
                    copy(hT[:, c, g * N:(g + 1) * N], bank[c][:, :]).then_inc(s_hT, 1)

            def queries_hi(b, h, blk, part):
                for i in range(part * U, (part + 1) * U):
                    u, c = i // C, i % C
                    last = nc.scalar.activation(QW_hi[blk % 2][:, i, :], QT[:, c, blk * QB:(blk + 1) * QB], ACT.Copy,
                                                scale=filt[:, c, h, u:u + 1])
                last.then_inc(s_qw_hi, 1)

            def copy_sum(b, h, qt, first=False):
                t = b * TILES + h * T + qt
                act.wait_ge(s_prod, t * U + 1)
                if not first:
                    act.wait_ge(s_comb, t * 2)
                copy(sum_sb, wide[SUM]).then_inc(s_sum, 1)

            def exponentials(b, h, qt):
                act.wait_ge(s_max, b * TILES + h * T + qt + 1)
                nc.scalar.activation(SC[qt % 2], SC[qt % 2], ACT.Exp, bias=exp_bias[:, qt % 2:qt % 2 + 1],
                                     accum_out=row_sum[:, qt % 2:qt % 2 + 1]).then_inc(s_exp, 1)

            def attention_head(b, h, last_head):
                for qt in range(T):
                    t = b * TILES + h * T + qt
                    for half in range(2):
                        act.wait_ge(s_tr, t * 2 + half + 1)
                        nc.scalar.activation(PT_hi[:, 4 * half:4 * half + 4, :].rearrange("p a b -> p (a b)"),
                                             bank[half][:, :], ACT.Copy, scale=PSCALE).then_inc(s_pt_hi, 1)
                    if qt < 4:
                        queries_hi(b, h, qt // 2 + 2, qt % 2)
                    elif not last_head:
                        queries_hi(b, h + 1, qt // 2 - 2, qt % 2)
                    if qt + 2 < T:
                        copy_sum(b, h, qt + 2)
                    elif not last_head:
                        copy_sum(b, h + 1, qt + 2 - T)
                    if qt + 1 < T:
                        exponentials(b, h, qt + 1)
                    elif not last_head:
                        exponentials(b, h + 1, 0)

            def project_out(b, layer, j, srcT):
                n = b * 2 * T + layer * T
                act.wait_ge(s_at_ps, n + j + 1)
                if j >= 2:
                    act.wait_ge(s_op, n + j - 1)
                copy(srcT[j % 2].rearrange("p a b -> p (a b)"), bank[j % 2][:, 0:E]).then_inc(s_at, 1)

            def ffn(b, g):
                for f in range(FC):
                    n = g * FC + f
                    act.wait_ge(s_fc, b * (G * FC) + n + 1)
                    if n >= 2:
                        act.wait_ge(s_hid, b * (G * FC) + n - 1)
                    nc.scalar.activation(relu[n % 2], wide[n % 4], ACT.Relu).then_inc(s_relu, 1)
                for i in range(2):
                    act.wait_ge(s_y, b * 4 + g * 2 + i + 1)
                    if g == 1:
                        act.wait_ge(s_h, b * (NLN * G) + 4)
                    copy(Y[:, 2 * i:2 * i + 2, :].rearrange("p a b -> p (a b)"), bank[2 + i][:, :]).then_inc(s_ysb, 1)

            def second_attention(b, g):
                for k in range(TG):
                    j = g * TG + k
                    act.wait_ge(s_t1, b * T + j + 1)
                    nc.scalar.activation(T1[:, k, 2 * E:4 * E], T1[:, k, 2 * E:4 * E], ACT.Silu).then_inc(s_silu1, 1)
                for k in range(TG):
                    j = g * TG + k
                    act.wait_ge(s_neg, b * T + j + 1)
                    nc.scalar.activation(EX[:, k, :], EX[:, k, :], ACT.Exp).then_inc(s_eluexp, 1)
                for k in range(TG):
                    j = g * TG + k
                    act.wait_ge(s_qk_ps, b * T + j + 1)
                    copy(qT[j % 2].rearrange("p a b -> p (a b)"), bank[0][:, 0:E])
                    copy(kT[j % 2].rearrange("p a b -> p (a b)"), bank[0][:, E:2 * E]).then_inc(s_qkT, 1)
                    act.wait_ge(s_o1, b * T + j + 1)
                    copy(O1[:, k, :], bank[0][:, 0:E])
                    nc.scalar.activation(prod1[0], bank[0][:, 0:E], ACT.Square,
                                         accum_out=sumsq[:, j:j + 1]).then_inc(s_o1sb, 1)
                nc.scalar.drain()
                nc.scalar.activation(rms[:, g * TG:(g + 1) * TG], sumsq[:, g * TG:(g + 1) * TG],
                                     ACT.Sqrt).then_inc(s_rms, 1)
                for k in range(TG):
                    project_out(b, 1, g * TG + k, AT1)

            def expert_pair(b, pair, last_pair):
                for u in range(2 * G * HC):
                    s, v = u // (G * HC), u % (G * HC)
                    n = b * (NX * G * HC) + pair * (2 * G * HC) + u
                    act.wait_ge(s_hx, n + 1)
                    nc.scalar.activation(silu[u % 2], wide[u % 2], ACT.Silu).then_inc(s_silux, 1)
                    if v == 0:
                        act.wait_ge(s_yx, b * (NX * G * HC + 1) + pair * (2 * G * HC) + u + 1)
                        copy(W3_hi, W3s[s]).then_inc(s_w3_hi, 1)
                    act.wait_ge(s_gatedx, n + 1)
                    copy(G_hi[u % 2], gated[u % 2]).then_inc(s_g_hi, 1)
                    if 1 <= v <= 2 * C and (s == 0 or not last_pair):
                        if v == 1:
                            act.wait_ge(s_w[1 - s], b * (NX // 2 * 48) + pair * 48 + (48 + 48 * s))
                        copy(W12_hi[1 - s][:, v - 1, :], W12s[1 - s][:, v - 1, :]).then_inc(s_w12_hi, 1)

            def experts(b):
                act.wait_ge(s_hT, b * 16 + 16)
                for i in range(C * G):
                    cols = slice((i % G) * N, (i % G + 1) * N)
                    copy(hT_hi[:, i // G, cols], hT[:, i // G, cols]).then_inc(s_hsp_hi, 1)
                act.wait_ge(s_w[0], b * (NX // 2 * 48) + 48)
                for k in range(2 * C):
                    copy(W12_hi[0][:, k, :], W12s[0][:, k, :]).then_inc(s_w12_hi, 1)
                act.wait_ge(s_gap, b + 1)
                nc.scalar.activation(top[:, 3, :], top[:, 2, :], ACT.Exp).then_inc(s_gexp, 1)
                with act.Fori(0, NX // 2 - 1) as pair:
                    expert_pair(b, pair, False)
                expert_pair(b, NX // 2 - 1, True)

            with act.Fori(0, B) as b:
                for g in range(G):
                    norm(b, 0, g)
                for u in range(8):
                    oc, g = (u % 4) // 2, u % 2
                    act.wait_ge(s_qkv_ps, b * 12 + u + 1)
                    if u < 4:
                        dst, bias = QT[:, oc, g * N:(g + 1) * N], bq_col
                    else:
                        dst, bias = K_raw[:, oc, 1 + g * N:1 + (g + 1) * N], bk_col
                    nc.scalar.activation(dst, wide[u % 4], ACT.Identity, bias=bias[:, oc:oc + 1]).then_inc(s_qk_act, 1)
                nc.scalar.drain()
                for blk in range(2):
                    for part in range(2):
                        queries_hi(b, 0, blk, part)
                for i in range(C * U):
                    act.wait_ge(s_kpair, b * (C * U) + i + 1)
                    copy(K_hi[:, i // U, i % U, :], K_pair[i // U][:, i % U, :]).then_inc(s_khi, 1)
                copy_sum(b, 0, 0, first=True)
                copy_sum(b, 0, 1)
                exponentials(b, 0, 0)
                with act.Fori(0, H0 - 1) as h:
                    attention_head(b, h, False)
                attention_head(b, H0 - 1, True)
                for j in range(T):
                    project_out(b, 0, j, AT)
                for g in range(G):
                    norm(b, 1, g)
                    ffn(b, g)
                for g in range(G):
                    norm(b, 2, g)
                    second_attention(b, g)
                for g in range(G):
                    norm(b, 3, g)
                experts(b)

        @block.vector
        def _(dve):
            V_ = nc.vector

            V_.memset(qexp[:, :, :, :], 0.0)
            V_.memset(blockdiag[:, :], 0.0)
            for x in range(NX):
                V_.memset(rank_bonus[:, x:x + 1], float(NX - x))
            V_.drain()
            for h in range(4):
                V_.memset(blockdiag[32 * h:32 * h + 32, 32 * h:32 * h + 32], 1.0)
            dve.wait_ge(s_load, 16 * NLOAD)
            isd = float(1.0 / np.sqrt(D0))
            V_.tensor_tensor(conv_sum[:, :, :], conv_raw[:, :, :, 0], conv_raw[:, :, :, 2], ALU.add)
            V_.tensor_scalar(filt[:, :, :, FIRST], conv_raw[:, :, :, 0], isd, None, ALU.mult)
            V_.tensor_scalar(filt[:, :, :, LAST], conv_raw[:, :, :, 2], isd, None, ALU.mult)
            V_.drain()
            V_.tensor_tensor(filt[:, :, :, SUM], conv_sum[:, :, :], conv_raw[:, :, :, 1], ALU.add)
            V_.tensor_tensor(filt[:, :, :, DIFF], conv_sum[:, :, :], conv_raw[:, :, :, 1], ALU.subtract)
            V_.drain()
            for u in (SUM, DIFF):
                V_.tensor_scalar(filt[:, :, :, u], filt[:, :, :, u], 0.5 * isd, None, ALU.mult)
            V_.drain()
            dve.wait_ge(s_modcp, 6)
            m6 = mod_rows[:, :, :].rearrange("b l (m e) -> b l m e", e=E)
            for m in (1, 4):
                V_.tensor_scalar(m6[:, :, m, :], m6[:, :, m, :], 1.0, None, ALU.add)
            for i, m in enumerate((2, 5)):
                V_.tensor_scalar(mod_tmp[:, :, i, :], m6[:, :, m, :], -1.0, None, ALU.mult)
                V_.tensor_scalar(mod_tmp2[:, :, i, :], m6[:, :, m, :], 0.0, 2.0, ALU.is_ge, ALU.mult)
            V_.drain()
            for i, m in enumerate((2, 5)):
                V_.tensor_tensor(mod_tmp[:, :, i, :], mod_tmp[:, :, i, :], m6[:, :, m, :], ALU.max)
            V_.tensor_scalar(mod_tmp2[:, :, :, :], mod_tmp2[:, :, :, :], -1.0, None, ALU.add)
            V_.drain()
            V_.tensor_scalar(mod_tmp[:, :, :, :], mod_tmp[:, :, :, :], 0.25, None, ALU.max)
            V_.drain()
            for i, m in enumerate((2, 5)):
                V_.tensor_tensor(m6[:, :, m, :], mod_tmp[:, :, i, :], mod_tmp2[:, :, i, :], ALU.mult)
            V_.drain()
            V_.memset(mod_tmp[:, 0, 0, 0:1], 0.0).then_inc(s_modrow, 1)

            def row(l, m, n):
                return MOD[:, l, m:m + 1, :].to_broadcast([P, n, E])

            def norm(b, k, g):
                l, m = k // 2, 3 * (k % 2)
                js = slice(g * TG, (g + 1) * TG)
                if k == 0:
                    dve.wait_ge(s_x, b * 32 + 32)
                for j in range(g * TG, (g + 1) * TG):
                    V_.bn_stats(stats[:, j, :], X[:, j, :])
                V_.drain()
                for j in range(g * TG, (g + 1) * TG):
                    last = V_.bn_aggr(mv[:, j, :], stats[:, j, :])
                last.then_inc(s_var, 1)
                dve.wait_ge(s_std, b * (NLN * G) + k * G + g + 1)
                V_.reciprocal(rstd[:, js], std[:, js])
                V_.drain()
                for j in range(g * TG, (g + 1) * TG):
                    V_.tensor_scalar(Hn[:, j, :], X[:, j, :], mv[:, j, 0:1], rstd[:, j:j + 1], ALU.subtract, ALU.mult)
                V_.drain()
                V_.tensor_tensor(Hn[:, js, :], Hn[:, js, :], row(l, m + 1, TG), ALU.mult)
                V_.drain()
                V_.tensor_tensor(Hn[:, js, :], Hn[:, js, :], row(l, m, TG), ALU.add).then_inc(s_h, 1)

            def queries_lo(b, h, blk, part):
                dve.wait_ge(s_qw_hi, b * (2 * NQB * H0) + h * (2 * NQB) + 2 * blk + part + 1)
                for i in range(part * U, (part + 1) * U):
                    u, c = i // C, i % C
                    last = V_.scalar_tensor_tensor(out=QW_lo[blk % 2][:, i, :], in0=QT[:, c, blk * QB:(blk + 1) * QB],
                                                   scalar=filt[:, c, h, u:u + 1],
                                                   in1=QW_hi[blk % 2][:, i, :].bitcast(F32),
                                                   op0=ALU.mult, op1=ALU.subtract)
                last.then_inc(s_qw_lo, 1)

            def combine(b, h, qt):
                i, t = qt % 2, b * TILES + h * T + qt
                dve.wait_ge(s_sum, t + 1)
                dve.wait_ge(s_prod, t * U + FIRST + 1)
                V_.tensor_tensor(SC[i][:, 0, :], sum_sb, wide[FIRST], ALU.add).then_inc(s_comb, 1)
                dve.wait_ge(s_prod, t * U + LAST + 1)
                V_.tensor_tensor(SC[i][:, 1, :], sum_sb, wide[LAST], ALU.subtract).then_inc(s_comb, 1)
                V_.drain()
                dve.wait_ge(s_prod, t * U + DIFF + 1)
                V_.memset(carrier[:, :], 0.0)
                for k, op in ((0, ALU.add), (1, ALU.subtract)):
                    V_.tensor_tensor_reduce(out=SC[i][:, k, :], in0=SC[i][:, k, :], in1=wide[DIFF], scale=1.0,
                                            scalar=-3.4e38, op0=op, op1=ALU.max, accum_out=row_max[:, i, k:k + 1])
                V_.drain()
                V_.tensor_scalar(max_b[:, i:i + 1], row_max[:, i, 0:1], row_max[:, i, 1:2],
                                 convb_row[:, bass.ds(h, 1)], ALU.max, ALU.add)
                V_.drain()
                V_.tensor_scalar(exp_bias[:, i:i + 1], convb_row[:, bass.ds(h, 1)], max_b[:, i:i + 1], None,
                                 ALU.subtract).then_inc(s_max, 1)

            def split_v(b, h):
                part = [V_head[:, :, i * D0:(i + 1) * D0] for i in range(VP)]
                V_.tensor_copy(part[0], V[:, :, bass.ds(h * D0, D0)])
                V_.drain()
                V_.tensor_tensor(V_rest[:, :, :], V[:, :, bass.ds(h * D0, D0)], part[0], ALU.subtract)
                V_.drain()
                V_.tensor_copy(part[1], V_rest[:, :, :])
                V_.drain()
                V_.tensor_tensor(part[2], V_rest[:, :, :], part[1], ALU.subtract).then_inc(s_vhead, 1)

            def attention_head(b, h, last_head):
                for qt in range(T):
                    t = b * TILES + h * T + qt
                    for half in range(2):
                        dve.wait_ge(s_pt_hi, t * 2 + half + 1)
                        ks = slice(4 * half, 4 * half + 4)
                        last = V_.scalar_tensor_tensor(out=PT_lo[:, ks, :].rearrange("p a b -> p (a b)"),
                                                       in0=bank[half][:, :], scalar=PSCALE,
                                                       in1=PT_hi[:, ks, :].rearrange("p a b -> p (a b)"),
                                                       op0=ALU.mult, op1=ALU.subtract)
                    last.then_inc(s_pt_lo, 1)
                    if qt == 0:
                        split_v(b, h)
                    V_.reciprocal(row_inv[:, qt % 2:qt % 2 + 1], row_sum[:, qt % 2:qt % 2 + 1])
                    if qt < 4:
                        queries_lo(b, h, qt // 2 + 2, qt % 2)
                    elif not last_head:
                        queries_lo(b, h + 1, qt // 2 - 2, qt % 2)
                    if qt + 2 < T:
                        combine(b, h, qt + 2)
                    elif not last_head:
                        combine(b, h + 1, qt + 2 - T)
                    dve.wait_ge(s_pv, t + 1)
                    V_.reduce_sum(pv_sum[:, :], bank[2 + qt % 2][:, 0:VP * D0].rearrange("p (v d) -> p d v", v=VP), AX)
                    V_.drain()
                    V_.tensor_scalar(A[:, qt, bass.ds(h * D0, D0)], pv_sum[:, :], row_inv[:, qt % 2:qt % 2 + 1],
                                     1.0 / PSCALE, ALU.mult, ALU.mult).then_inc(s_att, 1)

            def project_out(b, layer, j, buf, bias):
                n = b * 2 * T + layer * T
                t = buf[j % 2]
                dve.wait_ge(s_op, n + j + 1)
                V_.tensor_tensor(t, bank[2 + j % 2][:, 0:E], bias[:, :], ALU.add).then_inc(s_op_used, 1)
                V_.drain()
                V_.tensor_tensor(t, t, MOD[:, layer, 2, :], ALU.mult)
                V_.drain()
                V_.tensor_tensor(X[:, j, :], X[:, j, :], t, ALU.add)
                V_.drain()

            def ffn(b, g):
                js = slice(g * TG, (g + 1) * TG)
                for f in range(FC):
                    n = g * FC + f
                    dve.wait_ge(s_relu, b * (G * FC) + n + 1)
                    if g == 1 and f == 0:
                        dve.wait_ge(s_y, b * 4 + 2)
                    V_.tensor_tensor(hid[:, f, :], relu[n % 2], relu[n % 2], ALU.mult).then_inc(s_hid, 1)
                dve.wait_ge(s_ysb, b * 4 + g * 2 + 2)
                V_.tensor_scalar(cnt, Y, 1.0, None, ALU.is_gt)
                V_.tensor_scalar(spk, Y, 1.0, None, ALU.is_gt)
                for step in range(4):
                    V_.scalar_tensor_tensor(out=leak, in0=(Y if step == 0 else mem), scalar=0.9, in1=Y,
                                            op0=ALU.mult, op1=ALU.add)
                    V_.drain()
                    V_.tensor_tensor(mem, leak, spk, ALU.subtract)
                    V_.drain()
                    V_.tensor_scalar(spk, mem, 1.0, None, ALU.is_gt)
                    V_.scalar_tensor_tensor(out=cnt, in0=mem, scalar=1.0, in1=cnt, op0=ALU.is_gt, op1=ALU.add)
                V_.drain()
                V_.tensor_scalar(cnt, cnt, 0.2, None, ALU.mult)
                V_.drain()
                V_.tensor_tensor(cnt, cnt, row(0, 5, TG), ALU.mult)
                V_.drain()
                V_.tensor_tensor(X[:, js, :], X[:, js, :], cnt, ALU.add)
                V_.drain()

            def second_attention(b, g):
                js = slice(g * TG, (g + 1) * TG)
                for k in range(TG):
                    j = g * TG + k
                    dve.wait_ge(s_p1, b * T + j + 1)
                    V_.tensor_tensor(T1[:, k, :], scores[j % 2][:, :], bqkvu_row[:, :], ALU.add).then_inc(s_t1, 1)
                V_.drain()
                for k in range(TG):
                    V_.tensor_scalar(EX[:, k, :], T1[:, k, 0:2 * E], 0.0, None, ALU.min).then_inc(s_neg, 1)
                for k in range(TG):
                    j = g * TG + k
                    dve.wait_ge(s_eluexp, b * T + j + 1)
                    V_.tensor_scalar(EX[:, k, :], EX[:, k, :], -1.0, None, ALU.add)
                V_.drain()
                for k in range(TG):
                    V_.scalar_tensor_tensor(out=T1[:, k, 0:2 * E], in0=T1[:, k, 0:2 * E], scalar=0.0, in1=EX[:, k, :],
                                            op0=ALU.max, op1=ALU.add).then_inc(s_elu, 1)
                for k in range(TG):
                    j = g * TG + k
                    dve.wait_ge(s_qkT, b * T + j + 1)
                    for h in range(4):
                        r = slice(32 * h, 32 * h + 32)
                        last = V_.tensor_copy(qexp[r, :, h, :],
                                              bank[0][r, 0:E].rearrange("p (c n) -> p c n", c=C))
                    last.then_inc(s_qexp, 1)
                    dve.wait_ge(s_kvps, b * T + j + 1)
                    V_.tensor_tensor(kv_new[:, :, :], bank[1][:, 0:E].rearrange("p (c n) -> p c n", c=C),
                                     blockdiag[:, :].unsqueeze(1).to_broadcast([P, C, P]), ALU.mult)
                    dve.wait_ge(s_en, b * T + j + 1)
                    for c in range(C):
                        last = V_.tensor_tensor(EM[:, c, :, :], bank[2 + c][:, :].rearrange("p (h n) -> p h n", h=4),
                                                causal[:, :].unsqueeze(1).to_broadcast([P, 4, P]), ALU.mult)
                    last.then_inc(s_em, 1)
                    dve.wait_ge(s_o1, b * T + j + 1)
                    if j == 0:
                        V_.tensor_copy(KV[:, :, :], kv_new[:, :, :])
                    else:
                        V_.tensor_tensor(KV[:, :, :], KV[:, :, :], kv_new[:, :, :], ALU.add)
                    V_.drain()
                dve.wait_ge(s_rms, b * G + g + 1)
                V_.tensor_scalar(rms[:, js], rms[:, js], float(E) ** -0.5, 1e-8, ALU.mult, ALU.add)
                V_.drain()
                V_.reciprocal(rms_inv[:, js], rms[:, js])
                V_.drain()
                for k in range(TG):
                    j = g * TG + k
                    V_.scalar_tensor_tensor(out=O1[:, k, :], in0=O1[:, k, :], scalar=rms_inv[:, j:j + 1],
                                            in1=scale_row[:, :], op0=ALU.mult, op1=ALU.mult)
                V_.drain()
                V_.tensor_tensor(O1[:, :, :], O1[:, :, :], T1[:, :, 3 * E:4 * E], ALU.mult).then_inc(s_gated, 1)
                for k in range(TG):
                    project_out(b, 1, g * TG + k, prod1, bo1_row)

            def router(b):
                L, eq, one1, L2, one2, cmb = (gate[:, i, :, :] for i in range(6))
                bonus = rank_bonus[:, :].unsqueeze(1).to_broadcast([P, T, NX])

                def wide_(i):
                    return top[:, i, :].unsqueeze(2).to_broadcast([P, T, NX])

                def first_largest(src, one, m):
                    V_.tensor_reduce(top[:, m, :], src, AX, ALU.max)
                    V_.drain()
                    V_.tensor_tensor(eq, src, wide_(m), ALU.is_equal)
                    V_.drain()
                    V_.tensor_tensor(eq, eq, bonus, ALU.mult)
                    V_.drain()
                    V_.tensor_reduce(top[:, 4, :], eq, AX, ALU.max)
                    V_.drain()
                    V_.tensor_tensor(one, eq, wide_(4), ALU.is_equal)
                    V_.drain()

                dve.wait_ge(s_logit, b + 1)
                V_.tensor_copy(L, bank[2][:, 0:T * NX].rearrange("p (t x) -> p t x", x=NX))
                V_.drain()
                first_largest(L, one1, 0)
                V_.tensor_scalar(L2, one1, -1.0, 1.0, ALU.mult, ALU.add)
                V_.drain()
                V_.tensor_tensor(L2, L2, L, ALU.mult)
                V_.tensor_scalar(cmb, one1, -3.0e38, None, ALU.mult)
                V_.drain()
                V_.tensor_tensor(L2, L2, cmb, ALU.add)
                V_.drain()
                first_largest(L2, one2, 1)
                V_.tensor_tensor(top[:, 2, :], top[:, 1, :], top[:, 0, :], ALU.subtract).then_inc(s_gap, 1)
                dve.wait_ge(s_gexp, b + 1)
                V_.tensor_scalar(top[:, 5, :], top[:, 3, :], 1.0, None, ALU.add)
                V_.drain()
                V_.reciprocal(top[:, 6, :], top[:, 5, :])
                V_.drain()
                V_.tensor_tensor(top[:, 7, :], top[:, 3, :], top[:, 6, :], ALU.mult)
                V_.tensor_tensor(one1, one1, wide_(6), ALU.mult)
                V_.drain()
                V_.tensor_tensor(one2, one2, wide_(7), ALU.mult)
                V_.drain()
                V_.tensor_tensor(cmb, one1, one2, ALU.add)
                for j in range(T):
                    V_.memset(ACC[:, j, :], 0.0).then_inc(s_yx_used, 1)
                V_.drain()

            def add_outputs(b, pair, s, g):
                u = s * G * HC + (g + 1) * HC
                dve.wait_ge(s_yx, b * (NX * G * HC + 1) + pair * (2 * G * HC) + u + 1)
                for k in range(TG):
                    j = g * TG + k
                    V_.scalar_tensor_tensor(out=ACC[:, j, :], in0=bank[j // 2][:, (j % 2) * E:(j % 2 + 1) * E],
                                            scalar=gate[:, 5, j, bass.ds(pair * 2 + s, 1)], in1=ACC[:, j, :],
                                            op0=ALU.mult, op1=ALU.add).then_inc(s_yx_used, 1)

            def expert_pair(b, pair, last_pair):
                for u in range(2 * G * HC):
                    s, v = u // (G * HC), u % (G * HC)
                    n = b * (NX * G * HC) + pair * (2 * G * HC) + u
                    dve.wait_ge(s_silux, n + 1)
                    V_.tensor_tensor(gated[u % 2], silu[u % 2], wide[2 + u % 2], ALU.mult).then_inc(s_gatedx, 1)
                    if v == 0:
                        dve.wait_ge(s_w3_hi, b * NX + pair * 2 + s + 1)
                        V_.tensor_tensor(W3_lo, W3s[s], W3_hi.bitcast(F32), ALU.subtract).then_inc(s_w3_lo, 1)
                    dve.wait_ge(s_g_hi, n + 1)
                    V_.tensor_tensor(G_lo[u % 2], gated[u % 2], G_hi[u % 2].bitcast(F32), ALU.subtract).then_inc(s_g, 1)
                    if 1 <= v <= 2 * C and (s == 0 or not last_pair):
                        dve.wait_ge(s_w12_hi, b * (2 * C * NX) + pair * (4 * C) + (s + 1) * 2 * C + v)
                        V_.tensor_tensor(W12_lo[1 - s][:, v - 1, :], W12s[1 - s][:, v - 1, :],
                                         W12_hi[1 - s][:, v - 1, :].bitcast(F32), ALU.subtract).then_inc(s_w12_lo, 1)
                    if u > 0 and u % HC == 0:
                        add_outputs(b, pair, (u - 1) // (G * HC), (u - 1) // HC % G)
                add_outputs(b, pair, 1, G - 1)

            def expert_parts(b):
                for i in range(C * G):
                    cols = slice((i % G) * N, (i % G + 1) * N)
                    dve.wait_ge(s_hsp_hi, b * (C * G) + i + 1)
                    last = V_.tensor_tensor(hT_lo[:, i // G, cols], hT[:, i // G, cols],
                                            hT_hi[:, i // G, cols].bitcast(F32), ALU.subtract)
                last.then_inc(s_hsp_lo, 1)
                for k in range(2 * C):
                    dve.wait_ge(s_w12_hi, b * (2 * C * NX) + k + 1)
                    V_.tensor_tensor(W12_lo[0][:, k, :], W12s[0][:, k, :], W12_hi[0][:, k, :].bitcast(F32),
                                     ALU.subtract).then_inc(s_w12_lo, 1)

            def experts(b):
                with dve.Fori(0, NX // 2 - 1) as pair:
                    expert_pair(b, pair, False)
                expert_pair(b, NX // 2 - 1, True)
                V_.drain()
                for g in range(G):
                    js = slice(g * TG, (g + 1) * TG)
                    V_.tensor_tensor(ACC[:, js, :], ACC[:, js, :], row(1, 5, TG), ALU.mult)
                V_.drain()
                for g in range(G):
                    js = slice(g * TG, (g + 1) * TG)
                    V_.tensor_tensor(X[:, js, :], X[:, js, :], ACC[:, js, :], ALU.add).then_inc(s_fin, 1)

            with dve.Fori(0, B) as b:
                for g in range(G):
                    norm(b, 0, g)
                for i in range(C):
                    for edge in (0, S + 1):
                        V_.memset(K_raw[:, i, edge:edge + 1], 0.0)
                V_.drain()
                for u in range(8, 12):
                    j = 2 * (u - 8)
                    dve.wait_ge(s_qkv_ps, b * 12 + u + 1)
                    V_.tensor_tensor(V[:, j:j + 2, :], wide[u % 4].rearrange("p (k e) -> p k e", k=2),
                                     bv_row[:, :].unsqueeze(1).to_broadcast([P, 2, E]), ALU.add).then_inc(s_v, 1)
                dve.wait_ge(s_qk_act, b * 8 + 8)
                for c in range(C):
                    def key(first):
                        return K_raw[:, c, 1 + first:first + S:2]
                    for u, (x, y, op) in ((SUM, (0, 1, ALU.add)), (FIRST, (-1, 1, ALU.subtract)),
                                          (LAST, (0, 2, ALU.subtract)), (DIFF, (1, 0, ALU.subtract))):
                        V_.tensor_tensor(K_pair[c][:, u, :], key(x), key(y), op).then_inc(s_kpair, 1)
                for i in range(C * U):
                    dve.wait_ge(s_khi, b * (C * U) + i + 1)
                    last = V_.tensor_tensor(K_lo[:, i // U, i % U, :], K_pair[i // U][:, i % U, :],
                                            K_hi[:, i // U, i % U, :].bitcast(F32), ALU.subtract)
                last.then_inc(s_klo, 1)
                for blk in range(2):
                    for part in range(2):
                        queries_lo(b, 0, blk, part)
                combine(b, 0, 0)
                combine(b, 0, 1)
                with dve.Fori(0, H0 - 1) as h:
                    attention_head(b, h, False)
                attention_head(b, H0 - 1, True)
                for j in range(T):
                    project_out(b, 0, j, prod, bo0_row)
                for g in range(G):
                    norm(b, 1, g)
                    ffn(b, g)
                for g in range(G):
                    norm(b, 2, g)
                    second_attention(b, g)
                for g in range(G):
                    norm(b, 3, g)
                expert_parts(b)
                router(b)
                experts(b)


_INS = ['L0_attn_query', 'L0_attn_Wq', 'L0_attn_bq', 'L0_attn_Wk', 'L0_attn_bk', 'L0_attn_Wv', 'L0_attn_bv',
        'L0_attn_Wo', 'L0_attn_bo', 'L0_attn_conv_w', 'L0_attn_conv_b', 'L0_ffn_W_fc', 'L0_ffn_W_proj', 'L0_c',
        'L0_wmod', 'L1_attn_Wq', 'L1_attn_bq', 'L1_attn_Wk', 'L1_attn_bk', 'L1_attn_Wv', 'L1_attn_bv', 'L1_attn_Wu',
        'L1_attn_bu', 'L1_attn_Wo', 'L1_attn_bo', 'L1_attn_scale', 'L1_ffn_Wg', 'L1_ffn_W1', 'L1_ffn_W2',
        'L1_ffn_W3', 'L1_c', 'L1_wmod']
_OUTS = [((4, 1024, 256), 'float32')]


def kernel(**inputs):
    import numpy as _np
    import concourse.bacc as _bacc
    from concourse import mybir as _mybir
    from concourse.bass_utils import run_bass_kernel_spmd as _run

    nc = _bacc.Bacc("TRN2", target_bir_lowering=False, num_devices=1)
    arrays, args = {}, []
    for name in _INS:
        a = _np.ascontiguousarray(inputs[name])
        arrays[f"in_{name}_dram"] = a
        args.append(nc.dram_tensor(f"in_{name}_dram", a.shape, _mybir.dt.from_np(a.dtype), kind="ExternalInput").ap())
    for i, (shape, dtype) in enumerate(_OUTS):
        dt = _mybir.dt.from_np(_np.dtype(dtype))
        args.append(nc.dram_tensor(f"out_{i}_dram", shape, dt, kind="ExternalOutput").ap())
    adaln_two_layer_kernel(nc, *args)
    r = _run(nc, [arrays], core_ids=[0])
    got = tuple(r.results[0][f"out_{i}_dram"] for i in range(len(_OUTS)))
    return got[0]
```

```python
from contextlib import ExitStack

import numpy as np

import concourse.bass as bass
from concourse import mybir

ALU = mybir.AluOpType
ACT = mybir.ActivationFunctionType
AX = mybir.AxisListType.X
F32 = mybir.dt.float32
F32R = mybir.dt.float32r
F16 = mybir.dt.float16
BF16 = mybir.dt.bfloat16
P = 128


def adaln_two_layer_kernel(nc, query, Wq0, bq0, Wk0, bk0, Wv0, bv0, Wo0, bo0, conv_w, conv_b, W_fc, W_proj, c0, wmod0,
                           Wq1, bq1, Wk1, bk1, Wv1, bv1, Wu1, bu1, Wo1, bo1, scale1, Wg, W1, W2, W3, c1, wmod1, out):
    B, S, E = query.shape
    H0, _, KS = conv_w.shape
    D0 = E // H0
    H1, D1 = 8, E // 8
    F = W_fc.shape[0]
    NX, _, HID = W1.shape
    T = S // P
    C = E // P
    FC = F // P
    HC = HID // P
    G = 2
    TG = T // G
    N = S // G
    TILES = H0 * T
    QB = 2 * P
    NQB = S // QB
    NMOD = 6 * E
    U = 4
    SUM, FIRST, LAST, DIFF = range(U)
    VP = 3
    PSCALE = float(2 ** 15)
    NLN = 4

    mod_rows_dram = nc.dram_tensor("mod_rows_scratch", (2, B, NMOD), F32, kind="Internal").ap()

    with ExitStack() as ctx:
        def sb(name, shape, dt=F32):
            return ctx.enter_context(nc.sbuf_tensor(name, shape, dt))

        def sem(name):
            return ctx.enter_context(nc.semaphore(name))

        ident = sb("ident", [P, P])
        causal = sb("causal", [P, P])
        blockdiag = sb("blockdiag", [P, P])
        rank_bonus = sb("rank_bonus", [P, NX])
        eps_ln = sb("eps_ln", [P, 1])
        WqT0 = sb("WqT0", [P, C, E])
        WkT0 = sb("WkT0", [P, C, E])
        WvT0 = sb("WvT0", [P, C, E])
        WoT0 = sb("WoT0", [P, C, E])
        WqkvuT1 = sb("WqkvuT1", [P, C, 4 * E])
        WoT1 = sb("WoT1", [P, C, E])
        WfcT = sb("WfcT", [P, C, F])
        WprojT = sb("WprojT", [P, FC, E])
        Wg_sb = sb("Wg_sb", [P, C, NX])
        bq_col = sb("bq_col", [P, C])
        bk_col = sb("bk_col", [P, C])
        bv_row = sb("bv_row", [P, E])
        bo0_row = sb("bo0_row", [P, E])
        bqkvu_row = sb("bqkvu_row", [P, 4 * E])
        bo1_row = sb("bo1_row", [P, E])
        scale_row = sb("scale_row", [P, E])
        conv_raw = sb("conv_raw", [P, C, H0, KS])
        conv_sum = sb("conv_sum", [P, C, H0])
        filt = sb("filt", [P, C, H0, U])
        convb_row = sb("convb_row", [P, H0])
        siluT = sb("siluT", [P, 2, C, B])

        X = sb("X", [P, T, E])
        MOD = sb("MOD", [P, 2, 6, E])
        Hn = sb("Hn", [P, T, E])
        hT = sb("hT", [P, C, S])
        c_rows = X[0:B, 0:2, :]
        silu_rows = X[0:B, 2:4, :]
        mod_rows = MOD[0:B, :, :, :].rearrange("b l m e -> b l (m e)")
        mod_tmp = Hn[0:B, 0:4, :].rearrange("b (l i) e -> b l i e", l=2)
        mod_tmp2 = Hn[0:B, 4:8, :].rearrange("b (l i) e -> b l i e", l=2)
        stats = sb("stats", [P, T, 6])
        mv = sb("mv", [P, T, 2])
        std = sb("std", [P, T])
        rstd = sb("rstd", [P, T])
        V_head = sb("V_head", [P, T, VP * D0], BF16)
        pv_sum = sb("pv_sum", [P, D0])
        carrier = sb("carrier", [P, 1])
        row_max = sb("row_max", [P, 2, 2])
        max_b = sb("max_b", [P, 2])
        exp_bias = sb("exp_bias", [P, 2])
        row_sum = sb("row_sum", [P, 2])
        row_inv = sb("row_inv", [P, 2])
        qexp = sb("qexp", [P, C, 4, P])
        KV = [sb(f"KV{i}", [P, C, P]) for i in range(2)]
        kv_new = sb("kv_new", [P, C, P])
        V_rest = kv_new[:, 0, :].rearrange("p (t d) -> p t d", d=D0)
        pool_tick = sb("pool_tick", [P, T])
        sumsq = sb("sumsq", [P, T])
        rms = sb("rms", [P, T])
        rms_inv = sb("rms_inv", [P, T])
        gate = sb("gate", [P, 6, T, NX])
        top = sb("top", [P, 8, T])
        ACC = Hn

        KB = 256
        work = sb("work", [P, 52 * KB])
        split = sb("split", [P, 64 * KB], F32R)

        def at(kib, *shape, space=work):
            n = int(np.prod(shape))
            flat = space[:, int(kib * KB):int(kib * KB) + n]
            if len(shape) == 1:
                return flat
            if len(shape) == 2:
                return flat.rearrange("p (a b) -> p a b", b=shape[1])
            return flat.rearrange("p (a b c) -> p a b c", b=shape[1], c=shape[2])

        X_next = [at(16, 2, 2 * E), hT[:, :, N:2 * N]]

        stage_sq = [at(2 * i, C, E) for i in range(9)]
        stage_fc = at(18, FC, E)
        stage_proj = hT[:, :, :]
        stage_mod = [at(26 + 12 * l, C, NMOD) for l in range(2)]
        QT = at(0, C, S)
        V = at(8, T, E)
        SC = [at(16 + 4 * i, 2, N) for i in range(2)]
        PT_hi = at(24, 2 * KB).bitcast(F16).rearrange("p (t q) -> p t q", q=P)
        PT_lo = at(26, 2 * KB).bitcast(F16).rearrange("p (t q) -> p t q", q=P)
        sum_sb = at(28, N)
        QW = [at(40 + 4 * i, U, QB) for i in range(2)]
        K_raw = at(16, C, S + 2)
        K_pair = [at(24.5, U, N), Hn[:, :, :].rearrange("p (u a) e -> p u (a e)", u=U)]
        A = at(32, T, E)
        K_hi = at(0, C, U, N, space=split)
        K_lo = at(16, C, U, N, space=split)
        QW_hi = [at(32 + 8 * i, U * C, QB, space=split) for i in range(2)]
        QW_lo = [at(48 + 8 * i, U * C, QB, space=split) for i in range(2)]
        AT = [at(28 + i, C, P) for i in range(2)]
        prod = at(30, 2, E)
        hid = at(0, FC, N)
        neg = at(16, TG, E)
        Y = at(20, TG, E)
        leak = at(24, TG, E)
        cnt = at(28, TG * E // 2).bitcast(BF16).rearrange("p (t e) -> p t e", e=E)
        relu = [at(32 + 2 * i, N) for i in range(2)]
        gained = at(36, TG, E)
        T1 = at(0, T, 4 * E)
        EX = at(32, TG, 2 * E)
        qT = [hT[:, 0, i * E:(i + 1) * E].rearrange("p (c n) -> p c n", c=C) for i in range(3)]
        kT = [hT[:, 1, i * E:(i + 1) * E].rearrange("p (c n) -> p c n", c=C) for i in range(3)]
        qexps = [qexp, at(32, C, 4 * P).rearrange("p c (h n) -> p c h n", h=4)]
        EM = at(36, C, 4, P)
        O1 = Hn
        AT1 = [T1[:, i, 0:E].rearrange("p (c n) -> p c n", c=C) for i in range(2)]
        prod1 = at(32, 2, E)
        silu = [at(8 + 2 * i, N) for i in range(2)]
        gated = [at(12 + 2 * i, N) for i in range(2)]
        result = at(0, T, E)
        slot_at = (40, 20)
        W12s = [at(slot_at[s], 2 * C, HID) for s in range(2)]
        W3s = [at(slot_at[s] + 8, HC, E) for s in range(2)]
        hT_hi = at(0, C, S, space=split)
        hT_lo = at(8, C, S, space=split)
        W12_hi = [at(16 + 16 * s, 2 * C, HID, space=split) for s in range(2)]
        W12_lo = [at(24 + 16 * s, 2 * C, HID, space=split) for s in range(2)]
        W3_hi = at(48, HC, E, space=split)
        W3_lo = at(52, HC, E, space=split)
        G_hi = [at(56 + 2 * i, N, space=split) for i in range(2)]
        G_lo = [at(60 + 2 * i, N, space=split) for i in range(2)]

        bank = [ctx.enter_context(nc.psum_tensor(f"bank{i}", [P, 512], F32)) for i in range(4)]
        score_a = ctx.enter_context(nc.psum_tensor("score_a", [P, 1024], F32))
        score_b = ctx.enter_context(nc.psum_tensor("score_b", [P, 1024], F32))
        scores = [score_a, score_b]
        wide = [score_a[:, 0:512], score_a[:, 512:1024], score_b[:, 0:512], score_b[:, 512:1024]]

        s_ident = sem("s_ident")
        s_load = sem("s_load")
        s_table = sem("s_table")
        s_loadm = sem("s_loadm")
        s_wt_ps = sem("s_wt_ps")
        s_wt_sb = sem("s_wt_sb")
        s_silu_c = sem("s_silu_c")
        s_silu_ps = sem("s_silu_ps")
        s_silu_sb = sem("s_silu_sb")
        s_modps = sem("s_modps")
        s_modcp = sem("s_modcp")
        s_modrow = sem("s_modrow")
        s_modst = sem("s_modst")
        s_const = sem("s_const")
        s_next = sem("s_next")
        s_x = sem("s_x")
        s_out = sem("s_out")
        s_var = sem("s_var")
        s_std = sem("s_std")
        s_h = sem("s_h")
        s_hT_ps = sem("s_hT_ps")
        s_hT = sem("s_hT")
        s_qkv_ps = sem("s_qkv_ps")
        s_qk_act = sem("s_qk_act")
        s_v = sem("s_v")
        s_kpair = sem("s_kpair")
        s_khi = sem("s_khi")
        s_klo = sem("s_klo")
        s_vhead = sem("s_vhead")
        s_qw = sem("s_qw")
        s_qw_hi = sem("s_qw_hi")
        s_qw_lo = sem("s_qw_lo")
        s_prod = sem("s_prod")
        s_sum = sem("s_sum")
        s_comb = sem("s_comb")
        s_max = sem("s_max")
        s_exp = sem("s_exp")
        s_tr = sem("s_tr")
        s_pt_hi = sem("s_pt_hi")
        s_pt_lo = sem("s_pt_lo")
        s_pv = sem("s_pv")
        s_att = sem("s_att")
        s_at_ps = sem("s_at_ps")
        s_at = sem("s_at")
        s_op = sem("s_op")
        s_op_even = sem("s_op_even")
        s_op_used = sem("s_op_used")
        s_fc = sem("s_fc")
        s_relu = sem("s_relu")
        s_hid = sem("s_hid")
        s_y = sem("s_y")
        s_ysb = sem("s_ysb")
        s_p1 = sem("s_p1")
        s_p1sb = sem("s_p1sb")
        s_t1 = sem("s_t1")
        s_neg = sem("s_neg")
        s_eluexp = sem("s_eluexp")
        s_silu1 = sem("s_silu1")
        s_elu = sem("s_elu")
        s_qk_ps = sem("s_qk_ps")
        s_qkT = sem("s_qkT")
        s_qexp = sem("s_qexp")
        s_zero = sem("s_zero")
        s_en = sem("s_en")
        s_em = sem("s_em")
        s_kvps = sem("s_kvps")
        s_kv = sem("s_kv")
        s_o1 = sem("s_o1")
        s_o1sb = sem("s_o1sb")
        s_rms = sem("s_rms")
        s_gated = sem("s_gated")
        s_logit = sem("s_logit")
        s_gap = sem("s_gap")
        s_gexp = sem("s_gexp")
        s_hsp_hi = sem("s_hsp_hi")
        s_hsp_lo = sem("s_hsp_lo")
        s_w = [sem(f"s_w{s}") for s in range(2)]
        s_w12_hi = sem("s_w12_hi")
        s_w12_lo = sem("s_w12_lo")
        s_w3_hi = sem("s_w3_hi")
        s_w3_lo = sem("s_w3_lo")
        s_hx = sem("s_hx")
        s_silux = sem("s_silux")
        s_gatedx = sem("s_gatedx")
        s_g_hi = sem("s_g_hi")
        s_g = sem("s_g")
        s_yx = sem("s_yx")
        s_yx_used = sem("s_yx_used")
        s_acc = sem("s_acc")
        s_fin = sem("s_fin")

        NLOAD = 9 + 2 + 1
        NTABLE = 2 + 8 + 1 + H0
        square_weights = [(Wq0, WqT0, None), (Wk0, WkT0, None), (Wv0, WvT0, None), (Wo0, WoT0, None),
                          (Wq1, WqkvuT1, 0), (Wk1, WqkvuT1, 1), (Wv1, WqkvuT1, 2), (Wu1, WqkvuT1, 3),
                          (Wo1, WoT1, None)]
        wt_banks = []
        for i, (_, dst, slot) in enumerate(square_weights):
            blocks = [stage_sq[i][:, oc, ic * P:(ic + 1) * P] for ic in range(C) for oc in range(C)]
            wt_banks.append((blocks, dst[:, :, :] if slot is None else dst[:, :, slot * E:(slot + 1) * E]))
        for ic in range(C):
            for half in range(2):
                blocks = [stage_fc[:, 4 * half + k, ic * P:(ic + 1) * P] for k in range(4)]
                wt_banks.append((blocks, WfcT[:, ic:ic + 1, half * 512:(half + 1) * 512]))
        for pair in range(FC // 2):
            blocks = [stage_proj[:, oc, f * P:(f + 1) * P] for f in (2 * pair, 2 * pair + 1) for oc in range(C)]
            wt_banks.append((blocks, WprojT[:, 2 * pair:2 * pair + 2, :]))

        def w3_chunk(v):
            return {G * HC - 2: 0, G * HC - 1: 1, 0: 2, 1: 3}.get(v)

        x_dram = query.rearrange("b (t p) e -> b p t e", p=P)
        out_dram = out.rearrange("b (t p) e -> b p t e", p=P)

        block = ctx.enter_context(nc.Block())

        @block.sync
        def _(sp):
            for i, (w, _, _) in enumerate(square_weights):
                sp.dma_start(stage_sq[i], w.rearrange("(o p) i -> p o i", p=P)).then_inc(s_load, 16)
            sp.dma_start(stage_fc, W_fc.rearrange("(o p) i -> p o i", p=P)).then_inc(s_load, 16)
            sp.dma_start(stage_proj, W_proj.rearrange("(o p) i -> p o i", p=P)).then_inc(s_load, 16)
            sp.dma_start(Wg_sb[:, :, :], Wg.rearrange("(c p) x -> p c x", p=P)).then_inc(s_load, 16)

            def load_expert(e, s):
                for i, w in enumerate((W1, W2)):
                    sp.dma_start(W12s[s][:, C * i:C * i + C, :],
                                 w[e].rearrange("(c p) h -> p c h", p=P)).then_inc(s_w[s], 16)
                sp.dma_start(W3s[s], W3[e].rearrange("(c p) n -> p c n", p=P)).then_inc(s_w[s], 16)

            def later_experts(b):
                with sp.Fori(1, NX // 2) as pair:
                    for s in range(2):
                        sp.wait_ge(s_w3_lo, b * (NX * HC) + pair * (2 * HC) + (s - 1) * HC)
                        load_expert(pair * 2 + s, s)

            def load_batch(b, g):
                tiles = slice(g * TG, (g + 1) * TG)
                sp.dma_start(X[:, tiles, :], x_dram[b, :, tiles, :]).then_inc(s_x, 16)

            def load_mod(b, l, landed):
                sp.dma_start(MOD[:, l, :, :].rearrange("p m e -> p (m e)"),
                             mod_rows_dram[l, b, :].partition_broadcast(P)).then_inc(landed, 16)

            def load_next(b):
                for g in range(G):
                    for a in range(2):
                        first = g * TG + 2 * a
                        sp.dma_start(X_next[g][:, a, :].rearrange("p (k e) -> p k e", k=2),
                                     x_dram[b, :, first:first + 2, :]).then_inc(s_next, 16)
                load_mod(b, 0, s_next)

            def batch(b, last_batch):
                sp.wait_ge(s_op_used, b * T + 1)
                load_expert(0, 0)
                sp.wait_ge(s_h, b * (NLN * G) + (NLN * G - 1))
                load_expert(1, 1)
                if not last_batch:
                    sp.wait_ge(s_g, b * (NX * G * HC) + 1)
                    load_next(b + 1)
                later_experts(b)
                for g in range(G):
                    sp.wait_ge(s_fin, b * G + g + 1)
                    tiles = slice(g * TG, (g + 1) * TG)
                    sp.dma_start(out_dram[b, :, tiles, :], result[:, tiles, :]).then_inc(s_out, 16)
                if not last_batch:
                    sp.wait_ge(s_out, (b + 1) * G * 16)
                    for g in range(G):
                        load_batch(b + 1, g)
                    load_mod(b + 1, 1, s_x)

            sp.wait_ge(s_modrow, 1)
            for l in range(2):
                sp.dma_start(mod_rows_dram[l], mod_rows[:, l, :]).then_inc(s_modst, 16)
            sp.wait_ge(s_modst, 32)
            sp.wait_ge(s_wt_sb, len(wt_banks))
            load_next(0)
            for g in range(G):
                load_batch(0, g)
            load_mod(0, 1, s_x)
            with sp.Fori(0, B - 1) as b:
                batch(b, False)
            batch(B - 1, True)
            sp.wait_ge(s_out, B * G * 16)

        @block.gpsimd
        def _(pool):
            pool.dma_start(c_rows[:, 0, :], c0).then_inc(s_loadm, 16)
            pool.dma_start(c_rows[:, 1, :], c1).then_inc(s_loadm, 16)
            pool.dma_start(stage_mod[0], wmod0.rearrange("(c p) n -> p c n", p=P)).then_inc(s_loadm, 16)
            pool.dma_start(stage_mod[1], wmod1.rearrange("(c p) n -> p c n", p=P)).then_inc(s_loadm, 16)
            nc.gpsimd.memset(ident[:, :], 0.0)
            nc.gpsimd.memset(causal[:, :], 1.0)
            nc.gpsimd.drain()
            nc.gpsimd.affine_select(out=ident[:, :], in_=ident[:, :], compare_op=ALU.not_equal, fill=1.0, base=0,
                                    pattern=[[-1, P]], channel_multiplier=1)
            nc.gpsimd.affine_select(out=causal[:, :], in_=causal[:, :], compare_op=ALU.is_ge, fill=0.0, base=0,
                                    pattern=[[1, P]], channel_multiplier=-1)
            nc.gpsimd.drain()
            nc.gpsimd.memset(eps_ln[:, :], 1e-5).then_inc(s_ident, 1)

            nc.gpsimd.memset(pool_tick[:, :], 0.0)
            nc.gpsimd.drain()

            def filtered(h, m):
                blk, part = m // 2, m % 2
                us = slice(part * 2, part * 2 + 2)
                q = QT[:, :, blk * QB:(blk + 1) * QB].unsqueeze(1).to_broadcast([P, 2, C, QB])
                w = filt[:, :, h, us].rearrange("p c u -> p u c").unsqueeze(3).to_broadcast([P, 2, C, QB])
                out_ = QW[m % 2].rearrange("p (u c) q -> p u c q", c=C)
                nc.gpsimd.tensor_tensor(out_, q, w, ALU.mult).then_inc(s_qw, 1)

            def tick(m):
                return nc.gpsimd.tensor_tensor(pool_tick[:, m:m + 1], ident[:, 0:1], ident[:, 0:1], ALU.mult)

            def filter_head(b, h, last_head):
                for m in range(2 * NQB):
                    n = b * (2 * NQB * H0) + h * (2 * NQB) + m
                    if m + 1 < 2 * NQB or not last_head:
                        pool.wait_ge(s_qw_lo, n + (b + 1))
                        tick(m)
                        filtered(h if m + 1 < 2 * NQB else h + 1, (m + 1) % (2 * NQB))
                    pool.wait_ge(s_qw_hi, n + 1)
                    blk, part = m // 2, m % 2
                    nc.gpsimd.tensor_tensor(QW_lo[blk % 2][:, part * U:(part + 1) * U, :], QW[m % 2],
                                            QW_hi[blk % 2][:, part * U:(part + 1) * U, :].bitcast(F32),
                                            ALU.subtract).then_inc(s_qw_lo, 1)

            with pool.Fori(0, B) as b:
                pool.wait_ge(s_qk_act, b * 8 + 4)
                tick(0).then_inc(s_qw_lo, 1)
                nc.gpsimd.drain()
                filtered(0, 0)
                with pool.Fori(0, H0 - 1) as h:
                    filter_head(b, h, False)
                filter_head(b, H0 - 1, True)
                for j in range(T):
                    pool.wait_ge(s_p1sb, b * T + j + 1)
                    nc.gpsimd.tensor_tensor(T1[:, j, :], T1[:, j, :], bqkvu_row[:, :], ALU.add).then_inc(s_t1, 1)
                nc.gpsimd.drain()
                pool.wait_ge(s_elu, (b + 1) * T)
                tick(3)
                nc.gpsimd.memset(qexps[1], 0.0).then_inc(s_zero, 1)
                for k in range(2 * C):
                    pool.wait_ge(s_w12_hi, b * (2 * C * NX) + k + 1)
                    nc.gpsimd.tensor_tensor(W12_lo[0][:, k, :], W12s[0][:, k, :], W12_hi[0][:, k, :].bitcast(F32),
                                            ALU.subtract).then_inc(s_w12_lo, 1)
                for k in range(2):
                    pool.wait_ge(s_w3_hi, b * (NX * HC) + k + 1)
                    nc.gpsimd.tensor_tensor(W3_lo[:, k, :], W3s[0][:, k, :], W3_hi[:, k, :].bitcast(F32),
                                            ALU.subtract).then_inc(s_w3_lo, 1)
                nc.gpsimd.drain()
                pool.wait_ge(s_hT_ps, (b + 1) * (NLN * G * C))
                tick(2)
                nc.gpsimd.memset(ACC[:, :, :], 0.0).then_inc(s_acc, 1)

        @block.tensor
        def _(pe):
            mm = nc.tensor.matmul

            pe.wait_ge(s_ident, 1)
            pe.wait_ge(s_silu_c, 1)
            for l in range(2):
                for c in range(C):
                    k = l * C + c
                    last = nc.tensor.transpose(wide[0][:, k * B:(k + 1) * B], silu_rows[:, l, c * P:(c + 1) * P],
                                               ident[0:B, 0:B])
            last.then_inc(s_silu_ps, 1)
            pe.wait_ge(s_loadm, 64)
            pe.wait_ge(s_silu_sb, 1)
            for l in range(2):
                if l == 1:
                    pe.wait_ge(s_modcp, 3)
                for n in range(3):
                    for c in range(C):
                        last = mm(wide[n + 1][0:B, :], siluT[:, l, c, :],
                                  stage_mod[l][:, c, n * 512:(n + 1) * 512], start=(c == 0), stop=(c == C - 1))
                    last.then_inc(s_modps, 1)

            pe.wait_ge(s_load, 16 * NLOAD)
            for i, (blocks, _) in enumerate(wt_banks):
                if i >= 4:
                    pe.wait_ge(s_wt_sb, i - 3)
                for k, blk in enumerate(blocks):
                    last = nc.tensor.transpose(bank[i % 4][:, k * P:(k + 1) * P], blk, ident[:, :])
                last.then_inc(s_wt_ps, 1)

            def transpose_norm(b, k, g):
                for c in range(C):
                    pe.wait_ge(s_h, b * (NLN * G) + k * G + g + 1)
                    if g == 1:
                        if k < NLN - 1:
                            pe.wait_ge(s_hT, b * (NLN * G * C) + (k * G) * C + c + 1)
                        else:
                            pe.wait_ge(s_hsp_hi, b * (C * G) + c + 1)
                    for j in range(TG):
                        last = nc.tensor.transpose(bank[c][:, j * P:(j + 1) * P],
                                                   Hn[:, g * TG + j, c * P:(c + 1) * P], ident[:, :])
                    last.then_inc(s_hT_ps, 1)

            def project_qkv(b):
                pe.wait_ge(s_hT, b * 16 + 4)
                for u in range(12):
                    if u >= 4:
                        pe.wait_ge(s_qk_act, b * 8 + u - 3)
                    dst = wide[u % 4]
                    if u < 8:
                        w, oc, g = (WqT0, WkT0)[u // 4], (u % 4) // 2, u % 2
                        for c in range(C):
                            last = mm(dst, w[:, c, oc * P:(oc + 1) * P], hT[:, c, g * N:(g + 1) * N],
                                      start=(c == 0), stop=(c == C - 1))
                    else:
                        for k in range(2):
                            j = 2 * (u - 8) + k
                            start = 2 * P * (j % 4) + j // 4
                            for c in range(C):
                                last = mm(dst[:, k * E:(k + 1) * E], hT[:, c, start:start + 2 * P - 1:2], WvT0[:, c, :],
                                          start=(c == 0), stop=(c == C - 1))
                    last.then_inc(s_qkv_ps, 1)

            def score_tile(b, h, qt, first=False):
                ring, col = qt // 2 % 2, (qt % 2) * P
                t = b * TILES + h * T + qt
                if qt % 2 == 0:
                    pe.wait_ge(s_qw_lo, b * (2 * NQB * H0 + 1) + h * (2 * NQB) + qt + 3)
                for u in range(U):
                    if not first:
                        done, count = {SUM: (s_sum, t), FIRST: (s_comb, t * 2 - 1), LAST: (s_comb, t * 2),
                                       DIFF: (s_max, t)}[u]
                        pe.wait_ge(done, count)
                    for c in range(C):
                        i = u * C + c
                        hi, lo = QW_hi[ring][:, i, col:col + P], QW_lo[ring][:, i, col:col + P]
                        for w, k in ((hi, K_hi), (hi, K_lo), (lo, K_hi)):
                            last = mm(wide[u], w, k[:, c, u, :], start=(c == 0 and w is hi and k is K_hi),
                                      stop=(c == C - 1 and w is lo))
                    last.then_inc(s_prod, 1)

            def transpose_probs(b, h, qt):
                pe.wait_ge(s_exp, b * TILES + h * T + qt + 1)
                for half in range(2):
                    for k in range(4):
                        last = nc.tensor.transpose(bank[half][:, k * P:(k + 1) * P],
                                                   SC[qt % 2][:, half, k * P:(k + 1) * P], ident[:, :])
                    last.then_inc(s_tr, 1)

            def times_v(b, h, qt):
                if qt == 0:
                    pe.wait_ge(s_vhead, b * H0 + h + 1)
                pe.wait_ge(s_pt_lo, b * TILES + h * T + qt + 1)
                for kt in range(T):
                    mm(bank[2 + qt % 2][:, 0:3 * D0], PT_hi[:, kt, :], V_head[:, kt, :],
                       start=(kt == 0), stop=False)
                    last = mm(bank[2 + qt % 2][:, 0:2 * D0], PT_lo[:, kt, :], V_head[:, kt, 0:2 * D0],
                              start=False, stop=(kt == T - 1))
                last.then_inc(s_pv, 1)

            def attention_head(b, h, last_head):
                for qt in range(T):
                    transpose_probs(b, h, qt)
                    if qt + 2 < T:
                        score_tile(b, h, qt + 2)
                    elif not last_head:
                        score_tile(b, h + 1, qt + 2 - T)
                    times_v(b, h, qt)

            def project_out(b, layer, j, src, srcT, WoT, ready, need):
                n = b * 2 * T + layer * T
                if j < T:
                    if ready is not None:
                        pe.wait_ge(ready, need)
                    if j >= 2:
                        pe.wait_ge(s_at, n + j - 1)
                    for c in range(C):
                        last = nc.tensor.transpose(bank[j % 2][:, c * P:(c + 1) * P], src[:, c * P:(c + 1) * P],
                                                   ident[:, :])
                    last.then_inc(s_at_ps, 1)

            def project_out_mm(b, layer, j, srcT, WoT):
                pe.wait_ge(s_at, b * 2 * T + layer * T + j + 1)
                if j >= 4 and j % 2 == 0:
                    pe.wait_ge(s_op_used, b * T + layer * (T // 2) + j // 2 - 1)
                for c in range(C):
                    last = mm(bank[2 + j // 2 % 2][:, (j % 2) * E:(j % 2 + 1) * E], srcT[j % 2][:, c, :], WoT[:, c, :],
                              start=(c == 0), stop=(c == C - 1))
                if j % 2 == 1:
                    last.then_inc(s_op, 1)
                else:
                    last.then_inc(s_op_even, 1)

            def ffn(b, g):
                pe.wait_ge(s_hT, b * 16 + 4 + 2 * g + 2)
                for f in range(FC):
                    n = g * FC + f
                    if n >= 4:
                        pe.wait_ge(s_relu, b * (G * FC) + n - 3)
                    for c in range(C):
                        last = mm(wide[n % 4], WfcT[:, c, f * P:(f + 1) * P], hT[:, c, g * N:(g + 1) * N],
                                  start=(c == 0), stop=(c == C - 1))
                    last.then_inc(s_fc, 1)
                pe.wait_ge(s_hid, b * (G * FC) + (g + 1) * FC)
                for i in range(2):
                    if g == 1:
                        pe.wait_ge(s_ysb, b * 4 + i + 1)
                    for k in range(2):
                        j = 2 * i + k
                        for f in range(FC):
                            last = mm(bank[2 + i][:, k * E:(k + 1) * E], hid[:, f, j * P:(j + 1) * P],
                                      WprojT[:, f, :], start=(f == 0), stop=(f == FC - 1))
                    last.then_inc(s_y, 1)

            def project1(b, g):
                pe.wait_ge(s_hT, b * 16 + 8 + 2 * g + 2)
                for k in range(TG):
                    j = g * TG + k
                    if j >= 2:
                        pe.wait_ge(s_p1sb, b * T + j - 1)
                    for n in range(2):
                        for c in range(C):
                            last = mm(scores[j % 2][:, n * 512:(n + 1) * 512], hT[:, c, j * P:(j + 1) * P],
                                      WqkvuT1[:, c, n * 512:(n + 1) * 512], start=(c == 0), stop=(c == C - 1))
                    last.then_inc(s_p1, 1)

            def linear_a(b, j):
                if j == 0:
                    pe.wait_ge(s_p1sb, (b + 1) * T)
                pe.wait_ge(s_elu, b * T + j + 1)
                if j >= 2:
                    pe.wait_ge(s_qexp, b * T + j - 1)
                for i in range(4):
                    last = nc.tensor.transpose(wide[j % 2][:, i * P:(i + 1) * P], T1[:, j, i * P:(i + 1) * P],
                                               ident[:, :])
                last.then_inc(s_qk_ps, 1)

            def key_values(b, j):
                pe.wait_ge(s_silu1, b * T + j + 1)
                if j >= 2:
                    pe.wait_ge(s_kv, b * T + j - 1)
                for c in range(C):
                    last = mm(wide[2 + j % 2][:, c * P:(c + 1) * P], T1[:, j, E + c * P:E + (c + 1) * P],
                              T1[:, j, 2 * E + c * P:2 * E + (c + 1) * P], start=True, stop=True)
                last.then_inc(s_kvps, 1)

            def linear_b(b, j, c):
                pe.wait_ge(s_qkT, b * T + j + 1)
                pe.wait_ge(s_qexp, b * T + j + 1)
                if j >= 1:
                    pe.wait_ge(s_em, (b * T + j) * C + c - 1)
                last = mm(bank[2 + c][:, :], kT[j % 3][:, c, :], qexps[j % 2][:, c, :, :].rearrange("p h n -> p (h n)"),
                          start=True, stop=True)
                last.then_inc(s_en, 1)

            def linear_c(b, j):
                o = bank[j % 2][:, 0:E]
                if j >= 2:
                    pe.wait_ge(s_o1sb, b * T + j - 1)
                if j > 0:
                    pe.wait_ge(s_kv, b * T + j)
                    for c in range(C):
                        mm(o[:, c * P:(c + 1) * P], qT[j % 3][:, c, :], KV[j % 2][:, c, :], start=(c == 0), stop=False)
                pe.wait_ge(s_em, (b * T + j + 1) * C)
                for h in range(H1):
                    last = mm(o[:, h * D1:(h + 1) * D1], EM[:, h // 4, h % 4, :],
                              T1[:, j, 2 * E + h * D1:2 * E + (h + 1) * D1], start=(j == 0 and h == 0),
                              stop=(h == H1 - 1))
                last.then_inc(s_o1, 1)

            def three(dst, w_hi, w_lo, x_hi, x_lo, start, stop):
                mm(dst, w_hi, x_hi, start=start, stop=False)
                mm(dst, w_hi, x_lo, start=False, stop=False)
                return mm(dst, w_lo, x_hi, start=False, stop=stop)

            def expert_features(b, pair, u):
                s, g, hc = u // (G * HC), u // HC % G, u % HC
                if u % (G * HC) == 0:
                    pe.wait_ge(s_w12_lo, b * (2 * C * NX) + pair * (4 * C) + (s + 1) * 2 * C)
                if s == 0 and u % HC == 0:
                    pe.wait_ge(s_hsp_lo, b * G + g + 1)
                for i in range(2):
                    for c in range(C):
                        cols = slice(hc * P, (hc + 1) * P)
                        toks = slice(g * N, (g + 1) * N)
                        last = three(wide[2 * i + u % 2], W12_hi[s][:, C * i + c, cols], W12_lo[s][:, C * i + c, cols],
                                     hT_hi[:, c, toks], hT_lo[:, c, toks], start=(c == 0), stop=(c == C - 1))
                last.then_inc(s_hx, 1)

            def expert_output(b, pair, u):
                s, g, hc = u // (G * HC), u // HC % G, u % HC
                if g == 0:
                    pe.wait_ge(s_w3_lo, b * (NX * HC) + pair * (2 * HC) + s * HC + hc + 1)
                if hc == 0:
                    pe.wait_ge(s_yx_used, b * (NX * T + T) + pair * (2 * T) + s * T + (g + 1) * TG)
                pe.wait_ge(s_g, b * (NX * G * HC) + pair * (2 * G * HC) + u + 1)
                for k in range(TG):
                    toks = slice(k * P, (k + 1) * P)
                    last = three(bank[2 * g + k // 2][:, (k % 2) * E:(k % 2 + 1) * E], G_hi[u % 2][:, toks],
                                 G_lo[u % 2][:, toks], W3_hi[:, hc, :], W3_lo[:, hc, :],
                                 start=(hc == 0 and k % 2 == 0), stop=(hc == HC - 1 and k % 2 == 1))
                last.then_inc(s_yx, 1)

            def expert_pair(b, pair, last_pair):
                for u in range(2 * G * HC):
                    if u + 1 < 2 * G * HC:
                        expert_features(b, pair, u + 1)
                    elif not last_pair:
                        expert_features(b, pair + 1, 0)
                    expert_output(b, pair, u)

            def experts(b):
                expert_features(b, 0, 0)
                pe.wait_ge(s_hT, b * 16 + 16)
                for j in range(T):
                    for c in range(C):
                        last = mm(bank[2][:, j * NX:(j + 1) * NX], hT[:, c, j * P:(j + 1) * P], Wg_sb[:, c, :],
                                  start=(c == 0), stop=(c == C - 1))
                        if j == 0 and c == 0:
                            last.then_inc(s_yx, 1)
                last.then_inc(s_logit, 1)
                with pe.Fori(0, NX // 2 - 1) as pair:
                    expert_pair(b, pair, False)
                expert_pair(b, NX // 2 - 1, True)

            with pe.Fori(0, B) as b:
                for g in range(G):
                    transpose_norm(b, 0, g)
                project_qkv(b)
                pe.wait_ge(s_klo, b + 1)
                score_tile(b, 0, 0, first=True)
                score_tile(b, 0, 1)
                with pe.Fori(0, H0 - 1) as h:
                    attention_head(b, h, False)
                attention_head(b, H0 - 1, True)
                for j in range(T + 1):
                    if j < T:
                        project_out(b, 0, j, A[:, j, :], AT, WoT0, s_att, (b + 1) * TILES)
                    if j > 0:
                        project_out_mm(b, 0, j - 1, AT, WoT0)
                for g in range(G):
                    transpose_norm(b, 1, g)
                    ffn(b, g)
                for g in range(G):
                    transpose_norm(b, 2, g)
                    project1(b, g)
                linear_a(b, 0)
                key_values(b, 0)
                for j in range(T + 1):
                    if j + 1 < T:
                        linear_a(b, j + 1)
                    if j < T:
                        linear_b(b, j, 0)
                    if j >= 1:
                        linear_c(b, j - 1)
                    if j < T:
                        linear_b(b, j, 1)
                    if j + 1 < T:
                        key_values(b, j + 1)
                for j in range(T + 1):
                    if j < T:
                        project_out(b, 1, j, O1[:, j, :], AT1, WoT1, s_gated, b * G + j // TG + 1)
                    if j > 0:
                        project_out_mm(b, 1, j - 1, AT1, WoT1)
                for g in range(G):
                    transpose_norm(b, 3, g)
                experts(b)

        @block.scalar
        def _(act):
            def copy(dst, src):
                return nc.scalar.activation(dst, src, ACT.Copy)

            act.dma_start(bq_col[:, :], bq0.rearrange("(c p) -> p c", p=P), allow_slow_non_contiguous=True).then_inc(s_table, 16)
            act.dma_start(bk_col[:, :], bk0.rearrange("(c p) -> p c", p=P), allow_slow_non_contiguous=True).then_inc(s_table, 16)
            for dst, src in ((bv_row[:, :], bv0), (bo0_row[:, :], bo0), (bo1_row[:, :], bo1), (scale_row[:, :], scale1),
                             (bqkvu_row[:, 0:E], bq1), (bqkvu_row[:, E:2 * E], bk1),
                             (bqkvu_row[:, 2 * E:3 * E], bv1), (bqkvu_row[:, 3 * E:4 * E], bu1)):
                act.dma_start(dst, src.partition_broadcast(P)).then_inc(s_table, 16)
            act.dma_start(convb_row[:, :], conv_b.partition_broadcast(P)).then_inc(s_table, 16)
            for i in range(H0):
                rows = slice(D0 * (i % 8), D0 * (i % 8) + D0)
                act.dma_start(conv_raw[rows, i // 8, :, :],
                             conv_w[:, i, :].partition_broadcast(D0)).then_inc(s_table, 16)

            act.wait_ge(s_loadm, 64)
            nc.scalar.activation(silu_rows, c_rows, ACT.Silu).then_inc(s_silu_c, 1)
            act.wait_ge(s_silu_ps, 1)
            copy(siluT[:, :, :, :].rearrange("p l c b -> p (l c b)"), wide[0][:, 0:2 * C * B]).then_inc(s_silu_sb, 1)
            for l in range(2):
                for n in range(3):
                    act.wait_ge(s_modps, 3 * l + n + 1)
                    copy(mod_rows[:, l, n * 512:(n + 1) * 512], wide[n + 1][0:B, :]).then_inc(s_modcp, 1)
            for i, (_, dst) in enumerate(wt_banks):
                act.wait_ge(s_wt_ps, i + 1)
                copy(dst, bank[i % 4][:, :].rearrange("p (a b) -> p a b", a=dst.shape[1])).then_inc(s_wt_sb, 1)
            act.wait_ge(s_table, 16 * NTABLE)

            def roots(b, k, g):
                act.wait_ge(s_var, b * (NLN * G) + k * G + g + 1)
                nc.scalar.activation(std[:, g * TG:(g + 1) * TG], mv[:, g * TG:(g + 1) * TG, 1], ACT.Sqrt,
                                     bias=eps_ln[:, 0:1]).then_inc(s_std, 1)

            def norm(b, k, g):
                roots(b, k, g)
                features_out(b, k, g)

            def features_out(b, k, g):
                for c in range(C):
                    act.wait_ge(s_hT_ps, b * (NLN * G * C) + (k * G + g) * C + c + 1)
                    copy(hT[:, c, g * N:(g + 1) * N], bank[c][:, :]).then_inc(s_hT, 1)
                    if k == NLN - 1:
                        copy(hT_hi[:, c, g * N:(g + 1) * N], bank[c][:, :]).then_inc(s_hsp_hi, 1)

            def queries_hi(b, h, blk, part):
                act.wait_ge(s_qw, b * (2 * NQB * H0) + h * (2 * NQB) + 2 * blk + part + 1)
                copy(QW_hi[blk % 2][:, part * U:(part + 1) * U, :], QW[part]).then_inc(s_qw_hi, 1)

            def copy_sum(b, h, qt, first=False):
                t = b * TILES + h * T + qt
                act.wait_ge(s_prod, t * U + 1)
                if not first:
                    act.wait_ge(s_comb, t * 2)
                copy(sum_sb, wide[SUM]).then_inc(s_sum, 1)

            def exponentials(b, h, qt):
                act.wait_ge(s_max, b * TILES + h * T + qt + 1)
                nc.scalar.activation(SC[qt % 2], SC[qt % 2], ACT.Exp, bias=exp_bias[:, qt % 2:qt % 2 + 1],
                                     accum_out=row_sum[:, qt % 2:qt % 2 + 1]).then_inc(s_exp, 1)

            def attention_head(b, h, last_head):
                for qt in range(T):
                    t = b * TILES + h * T + qt
                    for half in range(2):
                        act.wait_ge(s_tr, t * 2 + half + 1)
                        nc.scalar.activation(PT_hi[:, 4 * half:4 * half + 4, :].rearrange("p a b -> p (a b)"),
                                             bank[half][:, :], ACT.Copy, scale=PSCALE).then_inc(s_pt_hi, 1)
                    if qt < 4:
                        queries_hi(b, h, qt // 2 + 2, qt % 2)
                    elif not last_head:
                        queries_hi(b, h + 1, qt // 2 - 2, qt % 2)
                    if qt + 2 < T:
                        copy_sum(b, h, qt + 2)
                    elif not last_head:
                        copy_sum(b, h + 1, qt + 2 - T)
                    if qt + 1 < T:
                        exponentials(b, h, qt + 1)
                    elif not last_head:
                        exponentials(b, h + 1, 0)

            def project_out(b, layer, j, srcT):
                n = b * 2 * T + layer * T
                act.wait_ge(s_at_ps, n + j + 1)
                if j >= 2:
                    act.wait_ge((s_op_even, s_op)[j % 2], b * T + layer * (T // 2) + j // 2)
                copy(srcT[j % 2].rearrange("p a b -> p (a b)"), bank[j % 2][:, 0:E]).then_inc(s_at, 1)

            def ffn(b, g):
                for f in range(FC + 1):
                    n = g * FC + f
                    if f < FC:
                        act.wait_ge(s_fc, b * (G * FC) + n + 1)
                        if n >= 2:
                            act.wait_ge(s_hid, b * (G * FC) + n - 1)
                        nc.scalar.activation(relu[n % 2], wide[n % 4], ACT.Relu).then_inc(s_relu, 1)
                    if f > 0:
                        act.wait_ge(s_relu, b * (G * FC) + n)
                        if g == 1 and f == 1:
                            act.wait_ge(s_y, b * 4 + 2)
                        nc.scalar.activation(hid[:, f - 1, :], relu[(n - 1) % 2], ACT.Square).then_inc(s_hid, 1)
                if g == 1:
                    roots(b, 2, 0)
                for i in range(2):
                    act.wait_ge(s_y, b * 4 + g * 2 + i + 1)
                    copy(Y[:, 2 * i:2 * i + 2, :].rearrange("p a b -> p (a b)"), bank[2 + i][:, :]).then_inc(s_ysb, 1)

            def activate1(b, g):
                for k in range(TG + 1):
                    j = g * TG + k
                    if k < TG:
                        act.wait_ge(s_p1, b * T + j + 1)
                        copy(T1[:, j, :], scores[j % 2][:, :]).then_inc(s_p1sb, 1)
                    if k > 0:
                        act.wait_ge(s_t1, b * T + j)
                        nc.scalar.activation(T1[:, j - 1, 2 * E:4 * E], T1[:, j - 1, 2 * E:4 * E],
                                             ACT.Silu).then_inc(s_silu1, 1)

            def exponentials1(b, g):
                for k in range(TG):
                    j = g * TG + k
                    act.wait_ge(s_neg, b * T + j + 1)
                    nc.scalar.activation(EX[:, k, :], EX[:, k, :], ACT.Exp).then_inc(s_eluexp, 1)

            def copy_qk(b, j):
                act.wait_ge(s_qk_ps, b * T + j + 1)
                if j >= 3:
                    act.wait_ge(s_o1, b * T + j - 2)
                copy(qT[j % 3].rearrange("p a b -> p (a b)"), wide[j % 2][:, 0:E])
                copy(kT[j % 3].rearrange("p a b -> p (a b)"), wide[j % 2][:, E:2 * E]).then_inc(s_qkT, 1)

            def copy_o(b, j):
                act.wait_ge(s_o1, b * T + j + 1)
                copy(O1[:, j, :], bank[j % 2][:, 0:E])
                nc.scalar.activation(T1[:, j, E:2 * E], bank[j % 2][:, 0:E], ACT.Square,
                                     accum_out=sumsq[:, j:j + 1]).then_inc(s_o1sb, 1)

            def roots1(b, g):
                act.wait_ge(s_o1sb, b * T + (g + 1) * TG)
                nc.scalar.activation(rms[:, g * TG:(g + 1) * TG], sumsq[:, g * TG:(g + 1) * TG],
                                     ACT.Sqrt).then_inc(s_rms, 1)

            def expert_pair(b, pair, last_pair):
                for u in range(2 * G * HC):
                    s, v = u // (G * HC), u % (G * HC)
                    n = b * (NX * G * HC) + pair * (2 * G * HC) + u
                    act.wait_ge(s_hx, n + 1)
                    nc.scalar.activation(silu[u % 2], wide[u % 2], ACT.Silu).then_inc(s_silux, 1)
                    act.wait_ge(s_gatedx, n + 1)
                    copy(G_hi[u % 2], gated[u % 2]).then_inc(s_g_hi, 1)
                    if 1 <= v <= 2 * C and (s == 0 or not last_pair):
                        if v == 1:
                            act.wait_ge(s_w[1 - s], b * (NX // 2 * 48) + pair * 48 + (48 + 48 * s))
                        copy(W12_hi[1 - s][:, v - 1, :], W12s[1 - s][:, v - 1, :]).then_inc(s_w12_hi, 1)
                    k = w3_chunk(v)
                    if k is not None and (k > 1 or s == 0 or not last_pair):
                        slot = s if k > 1 else 1 - s
                        copy(W3_hi[:, k, :], W3s[slot][:, k, :]).then_inc(s_w3_hi, 1)

            def first_expert_hi(b):
                act.wait_ge(s_w[0], b * (NX // 2 * 48) + 48)
                for k in range(2 * C):
                    copy(W12_hi[0][:, k, :], W12s[0][:, k, :]).then_inc(s_w12_hi, 1)
                for k in range(2):
                    copy(W3_hi[:, k, :], W3s[0][:, k, :]).then_inc(s_w3_hi, 1)

            def experts(b):
                act.wait_ge(s_gap, b + 1)
                nc.scalar.activation(top[:, 3, :], top[:, 2, :], ACT.Exp).then_inc(s_gexp, 1)
                with act.Fori(0, NX // 2 - 1) as pair:
                    expert_pair(b, pair, False)
                expert_pair(b, NX // 2 - 1, True)

            with act.Fori(0, B) as b:
                for g in range(G):
                    norm(b, 0, g)
                act.wait_ge(s_x, b * 48 + 48)
                for u in range(8):
                    oc, g = (u % 4) // 2, u % 2
                    act.wait_ge(s_qkv_ps, b * 12 + u + 1)
                    if u < 4:
                        dst, bias = QT[:, oc, g * N:(g + 1) * N], bq_col
                    else:
                        dst, bias = K_raw[:, oc, 1 + g * N:1 + (g + 1) * N], bk_col
                    nc.scalar.activation(dst, wide[u % 4], ACT.Identity, bias=bias[:, oc:oc + 1]).then_inc(s_qk_act, 1)
                nc.scalar.drain()
                for blk in range(2):
                    for part in range(2):
                        queries_hi(b, 0, blk, part)
                for i in range(C * U):
                    act.wait_ge(s_kpair, b * (C * U) + i + 1)
                    copy(K_hi[:, i // U, i % U, :], K_pair[i // U][:, i % U, :]).then_inc(s_khi, 1)
                copy_sum(b, 0, 0, first=True)
                copy_sum(b, 0, 1)
                exponentials(b, 0, 0)
                with act.Fori(0, H0 - 1) as h:
                    attention_head(b, h, False)
                attention_head(b, H0 - 1, True)
                for j in range(T):
                    project_out(b, 0, j, AT)
                for g in range(G):
                    roots(b, 1, g)
                    if g == 0:
                        features_out(b, 1, g)
                ffn(b, 0)
                features_out(b, 1, 1)
                ffn(b, 1)
                features_out(b, 2, 0)
                activate1(b, 0)
                first_expert_hi(b)
                norm(b, 2, 1)
                exponentials1(b, 0)
                activate1(b, 1)
                exponentials1(b, 1)
                copy_qk(b, 0)
                for j in range(T + 1):
                    if j + 1 < T:
                        copy_qk(b, j + 1)
                    if j >= 1:
                        copy_o(b, j - 1)
                for g in range(G):
                    roots1(b, g)
                for j in range(T):
                    project_out(b, 1, j, AT1)
                for g in range(G):
                    norm(b, 3, g)
                experts(b)

        @block.vector
        def _(dve):
            V_ = nc.vector

            V_.memset(qexp[:, :, :, :], 0.0)
            V_.memset(blockdiag[:, :], 0.0)
            for x in range(NX):
                V_.memset(rank_bonus[:, x:x + 1], float(NX - x))
            V_.drain()
            for h in range(4):
                V_.memset(blockdiag[32 * h:32 * h + 32, 32 * h:32 * h + 32], 1.0)
            dve.wait_ge(s_table, 16 * NTABLE)
            isd = float(1.0 / np.sqrt(D0))
            V_.tensor_tensor(conv_sum[:, :, :], conv_raw[:, :, :, 0], conv_raw[:, :, :, 2], ALU.add)
            V_.tensor_scalar(filt[:, :, :, FIRST], conv_raw[:, :, :, 0], isd, None, ALU.mult)
            V_.tensor_scalar(filt[:, :, :, LAST], conv_raw[:, :, :, 2], isd, None, ALU.mult)
            V_.drain()
            V_.tensor_tensor(filt[:, :, :, SUM], conv_sum[:, :, :], conv_raw[:, :, :, 1], ALU.add)
            V_.tensor_tensor(filt[:, :, :, DIFF], conv_sum[:, :, :], conv_raw[:, :, :, 1], ALU.subtract)
            V_.drain()
            for u in (SUM, DIFF):
                V_.tensor_scalar(filt[:, :, :, u], filt[:, :, :, u], 0.5 * isd, None, ALU.mult)
            V_.drain()
            dve.wait_ge(s_modcp, 6)
            m6 = mod_rows[:, :, :].rearrange("b l (m e) -> b l m e", e=E)
            for m in (1, 4):
                V_.tensor_scalar(m6[:, :, m, :], m6[:, :, m, :], 1.0, None, ALU.add)
            for i, m in enumerate((2, 5)):
                V_.tensor_scalar(mod_tmp[:, :, i, :], m6[:, :, m, :], -1.0, None, ALU.mult)
                V_.tensor_scalar(mod_tmp2[:, :, i, :], m6[:, :, m, :], 0.0, 2.0, ALU.is_ge, ALU.mult)
            V_.drain()
            for i, m in enumerate((2, 5)):
                V_.tensor_tensor(mod_tmp[:, :, i, :], mod_tmp[:, :, i, :], m6[:, :, m, :], ALU.max)
            V_.tensor_scalar(mod_tmp2[:, :, :, :], mod_tmp2[:, :, :, :], -1.0, None, ALU.add)
            V_.drain()
            V_.tensor_scalar(mod_tmp[:, :, :, :], mod_tmp[:, :, :, :], 0.25, None, ALU.max)
            V_.drain()
            for i, m in enumerate((2, 5)):
                V_.tensor_tensor(m6[:, :, m, :], mod_tmp[:, :, i, :], mod_tmp2[:, :, i, :], ALU.mult)
            V_.drain()
            V_.memset(mod_tmp[:, 0, 0, 0:1], 0.0).then_inc(s_modrow, 1)

            def row(l, m, n):
                return MOD[:, l, m:m + 1, :].to_broadcast([P, n, E])

            def norm(b, k, g):
                l, m = k // 2, 3 * (k % 2)
                js = slice(g * TG, (g + 1) * TG)
                if k == 0:
                    dve.wait_ge(s_next, b * 80 + 80)

                def x(j):
                    if k == 0:
                        return X_next[g][:, j % TG // 2, (j % 2) * E:(j % 2 + 1) * E]
                    return X[:, j, :]

                for j in range(g * TG, (g + 1) * TG):
                    V_.bn_stats(stats[:, j, :], x(j))
                V_.drain()
                for j in range(g * TG, (g + 1) * TG):
                    last = V_.bn_aggr(mv[:, j, :], stats[:, j, :])
                last.then_inc(s_var, 1)
                V_.drain()
                for j in range(g * TG, (g + 1) * TG):
                    V_.scalar_tensor_tensor(out=Hn[:, j, :], in0=x(j), scalar=mv[:, j, 0:1],
                                            in1=MOD[:, l, m + 1, :], op0=ALU.subtract, op1=ALU.mult)
                dve.wait_ge(s_std, b * (NLN * G) + k * G + g + 1)
                V_.reciprocal(rstd[:, js], std[:, js])
                V_.drain()
                for j in range(g * TG, (g + 1) * TG):
                    last = V_.scalar_tensor_tensor(out=Hn[:, j, :], in0=Hn[:, j, :], scalar=rstd[:, j:j + 1],
                                                   in1=MOD[:, l, m, :], op0=ALU.mult, op1=ALU.add)
                last.then_inc(s_h, 1)

            def combine(b, h, qt):
                i, t = qt % 2, b * TILES + h * T + qt
                dve.wait_ge(s_sum, t + 1)
                dve.wait_ge(s_prod, t * U + FIRST + 1)
                V_.tensor_tensor(SC[i][:, 0, :], sum_sb, wide[FIRST], ALU.add).then_inc(s_comb, 1)
                dve.wait_ge(s_prod, t * U + LAST + 1)
                V_.tensor_tensor(SC[i][:, 1, :], sum_sb, wide[LAST], ALU.subtract).then_inc(s_comb, 1)
                V_.drain()
                dve.wait_ge(s_prod, t * U + DIFF + 1)
                V_.memset(carrier[:, :], 0.0)
                for k, op in ((0, ALU.add), (1, ALU.subtract)):
                    V_.tensor_tensor_reduce(out=SC[i][:, k, :], in0=SC[i][:, k, :], in1=wide[DIFF], scale=1.0,
                                            scalar=-3.4e38, op0=op, op1=ALU.max, accum_out=row_max[:, i, k:k + 1])
                V_.drain()
                V_.tensor_scalar(max_b[:, i:i + 1], row_max[:, i, 0:1], row_max[:, i, 1:2],
                                 convb_row[:, bass.ds(h, 1)], ALU.max, ALU.add)
                V_.drain()
                V_.tensor_scalar(exp_bias[:, i:i + 1], convb_row[:, bass.ds(h, 1)], max_b[:, i:i + 1], None,
                                 ALU.subtract).then_inc(s_max, 1)

            def split_v(b, h):
                part = [V_head[:, :, i * D0:(i + 1) * D0] for i in range(VP)]
                V_.tensor_copy(part[0], V[:, :, bass.ds(h * D0, D0)])
                V_.drain()
                V_.tensor_tensor(V_rest, V[:, :, bass.ds(h * D0, D0)], part[0], ALU.subtract)
                V_.drain()
                V_.tensor_copy(part[1], V_rest)
                V_.drain()
                V_.tensor_tensor(part[2], V_rest, part[1], ALU.subtract).then_inc(s_vhead, 1)

            def attention_head(b, h, last_head):
                for qt in range(T):
                    t = b * TILES + h * T + qt
                    for half in range(2):
                        dve.wait_ge(s_pt_hi, t * 2 + half + 1)
                        ks = slice(4 * half, 4 * half + 4)
                        last = V_.scalar_tensor_tensor(out=PT_lo[:, ks, :].rearrange("p a b -> p (a b)"),
                                                       in0=bank[half][:, :], scalar=PSCALE,
                                                       in1=PT_hi[:, ks, :].rearrange("p a b -> p (a b)"),
                                                       op0=ALU.mult, op1=ALU.subtract)
                    last.then_inc(s_pt_lo, 1)
                    if qt == 0:
                        split_v(b, h)
                    V_.reciprocal(row_inv[:, qt % 2:qt % 2 + 1], row_sum[:, qt % 2:qt % 2 + 1])
                    if qt + 2 < T:
                        combine(b, h, qt + 2)
                    elif not last_head:
                        combine(b, h + 1, qt + 2 - T)
                    dve.wait_ge(s_pv, t + 1)
                    V_.reduce_sum(pv_sum[:, :], bank[2 + qt % 2][:, 0:VP * D0].rearrange("p (v d) -> p d v", v=VP), AX)
                    V_.drain()
                    V_.tensor_scalar(A[:, qt, bass.ds(h * D0, D0)], pv_sum[:, :], row_inv[:, qt % 2:qt % 2 + 1],
                                     1.0 / PSCALE, ALU.mult, ALU.mult).then_inc(s_att, 1)

            def project_out(b, layer, buf, bias):
                for i in range(T // 2):
                    js = slice(2 * i, 2 * i + 2)
                    dve.wait_ge(s_op, b * T + layer * (T // 2) + i + 1)
                    V_.tensor_tensor(buf, bank[2 + i % 2][:, :].rearrange("p (k e) -> p k e", k=2),
                                     bias[:, :].unsqueeze(1).to_broadcast([P, 2, E]), ALU.add).then_inc(s_op_used, 1)
                    V_.drain()
                    V_.tensor_tensor(buf, buf, row(layer, 2, 2), ALU.mult)
                    V_.drain()
                    V_.tensor_tensor(X[:, js, :], X[:, js, :], buf, ALU.add)
                    V_.drain()
                    if i % 2 == 1:
                        norm(b, 2 * layer + 1, i // 2)

            def spikes(b, g):
                js = slice(g * TG, (g + 1) * TG)
                dve.wait_ge(s_ysb, b * 4 + g * 2 + 2)
                V_.tensor_scalar(cnt, Y, 1.0, None, ALU.is_gt)
                for step in range(4):
                    old, unit, fires = (Y, 1.0, ALU.is_gt) if step == 0 else (neg, -1.0, ALU.is_lt)
                    V_.scalar_tensor_tensor(out=leak, in0=old, scalar=0.9 * unit, in1=Y, op0=ALU.mult, op1=ALU.add)
                    V_.drain()
                    V_.scalar_tensor_tensor(out=neg, in0=old, scalar=unit, in1=leak, op0=fires, op1=ALU.subtract)
                    V_.drain()
                    V_.scalar_tensor_tensor(out=cnt, in0=neg, scalar=-1.0, in1=cnt, op0=ALU.is_lt, op1=ALU.add)
                V_.drain()
                V_.scalar_tensor_tensor(out=gained, in0=cnt, scalar=0.2, in1=row(0, 5, TG), op0=ALU.mult, op1=ALU.mult)
                V_.drain()
                V_.tensor_tensor(X[:, js, :], X[:, js, :], gained, ALU.add)
                V_.drain()

            def activate1(b, g):
                for k in range(TG):
                    dve.wait_ge(s_t1, b * T + g * TG + k + 1)
                    V_.tensor_scalar(EX[:, k, :], T1[:, g * TG + k, 0:2 * E], 0.0, None, ALU.min).then_inc(s_neg, 1)
                for k in range(TG):
                    dve.wait_ge(s_eluexp, b * T + g * TG + k + 1)
                    V_.tensor_scalar(EX[:, k, :], EX[:, k, :], -1.0, None, ALU.add)
                V_.drain()
                for k in range(TG):
                    j = g * TG + k
                    V_.scalar_tensor_tensor(out=T1[:, j, 0:2 * E], in0=T1[:, j, 0:2 * E], scalar=0.0, in1=EX[:, k, :],
                                            op0=ALU.max, op1=ALU.add).then_inc(s_elu, 1)
                V_.drain()

            def spread(b, j):
                dve.wait_ge(s_qkT, b * T + j + 1)
                if j == 1:
                    dve.wait_ge(s_zero, b + 1)
                if j >= 2:
                    dve.wait_ge(s_en, (b * T + j - 1) * C)
                for h in range(4):
                    r = slice(32 * h, 32 * h + 32)
                    last = V_.tensor_copy(qexps[j % 2][r, :, h, :], wide[j % 2][r, 0:E].rearrange("p (c n) -> p c n", c=C))
                last.then_inc(s_qexp, 1)

            def sum_key_values(b, j):
                dve.wait_ge(s_kvps, b * T + j + 1)
                ps = wide[2 + j % 2][:, 0:E].rearrange("p (c n) -> p c n", c=C)
                diag = blockdiag[:, :].unsqueeze(1).to_broadcast([P, C, P])
                if j >= 1:
                    dve.wait_ge(s_o1, b * T + j)
                    V_.tensor_tensor(kv_new[:, :, :], ps, diag, ALU.mult)
                    V_.drain()
                    V_.tensor_tensor(KV[(j + 1) % 2][:, :, :], KV[j % 2][:, :, :], kv_new[:, :, :],
                                     ALU.add).then_inc(s_kv, 1)
                else:
                    V_.tensor_tensor(KV[1][:, :, :], ps, diag, ALU.mult).then_inc(s_kv, 1)
                V_.drain()

            def mask(b, j):
                for c in range(C):
                    dve.wait_ge(s_en, (b * T + j) * C + c + 1)
                    if j >= 1 and c == 0:
                        dve.wait_ge(s_o1, b * T + j)
                    V_.tensor_tensor(EM[:, c, :, :], bank[2 + c][:, :].rearrange("p (h n) -> p h n", h=4),
                                     causal[:, :].unsqueeze(1).to_broadcast([P, 4, P]), ALU.mult).then_inc(s_em, 1)

            def gate1(b, g):
                js = slice(g * TG, (g + 1) * TG)
                dve.wait_ge(s_rms, b * G + g + 1)
                V_.tensor_scalar(rms[:, js], rms[:, js], float(E) ** -0.5, 1e-8, ALU.mult, ALU.add)
                V_.drain()
                V_.reciprocal(rms_inv[:, js], rms[:, js])
                V_.drain()
                for j in range(g * TG, (g + 1) * TG):
                    V_.scalar_tensor_tensor(out=O1[:, j, :], in0=O1[:, j, :], scalar=rms_inv[:, j:j + 1],
                                            in1=scale_row[:, :], op0=ALU.mult, op1=ALU.mult)
                V_.drain()
                V_.tensor_tensor(O1[:, js, :], O1[:, js, :], T1[:, js, 3 * E:4 * E], ALU.mult).then_inc(s_gated, 1)

            def router(b):
                L, eq, one1, L2, one2, cmb = (gate[:, i, :, :] for i in range(6))
                bonus = rank_bonus[:, :].unsqueeze(1).to_broadcast([P, T, NX])

                def wide_(i):
                    return top[:, i, :].unsqueeze(2).to_broadcast([P, T, NX])

                def first_largest(src, one, m):
                    V_.tensor_reduce(top[:, m, :], src, AX, ALU.max)
                    V_.drain()
                    V_.tensor_tensor(eq, src, wide_(m), ALU.is_equal)
                    V_.drain()
                    V_.tensor_tensor(eq, eq, bonus, ALU.mult)
                    V_.drain()
                    V_.tensor_reduce(top[:, 4, :], eq, AX, ALU.max)
                    V_.drain()
                    V_.tensor_tensor(one, eq, wide_(4), ALU.is_equal)
                    V_.drain()

                dve.wait_ge(s_logit, b + 1)
                V_.tensor_copy(L, bank[2][:, 0:T * NX].rearrange("p (t x) -> p t x", x=NX))
                V_.drain()
                first_largest(L, one1, 0)
                V_.tensor_scalar(L2, one1, -1.0, 1.0, ALU.mult, ALU.add)
                V_.drain()
                V_.tensor_tensor(L2, L2, L, ALU.mult)
                V_.tensor_scalar(cmb, one1, -3.0e38, None, ALU.mult)
                V_.drain()
                V_.tensor_tensor(L2, L2, cmb, ALU.add)
                V_.drain()
                first_largest(L2, one2, 1)
                V_.tensor_tensor(top[:, 2, :], top[:, 1, :], top[:, 0, :], ALU.subtract).then_inc(s_gap, 1)
                dve.wait_ge(s_acc, b + 1)
                dve.wait_ge(s_gexp, b + 1)
                V_.tensor_scalar(top[:, 5, :], top[:, 3, :], 1.0, None, ALU.add)
                V_.drain()
                V_.reciprocal(top[:, 6, :], top[:, 5, :])
                V_.drain()
                V_.tensor_tensor(top[:, 7, :], top[:, 3, :], top[:, 6, :], ALU.mult)
                V_.tensor_tensor(one1, one1, wide_(6), ALU.mult)
                V_.drain()
                V_.tensor_tensor(one2, one2, wide_(7), ALU.mult)
                V_.drain()
                V_.tensor_tensor(cmb, one1, one2, ALU.add).then_inc(s_yx_used, T)
                V_.drain()

            def add_outputs(b, pair, s, g):
                u = s * G * HC + (g + 1) * HC
                dve.wait_ge(s_yx, b * (NX * G * HC + 1) + pair * (2 * G * HC) + u + 1)
                for k in range(TG):
                    j = g * TG + k
                    V_.scalar_tensor_tensor(out=ACC[:, j, :], in0=bank[j // 2][:, (j % 2) * E:(j % 2 + 1) * E],
                                            scalar=gate[:, 5, j, bass.ds(pair * 2 + s, 1)], in1=ACC[:, j, :],
                                            op0=ALU.mult, op1=ALU.add).then_inc(s_yx_used, 1)

            def finish(g):
                js = slice(g * TG, (g + 1) * TG)
                V_.drain()
                V_.tensor_tensor(ACC[:, js, :], ACC[:, js, :], row(1, 5, TG), ALU.mult)
                V_.drain()
                V_.tensor_tensor(result[:, js, :], X[:, js, :], ACC[:, js, :], ALU.add).then_inc(s_fin, 1)

            def expert_pair(b, pair, last_pair):
                for u in range(2 * G * HC):
                    s, v = u // (G * HC), u % (G * HC)
                    n = b * (NX * G * HC) + pair * (2 * G * HC) + u
                    dve.wait_ge(s_silux, n + 1)
                    V_.tensor_tensor(gated[u % 2], silu[u % 2], wide[2 + u % 2], ALU.mult).then_inc(s_gatedx, 1)
                    dve.wait_ge(s_g_hi, n + 1)
                    V_.tensor_tensor(G_lo[u % 2], gated[u % 2], G_hi[u % 2].bitcast(F32), ALU.subtract).then_inc(s_g, 1)
                    if 1 <= v <= 2 * C and (s == 0 or not last_pair):
                        dve.wait_ge(s_w12_hi, b * (2 * C * NX) + pair * (4 * C) + (s + 1) * 2 * C + v)
                        V_.tensor_tensor(W12_lo[1 - s][:, v - 1, :], W12s[1 - s][:, v - 1, :],
                                         W12_hi[1 - s][:, v - 1, :].bitcast(F32), ALU.subtract).then_inc(s_w12_lo, 1)
                    k = w3_chunk(v)
                    if k is not None and (k > 1 or s == 0 or not last_pair):
                        slot, e = (s, s) if k > 1 else (1 - s, s + 1)
                        dve.wait_ge(s_w3_hi, b * (NX * HC) + pair * (2 * HC) + e * HC + k + 1)
                        V_.tensor_tensor(W3_lo[:, k, :], W3s[slot][:, k, :], W3_hi[:, k, :].bitcast(F32),
                                         ALU.subtract).then_inc(s_w3_lo, 1)
                    if u > 0 and u % HC == 0:
                        add_outputs(b, pair, (u - 1) // (G * HC), (u - 1) // HC % G)
                        if last_pair and u == 2 * G * HC - HC:
                            finish(g=0)
                add_outputs(b, pair, 1, G - 1)

            def features_lo(b, g):
                cols = slice(g * N, (g + 1) * N)
                dve.wait_ge(s_hsp_hi, b * (C * G) + (g + 1) * C)
                V_.tensor_tensor(hT_lo[:, :, cols], hT[:, :, cols], hT_hi[:, :, cols].bitcast(F32),
                                 ALU.subtract).then_inc(s_hsp_lo, 1)

            def experts(b):
                with dve.Fori(0, NX // 2 - 1) as pair:
                    expert_pair(b, pair, False)
                expert_pair(b, NX // 2 - 1, True)
                finish(g=1)

            with dve.Fori(0, B) as b:
                for g in range(G):
                    norm(b, 0, g)
                for i in range(C):
                    for edge in (0, S + 1):
                        V_.memset(K_raw[:, i, edge:edge + 1], 0.0)
                V_.drain()
                for u in range(8, 12):
                    j = 2 * (u - 8)
                    dve.wait_ge(s_qkv_ps, b * 12 + u + 1)
                    V_.tensor_tensor(V[:, j:j + 2, :], wide[u % 4].rearrange("p (k e) -> p k e", k=2),
                                     bv_row[:, :].unsqueeze(1).to_broadcast([P, 2, E]), ALU.add).then_inc(s_v, 1)
                dve.wait_ge(s_qk_act, b * 8 + 8)
                for c in range(C):
                    def key(first):
                        return K_raw[:, c, 1 + first:first + S:2]
                    for u, (x, y, op) in ((SUM, (0, 1, ALU.add)), (FIRST, (-1, 1, ALU.subtract)),
                                          (LAST, (0, 2, ALU.subtract)), (DIFF, (1, 0, ALU.subtract))):
                        V_.tensor_tensor(K_pair[c][:, u, :], key(x), key(y), op).then_inc(s_kpair, 1)
                for i in range(C * U):
                    dve.wait_ge(s_khi, b * (C * U) + i + 1)
                    last = V_.tensor_tensor(K_lo[:, i // U, i % U, :], K_pair[i // U][:, i % U, :],
                                            K_hi[:, i // U, i % U, :].bitcast(F32), ALU.subtract)
                last.then_inc(s_klo, 1)
                combine(b, 0, 0)
                combine(b, 0, 1)
                with dve.Fori(0, H0 - 1) as h:
                    attention_head(b, h, False)
                attention_head(b, H0 - 1, True)
                dve.wait_ge(s_x, b * 48 + 48)
                project_out(b, 0, prod, bo0_row)
                for g in range(G):
                    spikes(b, g)
                    norm(b, 2, g)
                for g in range(G):
                    activate1(b, g)
                spread(b, 0)
                for j in range(T):
                    if j + 1 < T:
                        spread(b, j + 1)
                    mask(b, j)
                    sum_key_values(b, j)
                for g in range(G):
                    gate1(b, g)
                project_out(b, 1, prod1, bo1_row)
                for g in range(G):
                    features_lo(b, g)
                router(b)
                experts(b)


_INS = ['L0_attn_query', 'L0_attn_Wq', 'L0_attn_bq', 'L0_attn_Wk', 'L0_attn_bk', 'L0_attn_Wv', 'L0_attn_bv',
        'L0_attn_Wo', 'L0_attn_bo', 'L0_attn_conv_w', 'L0_attn_conv_b', 'L0_ffn_W_fc', 'L0_ffn_W_proj', 'L0_c',
        'L0_wmod', 'L1_attn_Wq', 'L1_attn_bq', 'L1_attn_Wk', 'L1_attn_bk', 'L1_attn_Wv', 'L1_attn_bv', 'L1_attn_Wu',
        'L1_attn_bu', 'L1_attn_Wo', 'L1_attn_bo', 'L1_attn_scale', 'L1_ffn_Wg', 'L1_ffn_W1', 'L1_ffn_W2',
        'L1_ffn_W3', 'L1_c', 'L1_wmod']
_OUTS = [((4, 1024, 256), 'float32')]


def kernel(**inputs):
    import numpy as _np
    import concourse.bacc as _bacc
    from concourse import mybir as _mybir
    from concourse.bass_utils import run_bass_kernel_spmd as _run

    nc = _bacc.Bacc("TRN2", target_bir_lowering=False, num_devices=1)
    arrays, args = {}, []
    for name in _INS:
        a = _np.ascontiguousarray(inputs[name])
        arrays[f"in_{name}_dram"] = a
        args.append(nc.dram_tensor(f"in_{name}_dram", a.shape, _mybir.dt.from_np(a.dtype), kind="ExternalInput").ap())
    for i, (shape, dtype) in enumerate(_OUTS):
        dt = _mybir.dt.from_np(_np.dtype(dtype))
        args.append(nc.dram_tensor(f"out_{i}_dram", shape, dt, kind="ExternalOutput").ap())
    adaln_two_layer_kernel(nc, *args)
    r = _run(nc, [arrays], core_ids=[0])
    got = tuple(r.results[0][f"out_{i}_dram"] for i in range(len(_OUTS)))
    return got[0]
```
